# Optimizing a Trainium2 kernel written in Bass

```python
import numpy as np
import jax
import jax.numpy as jnp

def _softmax(x, axis=-1):
    return jax.nn.softmax(x, axis=axis)

def _gelu(x):
    return jax.nn.gelu(x, approximate=True)

def _silu(x):
    return jax.nn.silu(x)

def _sigmoid(x):
    return jax.nn.sigmoid(x)

def _layernorm(x, axis=-1, eps=1e-05):
    m = jnp.mean(x, axis=axis, keepdims=True)
    v = jnp.var(x, axis=axis, keepdims=True)
    return (x - m) / jnp.sqrt(v + eps)

def _scatter_add(tgt, idx, src, axis=0):
    return tgt.at[idx].add(src)

def _segment_sum(src, seg, n):
    return jax.ops.segment_sum(src, seg, n)
kernel_name = 'mk_gnn_ffn_d1_gnn_r16_067506'

def setup_inputs(seed: int=0):
    np.random.seed(seed)
    _w = jnp.asarray

    def _rec_inputs():
        import jax
        import jax.numpy as jnp
        _gk = jax.random.key(seed)
        x = -0.0006008 + 1.001 * jax.random.normal(jax.random.fold_in(_gk, 1), (3125, 256), jnp.float32)
        src = jax.random.randint(jax.random.fold_in(_gk, 2), (100000,), 0, 3125, jnp.int32)
        dst = jnp.minimum((3125 * jax.random.uniform(jax.random.fold_in(_gk, 3), (100000,)) ** 2.0).astype(jnp.int32), 49999)
        _o = jnp.argsort(dst, stable=True)
        src = src[_o]
        dst = dst[_o]
        edge_weight = -0.00278149 + 0.998712 * jax.random.normal(jax.random.fold_in(_gk, 12), (100000,), jnp.float32)
        return (x, src, dst, edge_weight)
    x, src, dst, edge_weight = _rec_inputs()

    def _L0_gnn_setup():
        import jax, jax.numpy as jnp
        import numpy as np
        N = 625
        E = 20000
        D = 256
        EPS = 1e-05

        def layer_norm(x, g, b):
            mu = jnp.mean(x, axis=-1, keepdims=True)
            var = jnp.mean(jnp.square(x - mu), axis=-1, keepdims=True)
            return (x - mu) * jax.lax.rsqrt(var + EPS) * g + b

        def linear(x, w, b):
            return x @ w + b
        key = jax.random.key(seed)
        ks = jax.random.split(key, 20)
        s = 1.0 / np.sqrt(D)
        inp = {'x': jax.random.normal(ks[0], (N, D), jnp.float32), 'edge_index': jax.random.randint(ks[1], (2, E), 0, N, jnp.int64), 'edge_weight': jax.random.normal(ks[2], (E,), jnp.float32), 'wq': jax.random.normal(ks[3], (D, D), jnp.float32) * s, 'bq': jnp.zeros((D,), jnp.float32), 'wk': jax.random.normal(ks[4], (D, D), jnp.float32) * s, 'bk': jnp.zeros((D,), jnp.float32), 'wv': jax.random.normal(ks[5], (D, D), jnp.float32) * s, 'bv': jnp.zeros((D,), jnp.float32), 'ws': jax.random.normal(ks[6], (D, D), jnp.float32) * s, 'bs': jnp.zeros((D,), jnp.float32), 'we': jax.random.normal(ks[7], (1, 1), jnp.float32), 'be': jnp.zeros((1,), jnp.float32), 'g1': jnp.ones((D,), jnp.float32), 'b1': jnp.zeros((D,), jnp.float32), 'g2': jnp.ones((D,), jnp.float32), 'b2': jnp.zeros((D,), jnp.float32), 'w_ff1': jax.random.normal(ks[8], (D, 2 * D), jnp.float32) * s, 'b_ff1': jnp.zeros((2 * D,), jnp.float32), 'w_ff2': jax.random.normal(ks[9], (2 * D, D), jnp.float32) * (1.0 / np.sqrt(2 * D)), 'b_ff2': jnp.zeros((D,), jnp.float32)}
        return inp
    _L0_gnn_all = _L0_gnn_setup()
    _L0_gnn_in = {k: v for k, v in _L0_gnn_all.items() if k in ('wq', 'bq', 'wk', 'bk', 'wv', 'bv', 'ws', 'bs', 'we', 'be', 'g1', 'b1', 'g2', 'b2', 'w_ff1', 'b_ff1', 'w_ff2', 'b_ff2')}
    del _L0_gnn_all

    def _L0_ffn_setup():
        import jax, jax.numpy as jnp
        import numpy as np
        B, K, D = (512, 16, 256)
        E = 32
        H = int(D * 0.25)
        key = jax.random.key(seed)
        ks = jax.random.split(key, 7)
        d_rs = D ** (-0.5)
        h_rs = H ** (-0.5)
        x = jax.random.normal(ks[0], (B, K, D), dtype=jnp.float32)
        router_w = jax.random.uniform(ks[1], (E, D), jnp.float32, -d_rs, d_rs)
        router_b = jax.random.uniform(ks[2], (E,), jnp.float32, -d_rs, d_rs)
        W1 = jax.random.uniform(ks[3], (E, D, H), jnp.float32, -h_rs, h_rs)
        b1 = jax.random.uniform(ks[4], (E, H), jnp.float32, -h_rs, h_rs)
        W2 = jax.random.uniform(ks[5], (E, H, D), jnp.float32, -d_rs, d_rs)
        b2 = jax.random.uniform(ks[6], (E, D), jnp.float32, -d_rs, d_rs)
        return {'x': x, 'router_w': router_w, 'router_b': router_b, 'W1': W1, 'b1': b1, 'W2': W2, 'b2': b2}
    _L0_ffn_all = _L0_ffn_setup()
    _L0_ffn_in = {k: v for k, v in _L0_ffn_all.items() if k in ('router_w', 'router_b', 'W1', 'b1', 'W2', 'b2')}
    del _L0_ffn_all
    return {'x': x, 'src': src, 'dst': dst, 'edge_weight': edge_weight, 'L0_gnn_wq': _L0_gnn_in['wq'], 'L0_gnn_bq': _L0_gnn_in['bq'], 'L0_gnn_wk': _L0_gnn_in['wk'], 'L0_gnn_bk': _L0_gnn_in['bk'], 'L0_gnn_wv': _L0_gnn_in['wv'], 'L0_gnn_bv': _L0_gnn_in['bv'], 'L0_gnn_ws': _L0_gnn_in['ws'], 'L0_gnn_bs': _L0_gnn_in['bs'], 'L0_gnn_we': _L0_gnn_in['we'], 'L0_gnn_be': _L0_gnn_in['be'], 'L0_gnn_g1': _L0_gnn_in['g1'], 'L0_gnn_b1': _L0_gnn_in['b1'], 'L0_gnn_g2': _L0_gnn_in['g2'], 'L0_gnn_b2': _L0_gnn_in['b2'], 'L0_gnn_w_ff1': _L0_gnn_in['w_ff1'], 'L0_gnn_b_ff1': _L0_gnn_in['b_ff1'], 'L0_gnn_w_ff2': _L0_gnn_in['w_ff2'], 'L0_gnn_b_ff2': _L0_gnn_in['b_ff2'], 'L0_ffn_router_w': _L0_ffn_in['router_w'], 'L0_ffn_router_b': _L0_ffn_in['router_b'], 'L0_ffn_W1': _L0_ffn_in['W1'], 'L0_ffn_b1': _L0_ffn_in['b1'], 'L0_ffn_W2': _L0_ffn_in['W2'], 'L0_ffn_b2': _L0_ffn_in['b2']}

def reference(x, src, dst, edge_weight, L0_gnn_wq, L0_gnn_bq, L0_gnn_wk, L0_gnn_bk, L0_gnn_wv, L0_gnn_bv, L0_gnn_ws, L0_gnn_bs, L0_gnn_we, L0_gnn_be, L0_gnn_g1, L0_gnn_b1, L0_gnn_g2, L0_gnn_b2, L0_gnn_w_ff1, L0_gnn_b_ff1, L0_gnn_w_ff2, L0_gnn_b_ff2, L0_ffn_router_w, L0_ffn_router_b, L0_ffn_W1, L0_ffn_b1, L0_ffn_W2, L0_ffn_b2):
    import jax
    import jax.numpy as jnp

    def _L0_gnn_ref(x, edge_index, edge_weight, wq, bq, wk, bk, wv, bv, ws, bs, we, be, g1, b1, g2, b2, w_ff1, b_ff1, w_ff2, b_ff2):
        import jax, jax.numpy as jnp
        import numpy as np
        N = 625
        E = 20000
        D = 256
        EPS = 1e-05

        def layer_norm(x, g, b):
            mu = jnp.mean(x, axis=-1, keepdims=True)
            var = jnp.mean(jnp.square(x - mu), axis=-1, keepdims=True)
            return (x - mu) * jax.lax.rsqrt(var + EPS) * g + b

        def linear(x, w, b):
            return x @ w + b
        n = x.shape[0]
        scale = x.shape[-1] ** (-0.5)
        q = linear(x, wq, bq)
        k = linear(x, wk, bk)
        v = linear(x, wv, bv)
        src, dst = (edge_index[0], edge_index[1])
        scores = jnp.sum(q[dst] * k[src], axis=-1) * scale
        scores = scores + (edge_weight[:, None] @ we + be)[:, 0]
        seg_max = jax.ops.segment_max(scores, dst, num_segments=n)
        exp_s = jnp.exp(scores - seg_max[dst])
        denom = jax.ops.segment_sum(exp_s, dst, num_segments=n)
        attn = exp_s / jnp.maximum(denom[dst], 1e-12)
        message = v[src] * attn[:, None]
        out = jax.ops.segment_sum(message, dst, num_segments=n)
        x = layer_norm(x + out + linear(x, ws, bs), g1, b1)
        ffn = linear(jax.nn.gelu(linear(x, w_ff1, b_ff1)), w_ff2, b_ff2)
        x = layer_norm(x + ffn, g2, b2)
        return x

    def _L0_ffn_ref(x, router_w, router_b, W1, b1, W2, b2):
        import jax, jax.numpy as jnp
        import numpy as np
        B, K, D = (512, 16, 256)
        E = 32
        H = int(D * 0.25)
        xf = x.reshape(-1, D)
        logits = xf @ router_w.T + router_b
        idx = jnp.argmax(logits, axis=-1)
        w1t = jnp.take(W1, idx, axis=0)
        h = jnp.einsum('nd,ndh->nh', xf, w1t) + jnp.take(b1, idx, axis=0)
        h = jax.nn.relu(h)
        w2t = jnp.take(W2, idx, axis=0)
        out = jnp.einsum('nh,nhd->nd', h, w2t) + jnp.take(b2, idx, axis=0)
        out = jax.nn.relu(out)
        return out.reshape(x.shape)
    edge_index = jnp.stack([src, dst])
    x = x + _L0_gnn_ref(_layernorm(x, axis=-1), edge_index, edge_weight, L0_gnn_wq, L0_gnn_bq, L0_gnn_wk, L0_gnn_bk, L0_gnn_wv, L0_gnn_bv, L0_gnn_ws, L0_gnn_bs, L0_gnn_we, L0_gnn_be, L0_gnn_g1, L0_gnn_b1, L0_gnn_g2, L0_gnn_b2, L0_gnn_w_ff1, L0_gnn_b_ff1, L0_gnn_w_ff2, L0_gnn_b_ff2)
    x = x + _L0_ffn_ref(_layernorm(x, axis=-1)[None], L0_ffn_router_w, L0_ffn_router_b, L0_ffn_W1, L0_ffn_b1, L0_ffn_W2, L0_ffn_b2)[0]
    return x

_drawn_inputs = setup_inputs


def setup_inputs(seed=0):
    import zlib

    import numpy as np

    out = dict(_drawn_inputs(seed))
    spreads = {'L0_gnn_bq': (0.0, 0.498),
     'L0_gnn_bk': (0.0, 0.8),
     'L0_gnn_bv': (0.0, 0.1),
     'L0_gnn_bs': (0.0, 0.1),
     'L0_gnn_g1': (1.0, 0.2),
     'L0_gnn_b1': (0.0, 0.1),
     'L0_gnn_g2': (1.0, 0.2),
     'L0_gnn_b2': (0.0, 0.1),
     'L0_gnn_b_ff1': (0.0, 0.1),
     'L0_gnn_b_ff2': (0.0, 0.1)}
    factors = {'edge_weight': 5.687, 'L0_ffn_b1': 8.0, 'L0_ffn_b2': 4.032}
    for name, (base, spread) in spreads.items():
        noise = np.random.default_rng([zlib.crc32(name.encode()), seed]).standard_normal(out[name].shape)
        drawn = base * np.exp(spread * noise) if base else spread * noise
        out[name] = jnp.asarray(drawn.astype(out[name].dtype))
    for name, factor in factors.items():
        out[name] = (out[name] * factor).astype(out[name].dtype)
    return out
```

```python
import concourse.bass as bass
from concourse import mybir
from contextlib import ExitStack

F32 = mybir.dt.float32
BF16 = mybir.dt.bfloat16
I32 = mybir.dt.int32
U32 = mybir.dt.uint32
ALU = mybir.AluOpType
ACT = mybir.ActivationFunctionType
AX = mybir.AxisListType.X

N, D, E = 3125, 256, 100000
FF = 2 * D
NEXP, HID = 32, 64
EPS = 1e-5
RSQRT = float(0x5F3759DF)
NEWTON = 3
NORM = 5 + 3 * NEWTON
P = 128
TILE = 125
NT = N // TILE
KH = D // P
CHUNK = 128
NC = -(-E // CHUNK)
EROW = NC
WIN = 5
NW = N // WIN
STEPS = NC + NW - 1
GROUP = 4
NG = -(-STEPS // (2 * GROUP)) * 2
SLOTS = NG * GROUP
SBLK = SLOTS // P
CB = -(-NC // P)
LO = 128
ROW = NT * LO
BIG = 1e30
MAGIC = 12582912.0
SHIFT = 30.0
SCALE = float(D) ** -0.5
NM = NEXP * HID // P
SCH = [(c, min(512, ROW - c)) for c in range(0, ROW, 512)]
TRG = [(g, min(4, NT - g)) for g in range(0, NT, 4)]


class Order:

    def __init__(self, eng, sem, per=None):
        self.eng, self.sem, self.per, self.base, self.n = eng, sem, per, 0, 0

    def begin(self, t):
        self.base, self.n = t * self.per, 0

    def end(self):
        assert self.n == self.per, (self.n, self.per)

    def __call__(self, ins, mark=None):
        ins.then_inc(self.sem, 1)
        self.n += 1
        self.eng.wait_ge(self.sem, self.base + self.n)
        if mark is not None:
            self.eng.sem_inc(mark, 1)


def gnn_moe(nc, x, src, dst, edge_weight, wq, bq, wk, bk, wv, bv, ws, bs, we, be, g1, b1, g2, b2,
            w_ff1, b_ff1, w_ff2, b_ff2, router_w, router_b, W1, eb1, W2, eb2, out):
    ctx = ExitStack()
    with ctx:
        def sb(name, shape, dt=F32):
            return ctx.enter_context(nc.sbuf_tensor(name, shape, dt))

        def sem(name):
            return ctx.enter_context(nc.semaphore(name))

        code_lin = nc.dram_tensor("code_lin", [NC, CHUNK], F32)
        lo_lin = nc.dram_tensor("lo_lin", [NC, CHUNK], F32)
        val_lin = nc.dram_tensor("val_lin", [NC, CHUNK], F32)
        last_lin = nc.dram_tensor("last_lin", [NW], U32)
        adj = nc.dram_tensor("adj", [SLOTS * WIN, ROW], F32)

        ident = sb("ident", [P, P])
        ones = sb("ones", [P, P])
        iota_row = sb("iota_row", [P, P])
        iota_c = sb("iota_c", [P, CB * P])
        step_col = sb("step_col", [P, SBLK])
        win_col = sb("win_col", [P, NW // TILE])
        pmod = sb("pmod", [P, 1])
        sel = sb("sel", [NEXP, NM, 2, HID], BF16)
        wq_sb = sb("wq_sb", [P, KH, D])
        wk_sb = sb("wk_sb", [P, KH, D])
        wv_sb = sb("wv_sb", [P, KH, D])
        ws_sb = sb("ws_sb", [P, KH, D])
        wf1_sb = sb("wf1_sb", [P, KH, FF])
        wf2_sb = sb("wf2_sb", [P, FF // P, D])
        rw_sb = sb("rw_sb", [P, KH, NEXP])
        w2_sb = sb("w2_sb", [P, NM, D])
        eb2_sb = sb("eb2_sb", [NEXP, D])
        bq_col = sb("bq_col", [P, KH])
        bqs_col = sb("bqs_col", [P, KH])
        bk_col = sb("bk_col", [P, KH])
        bf1_col = sb("bf1_col", [P, FF // P])
        eb1_col = sb("eb1_col", [P, NM])
        rows = {}
        for nm, src_ap, n in (("bv", bv, D), ("bs", bs, D), ("g1", g1, D), ("b1", b1, D), ("g2", g2, D),
                              ("b2", b2, D), ("bf2", b_ff2, D), ("rb", router_b, NEXP), ("be", be, 1),
                              ("we", we, 1)):
            rows[nm] = (sb(nm + "_row", [P, n]), src_ap)
        row = {k: v[0] for k, v in rows.items()}

        kT = sb("kT", [P, KH, NT, LO])
        w1_sb = kT[:, :, :, :].rearrange("p k j l -> p (k j l)")[:, 0:KH * NEXP * HID].rearrange(
            "p (k e h) -> p k e h", k=KH, e=NEXP)
        V = sb("V", [TILE, NT, D])
        x1_buf = sb("x1", [P, NT * D])
        x1 = x1_buf[0:TILE, :].rearrange("p (t d) -> p t d", d=D)
        ARENA = 17024
        arena = sb("arena", [P, ARENA])
        at = [0]

        def view(cols):
            at[0] += cols
            assert at[0] <= ARENA, at[0]
            return arena[:, at[0] - cols:at[0]]

        w_e, neg_e, F_e, B_e, t_e, code_e, dstf = (view(EROW + 1) for _ in range(7))
        di, si = view(EROW).bitcast(I32), view(EROW).bitcast(I32)
        srcf, hi_e = F_e, neg_e
        cmp_o = view(CB * P)
        s_row, o_row = view(CB * P), view(CB * P)
        cv_tab = view(2 * SLOTS).rearrange("p (i c) -> p i c", c=2)
        lo_tab = view(SLOTS)
        keep_tab = view(SLOTS)
        c_row = view(SLOTS)
        at[0] = 0
        Xs = view(2 * GROUP * TILE).rearrange("p (s k m) -> p s k m", s=2, k=GROUP)
        Ys = view(2 * GROUP * LO).rearrange("p (s k l) -> p s k l", s=2, k=GROUP)
        stage = view(2 * GROUP * LO).rearrange("p (s k l) -> p s k l", s=2, k=GROUP)
        cur = view(2 * 2 * GROUP).rearrange("p (s k c) -> p s k c", s=2, c=2)
        at[0] = 0
        A_sb = view(2 * ROW).rearrange("p (s c) -> p s c", s=2)
        Z = view(2 * ROW).rearrange("p (s c) -> p s c", s=2)
        PT = view(NT * TILE).rearrange("p (j d) -> p j d", j=NT)
        at[0] = 0

        def two(*shape):
            n = 2
            for d in shape:
                n *= d
            v = view(n)
            if len(shape) == 1:
                return v.rearrange("p (s c) -> p s c", s=2)
            return v.rearrange("p (s a c) -> p s a c", s=2, a=shape[0])

        gT, hmT, x1T, xfT = two(FF // P, TILE), two(NM, TILE), two(KH, TILE), two(KH, TILE)
        x1c, x2, xf, y2, o_sb = two(D), two(D), two(D), two(D), two(D)
        lg, hot, ohT = two(NEXP), two(NEXP), two(TILE)
        negT = sb("negT", [NEXP, 2, TILE], BF16)

        x1_at = [0]

        def small(cols):
            x1_at[0] += cols
            assert x1_at[0] <= NT * D
            return x1_buf[:, x1_at[0] - cols:x1_at[0]]

        firstc = small(CB * CHUNK).bitcast(I32).rearrange("p (b e) -> p b e", b=CB)
        fcol = sb("fcol", [P, CB])
        diag = small(SBLK * P).rearrange("p (b e) -> p b e", b=SBLK)
        segcmp = small(2 * P)
        segval = small(2 * P)
        guards = sb("guards", [P, 2])
        cnt = sb("cnt", [P, SBLK])
        cidx = sb("cidx", [P, SBLK], U32)
        wneg = sb("wneg", [P, SBLK])
        wcnt = sb("wcnt", [P, NW // TILE])
        wrow = sb("wrow", [P, NW // TILE], U32)
        arow0 = sb("arow0", [P, NT], U32)
        arowf = sb("arowf", [P, NT])
        arow = sb("arow", [P, NT], U32)
        gidx = sb("gidx", [P, 2], U32)
        gath = small(2 * 3 * CHUNK).rearrange("p (s c e) -> p s c e", s=2, c=3)

        xt = sb("xt", [TILE, 2, D])
        h = sb("h", [TILE, 2, D])
        hT = sb("hT", [P, 2, KH, TILE])
        qT = sb("qT", [P, 2, KH, TILE])
        st6 = sb("st6", [TILE, 6])
        mv = sb("mv", [TILE, 2])
        rstd = sb("rstd", [TILE, 1])
        var = sb("var", [TILE, 1])
        half = sb("half", [TILE, 1])
        mx = sb("mx", [TILE, 8])
        mxr = sb("mxr", [TILE, 1])
        nmax = sb("nmax", [TILE, 2])
        den = sb("den", [TILE, 2])
        rden = sb("rden", [TILE, 2])
        yt = sb("yt", [TILE, D])
        mx8 = sb("mx8", [TILE, 8])
        ix8 = sb("ix8", [TILE, 8], U32)
        ixf = sb("ixf", [TILE, 1])

        bank = [ctx.enter_context(nc.psum_tensor(f"bank{i}", [P, 512], F32)) for i in range(8)]

        pads_set, edges_in, chunks_in, scal_in, params_in = (sem(n) for n in (
            "pads_set", "edges_in", "chunks_in", "scal_in", "params_in"))
        pool_ord, consts_set = sem("pool_ord"), sem("consts_set")
        dve_mark, pool_mark = sem("dve_mark"), sem("pool_mark")
        dve_ord, diag_set, rows_bc = sem("dve_ord"), sem("diag_set"), sem("rows_bc")
        guard_set, val_set, tab_stored = sem("guard_set"), sem("val_set"), sem("tab_stored")
        code_set, idx_set, rel_set, tabT_done, tab_set, keep_set = (sem(n) for n in (
            "code_set", "idx_set", "rel_set", "tabT_done", "tab_set", "keep_set"))
        gath_in = [sem("gath_in0"), sem("gath_in1")]
        last_set, last_stored, last_in, arow_set = (sem(n) for n in ("last_set", "last_stored", "last_in", "arow_set"))
        kx_in = [sem("kx_in0"), sem("kx_in1")]
        kh_ready, khT_ps, khT_ready, k_ps, v_ps, k_ready, v_ready, kv_ord = (sem(n) for n in (
            "kh_ready", "khT_ps", "khT_ready", "k_ps", "v_ps", "k_ready", "v_ready", "kv_ord"))
        cur_set, x_ready, y_ready, prod_done, acc_ord, stage_ready = (sem(n) for n in (
            "cur_set", "x_ready", "y_ready", "prod_done", "acc_ord", "stage_ready"))
        stored = [sem("stored0"), sem("stored1")]
        x_in = [sem("x_in0"), sem("x_in1")]
        a_in = [sem("a_in0"), sem("a_in1")]
        (h_ready, hT_ps, hT_ready, q_ps, q_ready, gidx_set, mask_set, s_ready, s_used, nmax_set, e_ready, p_ready,
         front_ord, tr_ready, pt_ready, attn_done, o_used, back_ord, norm_set, x1_ready) = (sem(n) for n in (
            "h_ready", "hT_ps", "hT_ready", "q_ps", "q_ready", "gidx_set", "mask_set", "s_ready", "s_used", "nmax_set",
            "e_ready", "p_ready", "front_ord", "tr_ready", "pt_ready", "attn_done", "o_used", "back_ord", "norm_set", "x1_ready"))
        cx_in = [sem("cx_in0"), sem("cx_in1")]
        (x1c_set, x1T_ps, x1T_set, f1_ps, g_set, f2_ps, y2_set, cf_ord, x2_set, xf_set, xfT_ps, xfT_set, lg_ps, lg_used,
         hot_set, ohT_ps, oh_set, hm_ps, hm_set, moe_ps, o_set, ix_set) = (sem(n) for n in (
            "x1c_set", "x1T_ps", "x1T_set", "f1_ps", "g_set", "f2_ps", "y2_set", "cf_ord", "x2_set", "xf_set", "xfT_ps",
            "xfT_set", "lg_ps", "lg_used", "hot_set", "ohT_ps", "oh_set", "hm_ps", "hm_set", "moe_ps", "o_set", "ix_set"))
        w1_in = sem("w1_in")
        out_done = [sem("out_done0"), sem("out_done1")]

        NWB = NW // TILE
        EDGE_DMAS, CHUNK_DMAS = 9, 3
        pad0 = E - (P - 1) * EROW
        x_t = x.rearrange("(t p) d -> p t d", p=TILE)
        out_t = out.rearrange("(t p) d -> p t d", p=TILE)
        adj_v = adj.ap().rearrange("(s d) (h l) -> (d h) s l", d=WIN, l=LO)

        def lin(t):
            return t.ap().rearrange("c e -> (c e)").rearrange("(p j) -> p j", j=EROW)

        def node_tile(v, t):
            return v[:, bass.ds(t, 1), :].rearrange("p t d -> p (t d)")

        def skewed(eng, front, back):

            def pair(i):
                front(2 * i + 1, 1, i)
                back(2 * i, 0, i)
                front(2 * i + 2, 0, i + 1)
                back(2 * i + 1, 1, i)

            front(0, 0, 0)
            pair(0)
            with eng.Fori(1, NT // 2) as i:
                pair(i)
            back(NT - 1, 0, NT // 2)

        def each(eng, step):
            for t in range(3):
                step(t, t % 2, t // 2)
            with eng.Fori(1, NT // 2) as i:
                step(2 * i + 1, 1, i)
                step(2 * i + 2, 0, i + 1)

        def grouped(eng, first, rest, last=None):
            first()
            with eng.Fori(0, NG // 2 - 1) as i:
                rest(2 * i + 2, 0, i + 1)
                rest(2 * i + 3, 1, i + 1)
            if last:
                last()

        def wait_from(eng, s, value):
            if not (isinstance(value, int) and value <= 0):
                eng.wait_ge(s, value)

        params = []

        def param(dst_ap, src_ap):
            params.append((dst_ap, src_ap))

        for w_sb, w in ((wk_sb, wk), (wv_sb, wv), (wq_sb, wq), (ws_sb, ws), (wf1_sb, w_ff1), (wf2_sb, w_ff2)):
            param(w_sb[:, :, :], w.rearrange("(k p) n -> p k n", p=P))
        for c_sb, v in ((bk_col, bk), (bq_col, bq), (bf1_col, b_ff1)):
            param(c_sb[:, :], v.rearrange("(k p) -> p k", p=P))
        for nm in ("bv", "bs", "g1", "b1", "g2", "b2", "bf2", "rb"):
            param(rows[nm][0][:, :], rows[nm][1].partition_broadcast(P))
        param(eb1_col[:, :], eb1.rearrange("e h -> (e h)").rearrange("(m p) -> p m", p=P))
        param(eb2_sb[:, :], eb2)
        for k in range(KH):
            param(rw_sb[:, k, :], router_w[:, k * P:(k + 1) * P].rearrange("e p -> p e"))
        param(w2_sb[:, :, :], W2.rearrange("e h d -> (e h) d").rearrange("(m p) d -> p m d", p=P))

        block = ctx.enter_context(nc.Block())

        @block.sync
        def _(sp):
            sp.wait_ge(pads_set, 4)
            cut = 112
            for ap, dram in ((di, dst), (si, src), (w_e, edge_weight)):
                v = dram[0:(P - 1) * EROW].rearrange("(p j) -> p j", j=EROW)
                sp.dma_start(ap[0:cut, 0:EROW], v[0:cut, :]).then_inc(edges_in, 16)
                sp.dma_start(ap[cut:P - 1, 0:EROW], v[cut:P - 1, :]).then_inc(edges_in, 16)
                sp.dma_start(ap[P - 1:P, 0:pad0], dram[(P - 1) * EROW:E].unsqueeze(0)).then_inc(edges_in, 16)
            whole = E // CHUNK // P
            full = whole * P
            rest = E // CHUNK - full
            sp.dma_start(firstc[:, 0:whole, :],
                         dst[0:full * CHUNK].rearrange("(b p e) -> p b e", p=P, e=CHUNK)).then_inc(chunks_in, 16)
            sp.dma_start(firstc[0:rest, whole, :],
                         dst[full * CHUNK:(full + rest) * CHUNK].rearrange("(p e) -> p e", e=CHUNK)).then_inc(chunks_in, 16)
            sp.dma_start(firstc[rest:rest + 1, whole, 0:E % CHUNK],
                         dst[(full + rest) * CHUNK:E].unsqueeze(0)).then_inc(chunks_in, 16)
            sp.wait_ge(code_set, 1)
            sp.dma_start(lin(code_lin), code_e[:, 0:EROW]).then_inc(tab_stored, 16)
            sp.dma_start(lin(lo_lin), srcf[:, 0:EROW]).then_inc(tab_stored, 16)
            sp.wait_ge(val_set, 1)
            sp.dma_start(lin(val_lin), t_e[:, 0:EROW]).then_inc(tab_stored, 16)
            sp.wait_ge(last_set, 1)
            sp.dma_start(last_lin.ap().rearrange("(b p) -> p b", p=TILE), wrow[0:TILE, :],
                         allow_slow_non_contiguous=True).then_inc(last_stored, 16)
            sp.wait_ge(last_stored, 16)
            spread = last_lin.ap().rearrange("(t a) -> a t", a=TILE // WIN)
            for b in range(WIN):
                sp.dma_start(arow0[b:TILE:WIN, :], spread, allow_slow_non_contiguous=True).then_inc(last_in, 16)

            def load(t, s, u):
                wait_from(sp, kh_ready, t - 1)
                sp.dma_start(xt[:, s, :], node_tile(x_t, t)).then_inc(kx_in[s], 16)

            each(sp, load)

            def put(g, s, u):
                sp.wait_ge(stage_ready, g + 1)
                sp.dma_start(adj_v[:, bass.ds(g * GROUP, GROUP), :], stage[0:TILE, s, :, :]).then_inc(stored[s], 16)

            grouped(sp, lambda: (put(0, 0, 0), put(1, 1, 0)), put)

            def load_x(t, s, u):
                wait_from(sp, h_ready, t - 1)
                sp.dma_start(xt[:, s, :], node_tile(x_t, t)).then_inc(x_in[s], 16)

            sp.wait_ge(kh_ready, NT)
            each(sp, load_x)

            sp.wait_ge(s_used, len(SCH) * NT)
            for k in range(KH):
                sp.dma_start(w1_sb[:, k, :, :], W1[:, k * P:(k + 1) * P, :].rearrange("e p h -> p e h")).then_inc(w1_in, 16)

            def load_c(t, s, u):
                wait_from(sp, x2_set, t - 1)
                sp.dma_start(xt[:, s, :], node_tile(x_t, t)).then_inc(cx_in[s], 16)

            def put_o(t, s, u):
                sp.wait_ge(o_set, t + 1)
                sp.dma_start(node_tile(out_t, t), o_sb[0:TILE, s, :]).then_inc(out_done[s], 16)

            sp.wait_ge(h_ready, NT)
            skewed(sp, load_c, put_o)
            sp.wait_ge(out_done[0], 16 * (NT // 2 + 1))
            sp.wait_ge(out_done[1], 16 * (NT // 2))

        @block.gpsimd
        def _(pool):
            order = Order(pool, pool_ord)
            nc.gpsimd.memset(ident[:, :], 0.0).then_inc(pool_ord, 1)
            nc.gpsimd.memset(sel[:, :, :, :], 0.0).then_inc(pool_ord, 1)
            order.n = 2
            nc.gpsimd.memset(ones[:, :], 1.0).then_inc(consts_set, 1)
            nc.gpsimd.memset(kT[:, :, :, TILE:LO], 0.0).then_inc(consts_set, 1)
            nc.gpsimd.iota(iota_row[:, :], [[1, P]], base=0, channel_multiplier=0,
                           allow_small_or_imprecise_dtypes=True).then_inc(consts_set, 1)
            nc.gpsimd.iota(iota_c[:, :], [[1, CB * P]], base=0, channel_multiplier=0,
                           allow_small_or_imprecise_dtypes=True).then_inc(consts_set, 1)
            nc.gpsimd.iota(step_col[:, :], [[P, SBLK]], base=0, channel_multiplier=1,
                           allow_small_or_imprecise_dtypes=True).then_inc(consts_set, 1)
            nc.gpsimd.iota(win_col[:, :], [[TILE, NWB]], base=0, channel_multiplier=1,
                           allow_small_or_imprecise_dtypes=True).then_inc(consts_set, 1)
            pool.wait_ge(pool_ord, 2)
            nc.gpsimd.affine_select(out=ident[:, :], in_=ident[:, :], compare_op=ALU.not_equal, fill=1.0, base=0,
                                    pattern=[[-1, P]], channel_multiplier=1).then_inc(consts_set, 1)
            nc.gpsimd.affine_select(out=sel[:, :, :, :], in_=sel[:, :, :, :], compare_op=ALU.not_equal, fill=1.0, base=0,
                                    pattern=[[-2, NM], [-1, 2], [0, HID]], channel_multiplier=1).then_inc(consts_set, 1)

            pool.wait_ge(idx_set, 1)
            pool.wait_ge(tab_stored, 3 * 16)
            for b in range(SBLK):
                if b >= 2:
                    pool.wait_ge(tabT_done, b - 1)
                for c, t in enumerate((code_lin, lo_lin, val_lin)):
                    nc.gpsimd.indirect_dma_start(
                        gath[:, b % 2, c, :], None, t.ap()[:, :],
                        bass.IndirectOffsetOnAxis(ap=cidx[:, b:b + 1], axis=0)).then_inc(gath_in[b % 2], 16)

            def one_hot(g, s, u):
                if not (isinstance(g, int) and g < 2):
                    pool.wait_ge(prod_done, g - 1)
                nc.gpsimd.tensor_copy(cur[:, s, :, :], cv_tab[:, bass.ds(g * GROUP, GROUP), :]).then_inc(cur_set, 1)
                pool.wait_ge(cur_set, g + 1)
                pool.sem_inc(pool_mark, 1)
                for k in range(GROUP):
                    ins = nc.gpsimd.tensor_scalar(Xs[:, s, k, :], iota_row[:, 0:TILE], cur[:, s, k, 0:1],
                                                  cur[:, s, k, 1:2], ALU.is_equal, ALU.mult)
                ins.then_inc(x_ready, 1)

            pool.wait_ge(tab_set, SBLK)
            grouped(pool, lambda: (one_hot(0, 0, 0), one_hot(1, 1, 0)), one_hot)

            pool.wait_ge(arow_set, 1)
            for s in range(2):
                pool.wait_ge(stored[s], 16 * (NG // 2))

            def fetch(t, s, u):
                wait_from(pool, p_ready, t - 1)
                nc.gpsimd.tensor_copy(gidx[0:TILE, s:s + 1], arow[0:TILE, bass.ds(t, 1)]).then_inc(gidx_set, 1)
                pool.wait_ge(gidx_set, t + 1)
                pool.sem_inc(pool_mark, 1)
                nc.gpsimd.indirect_dma_start(
                    A_sb[0:TILE, s, :], None, adj.ap()[:, :],
                    bass.IndirectOffsetOnAxis(ap=gidx[0:TILE, s:s + 1], axis=0)).then_inc(a_in[s], 16)

            each(pool, fetch)

            pool.wait_ge(x1_ready, NT)

            def pick(t, s, u):
                wait_from(pool, y2_set, t - 1)
                nc.gpsimd.tensor_copy(x1c[0:TILE, s, :], node_tile(x1, t)).then_inc(x1c_set, 1)

            each(pool, pick)

        @block.scalar
        def _(act):
            for nm in ("we", "be"):
                act.dma_start(rows[nm][0][:, :], rows[nm][1].rearrange("a b -> (a b)").partition_broadcast(P) if nm == "we" else rows[nm][1].partition_broadcast(P)).then_inc(scal_in, 16)
            for dst_ap, src_ap in params:
                act.dma_start(dst_ap, src_ap, allow_slow_non_contiguous=True).then_inc(params_in, 16)
            act.wait_ge(guard_set, 1)
            nc.scalar.activation(t_e[:, 0:EROW], t_e[:, 0:EROW], ACT.Exp).then_inc(val_set, 1)
            for b in range(SBLK):
                act.wait_ge(tabT_done, b + 1)
                cols = slice(b * P, (b + 1) * P)
                ps = bank[6 + b % 2]
                nc.scalar.copy(cv_tab[:, cols, 0], ps[:, 0:P])
                nc.scalar.copy(lo_tab[:, cols], ps[:, P:2 * P])
                nc.scalar.copy(cv_tab[:, cols, 1], ps[:, 2 * P:3 * P]).then_inc(tab_set, 1)
            act.wait_ge(params_in, 16 * len(params))

            def k_front(t, s, u):
                act.wait_ge(khT_ps, t + 1)
                wait_from(act, v_ps, t - 1)
                nc.scalar.copy(hT[:, s, :, :], bank[2 + s][:, 0:KH * TILE].rearrange("p (k t) -> p k t", k=KH)).then_inc(khT_ready, 1)

            def k_back(t, s, u):
                act.wait_ge(k_ps, t + 1)
                if isinstance(t, int) and t == NT - 1:
                    pass
                for m in range(KH):
                    ins = nc.scalar.activation(kT[:, m, bass.ds(t, 1), 0:TILE].rearrange("p a l -> p (a l)"),
                                               bank[4 + s][:, m * TILE:(m + 1) * TILE], ACT.Identity, bias=bk_col[:, m:m + 1])
                ins.then_inc(k_ready, 1)

            act.wait_ge(consts_set, 8)
            skewed(act, k_front, k_back)

            nc.scalar.mul(bqs_col[:, :], bq_col[:, :], SCALE).then_inc(q_ready, 1)

            def front(t, s, u):
                act.wait_ge(hT_ps, t + 1)
                wait_from(act, attn_done, t - 1)
                nc.scalar.copy(hT[:, s, :, :], bank[6][:, 0:KH * TILE].rearrange("p (k t) -> p k t", k=KH)).then_inc(hT_ready, 1)
                act.wait_ge(q_ps, t + 1)
                if isinstance(t, int):
                    act.wait_ge(q_ready, 1)
                for m in range(KH):
                    ins = nc.scalar.activation(qT[:, s, m, :], bank[7][:, m * TILE:(m + 1) * TILE], ACT.Identity,
                                               bias=bqs_col[:, m:m + 1], scale=SCALE)
                ins.then_inc(q_ready, 1)
                act.wait_ge(nmax_set, t + 1)
                nc.scalar.activation(Z[0:TILE, s, :], Z[0:TILE, s, :], ACT.Exp, bias=nmax[:, s:s + 1]).then_inc(e_ready, 1)

            def back(t, s, u):
                wait_from(act, attn_done, t)
                for g, (j, n) in enumerate(TRG):
                    act.wait_ge(tr_ready, len(TRG) * t + g + 1)
                    nc.scalar.copy(PT[0:TILE, j:j + n, :], bank[3 + g % 2][0:TILE, 0:n * TILE].rearrange(
                        "p (n d) -> p n d", n=n)).then_inc(pt_ready, 1)

            skewed(act, front, back)

            def c_front(t, s, u):
                act.wait_ge(x1T_ps, t + 1)
                nc.scalar.copy(x1T[:, s, :, :], bank[0][:, 0:KH * TILE].rearrange("p (k t) -> p k t", k=KH)).then_inc(x1T_set, 1)
                act.wait_ge(f1_ps, t + 1)
                for m in range(FF // P):
                    ins = nc.scalar.activation(gT[:, s, m, :], bank[1][:, m * TILE:(m + 1) * TILE], ACT.Gelu_apprx_tanh,
                                               bias=bf1_col[:, m:m + 1])
                ins.then_inc(g_set, 1)
                act.wait_ge(xfT_ps, t + 1)
                wait_from(act, moe_ps, t - 1)
                nc.scalar.copy(xfT[:, s, :, :], bank[3][:, 0:KH * TILE].rearrange("p (k t) -> p k t", k=KH)).then_inc(xfT_set, 1)

            def c_back(t, s, u):
                for q in range(NM // 4):
                    act.wait_ge(hm_ps, NM // 4 * t + q + 1)
                    for j in range(4):
                        m = 4 * q + j
                        ins = nc.scalar.activation(hmT[:, s, m, :], bank[6 + q % 2][:, j * TILE:(j + 1) * TILE], ACT.Relu,
                                                   bias=eb1_col[:, m:m + 1])
                    ins.then_inc(hm_set, 1)

            skewed(act, c_front, c_back)

        @block.vector
        def _(dve):
            V_ = nc.vector
            V_.memset(di[:, pad0:EROW], N).then_inc(pads_set, 1)
            V_.memset(si[:, pad0:EROW], 0).then_inc(pads_set, 1)
            V_.memset(w_e[:, pad0:EROW], 0.0).then_inc(pads_set, 1)
            V_.memset(firstc[:, CB - 1, :], 1000000).then_inc(pads_set, 1)
            od = Order(dve, dve_ord)
            ed = slice(0, EROW)
            dve.wait_ge(edges_in, 16 * EDGE_DMAS)
            dve.wait_ge(scal_in, 32)
            dve.wait_ge(consts_set, 8)
            dve.wait_ge(chunks_in, 16 * CHUNK_DMAS)
            od(V_.tensor_copy(fcol[:, :], firstc[:, :, 0]))
            od(V_.tensor_scalar(fcol[:, :], fcol[:, :], 1.0 / WIN, 0.5 / WIN - 0.5, ALU.mult, ALU.add))
            od(V_.tensor_scalar_add(fcol[:, :], fcol[:, :], MAGIC))
            od(V_.tensor_scalar_add(fcol[:, :], fcol[:, :], -MAGIC))
            for b in range(CB):
                ins = V_.tensor_scalar(diag[:, b, :], ident[:, :], fcol[:, b:b + 1], None, ALU.mult)
            ins.then_inc(diag_set, 1)
            od(V_.tensor_scalar(w_e[:, ed], w_e[:, ed], row["we"][:, 0:1], row["be"][:, 0:1], ALU.mult, ALU.add))
            od(V_.tensor_copy(dstf[:, ed], di[:, ed]))
            od(V_.tensor_tensor(neg_e[:, 1:EROW], dstf[:, 1:EROW], dstf[:, 0:EROW - 1], ALU.is_equal))
            od(V_.tensor_scalar(neg_e[:, 1:EROW], neg_e[:, 1:EROW], -1.0, BIG, ALU.add, ALU.mult))
            od(V_.memset(neg_e[:, 0:1], -BIG))
            od(V_.memset(neg_e[:, EROW:EROW + 1], -BIG))
            od(V_.tensor_tensor_scan(F_e[:, ed], neg_e[:, ed], w_e[:, ed], -BIG, ALU.add, ALU.max))
            od(V_.tensor_tensor_scan(B_e[:, ed][:, ::-1], neg_e[:, 1:EROW + 1][:, ::-1], F_e[:, ed][:, ::-1], -BIG,
                                     ALU.add, ALU.max))
            dve.wait_ge(rows_bc, 1)
            od(V_.tensor_copy(s_row[:, 0:512], bank[1][:, 0:512]))
            od(V_.tensor_copy(s_row[:, 512:CB * P], bank[2][:, 0:CB * P - 512]))
            od(V_.memset(s_row[:, 0:1], 0.0))
            od(V_.tensor_tensor(o_row[:, :], s_row[:, :], iota_c[:, :], ALU.add))
            firsts, lasts = dstf[:, 0:1], dstf[:, EROW - 1:EROW]
            for q, col in enumerate((firsts, lasts, B_e[:, 0:1], B_e[:, EROW - 1:EROW])):
                ins = V_.tensor_scalar(diag[:, q, :], ident[:, :], col, None, ALU.mult)
            ins.then_inc(diag_set, 1)
            for b in range(SBLK):
                od(V_.tensor_scalar(cmp_o[:, :], o_row[:, :], step_col[:, b:b + 1], None, ALU.is_le))
                od(V_.tensor_reduce(cnt[:, b:b + 1], cmp_o[:, :], AX, ALU.add))
            od(V_.tensor_scalar_add(cnt[:, :], cnt[:, :], -1.0))
            V_.tensor_copy(cidx[:, :], cnt[:, :]).then_inc(idx_set, 1)
            od(V_.tensor_tensor(wneg[:, :], cnt[:, :], step_col[:, :], ALU.subtract))
            od(V_.tensor_scalar_mul(wneg[:, :], wneg[:, :], float(WIN * NT)))
            for b in range(NWB):
                od(V_.tensor_scalar(cmp_o[0:TILE, :], s_row[0:TILE, :], win_col[0:TILE, b:b + 1], None, ALU.is_le))
                od(V_.tensor_reduce(wcnt[0:TILE, b:b + 1], cmp_o[0:TILE, :], AX, ALU.add))
            od(V_.tensor_tensor(wcnt[0:TILE, :], wcnt[0:TILE, :], win_col[0:TILE, :], ALU.add))
            od(V_.tensor_scalar(wcnt[0:TILE, :], wcnt[0:TILE, :], -1.0, float(WIN), ALU.add, ALU.mult))
            V_.tensor_copy(wrow[0:TILE, :], wcnt[0:TILE, :]).then_inc(last_set, 1)
            dve.wait_ge(rows_bc, 2)
            for q, col in enumerate((firsts, lasts)):
                od(V_.tensor_scalar(segcmp[:, :], bank[0][:, 0:2 * P], col, -1.0, ALU.is_equal, ALU.add))
                od(V_.scalar_tensor_tensor(segval[:, :], segcmp[:, :], BIG, bank[0][:, 2 * P:4 * P], ALU.mult, ALU.add))
                od(V_.tensor_reduce(guards[:, q:q + 1], segval[:, :], AX, ALU.max))
            for q, col in enumerate((firsts, lasts)):
                od(V_.tensor_scalar(t_e[:, ed], dstf[:, ed], col, -1.0, ALU.is_equal, ALU.add))
                od(V_.tensor_scalar(t_e[:, ed], t_e[:, ed], BIG, guards[:, q:q + 1], ALU.mult, ALU.add))
                od(V_.tensor_tensor(B_e[:, ed], B_e[:, ed], t_e[:, ed], ALU.max))
            V_.scalar_tensor_tensor(t_e[:, ed], w_e[:, ed], SHIFT, B_e[:, ed], ALU.add, ALU.subtract).then_inc(guard_set, 1)
            od(V_.tensor_copy(srcf[:, ed], si[:, ed]))
            od(V_.tensor_scalar(hi_e[:, ed], srcf[:, ed], 1.0 / TILE, 0.5 / TILE - 0.5, ALU.mult, ALU.add))
            od(V_.tensor_scalar_add(hi_e[:, ed], hi_e[:, ed], MAGIC))
            od(V_.tensor_scalar_add(hi_e[:, ed], hi_e[:, ed], -MAGIC))
            od(V_.scalar_tensor_tensor(code_e[:, ed], dstf[:, ed], float(NT), hi_e[:, ed], ALU.mult, ALU.add))
            V_.scalar_tensor_tensor(srcf[:, ed], hi_e[:, ed], -float(TILE), srcf[:, ed], ALU.mult, ALU.add).then_inc(code_set, 1)
            for b in range(SBLK):
                if b == 0:
                    dve.wait_ge(rows_bc, 2)
                ins = V_.tensor_scalar(diag[:, b, :], ident[:, :], cnt[:, b:b + 1], None, ALU.mult)
            ins.then_inc(diag_set, 1)
            dve.wait_ge(rows_bc, 3)
            for c in range(0, SLOTS, 512):
                n = min(512, SLOTS - c)
                od(V_.tensor_copy(c_row[:, c:c + n], bank[3 + c // 512][:, 0:n]))
            od(V_.tensor_tensor(keep_tab[:, 1:SLOTS], c_row[:, 1:SLOTS], c_row[:, 0:SLOTS - 1], ALU.subtract))
            od(V_.memset(keep_tab[:, 0:1], 0.0))
            od(V_.tensor_scalar(pmod[:, :], step_col[:, 0:1], 1.0 / WIN, 0.5 / WIN - 0.5, ALU.mult, ALU.add))
            od(V_.tensor_scalar_add(pmod[:, :], pmod[:, :], MAGIC))
            od(V_.tensor_scalar_add(pmod[:, :], pmod[:, :], -MAGIC))
            od(V_.scalar_tensor_tensor(pmod[:, :], pmod[:, :], -float(WIN), step_col[:, 0:1], ALU.mult, ALU.add))
            dve.wait_ge(last_in, 16 * WIN)
            od(V_.tensor_copy(arowf[0:TILE, :], arow0[0:TILE, :]))
            od(V_.tensor_scalar_add(arowf[0:TILE, :], arowf[0:TILE, :], pmod[0:TILE, 0:1]))
            V_.tensor_copy(arow[0:TILE, :], arowf[0:TILE, :]).then_inc(arow_set, 1)
            for b in range(SBLK):
                dve.wait_ge(gath_in[b % 2], 3 * 16 * (b // 2 + 1))
                V_.tensor_scalar_add(gath[:, b % 2, 0, :], gath[:, b % 2, 0, :], wneg[:, b:b + 1]).then_inc(rel_set, 1)

            def norm(order, src_ap, out_ap):
                order(V_.bn_stats(st6[:, :], src_ap), dve_mark)
                order(V_.bn_aggr(mv[:, :], st6[:, :]))
                order(V_.tensor_scalar_add(var[:, :], mv[:, 1:2], EPS))
                order(V_.tensor_single_scalar(rstd[:, :].bitcast(I32), var[:, :].bitcast(I32), 1, ALU.logical_shift_right))
                order(V_.tensor_scalar(rstd[:, :].bitcast(I32), rstd[:, :].bitcast(I32), -1.0, RSQRT, ALU.mult, ALU.add))
                for _ in range(NEWTON):
                    order(V_.scalar_tensor_tensor(half[:, :], rstd[:, :], var[:, 0:1], rstd[:, :], ALU.mult, ALU.mult))
                    order(V_.tensor_scalar(half[:, :], half[:, :], -0.5, 1.5, ALU.mult, ALU.add))
                    order(V_.tensor_tensor(rstd[:, :], rstd[:, :], half[:, :], ALU.mult))
                return V_.tensor_scalar(out_ap, src_ap, mv[:, 0:1], rstd[:, 0:1], ALU.subtract, ALU.mult)

            k_ord = Order(dve, kv_ord, NORM)
            dve.wait_ge(params_in, 16 * len(params))

            def k_front(t, s, u):
                k_ord.begin(t)
                dve.wait_ge(kx_in[s], 16 * (u + 1))
                wait_from(dve, khT_ps, t - 1)
                norm(k_ord, xt[:, s, :], h[:, s, :]).then_inc(kh_ready, 1)
                k_ord.end()

            def k_back(t, s, u):
                dve.wait_ge(v_ps, t + 1)
                V_.tensor_tensor(node_tile(V, t), bank[6 + s][0:TILE, 0:D], row["bv"][0:TILE, :], ALU.add).then_inc(v_ready, 1)

            skewed(dve, k_front, k_back)

            def columns(g, s, u):
                if not (isinstance(g, int) and g < 2):
                    dve.wait_ge(prod_done, g - 1)
                V_.tensor_tensor(Ys[:, s, :, :], iota_row[:, :].unsqueeze(1).to_broadcast([P, GROUP, LO]),
                                 lo_tab[:, bass.ds(g * GROUP, GROUP)].unsqueeze(2).to_broadcast([P, GROUP, LO]),
                                 ALU.is_equal).then_inc(y_ready, 1)

            a_ord = Order(dve, acc_ord, GROUP - 1)

            def sums(g, s, u):
                a_ord.begin(g)
                dve.wait_ge(prod_done, g + 1)
                wait_from(dve, stored[s], 16 * u)
                if not (isinstance(g, int) and g < 1):
                    dve.wait_ge(stage_ready, g)
                for k in range(GROUP):
                    prev = stage[0:TILE, s, k - 1, :] if k else stage[0:TILE, 1 - s, GROUP - 1, :]
                    ps = bank[s][0:TILE, k * LO:(k + 1) * LO]
                    if isinstance(g, int) and g == 0 and k == 0:
                        ins = V_.tensor_copy(stage[0:TILE, s, k, :], ps)
                    else:
                        ins = V_.scalar_tensor_tensor(stage[0:TILE, s, k, :], prev,
                                                      keep_tab[0:TILE, bass.ds(g * GROUP + k, 1)], ps, ALU.mult, ALU.add)
                    if k < GROUP - 1:
                        a_ord(ins)
                ins.then_inc(stage_ready, 1)
                a_ord.end()

            dve.wait_ge(tab_set, SBLK)

            def ahead(i):
                columns(2 * i + 2, 0, i + 1)
                sums(2 * i + 1, 1, i)
                columns(2 * i + 3, 1, i + 1)
                sums(2 * i + 2, 0, i + 1)

            columns(0, 0, 0)
            columns(1, 1, 0)
            sums(0, 0, 0)
            ahead(0)
            with dve.Fori(1, NG // 2 - 1) as i:
                ahead(i)
            sums(NG - 1, 1, NG // 2 - 1)

            f_ord = Order(dve, front_ord, NORM + 1 + 1)
            b_ord = Order(dve, back_ord, NORM + 4)
            pool_free = [None]

            def front(t, s, u):
                f_ord.begin(t)
                dve.wait_ge(x_in[s], 16 * (u + 1))
                wait_from(dve, hT_ps, t - 1)
                norm(f_ord, xt[:, s, :], h[:, s, :]).then_inc(h_ready, 1)
                dve.wait_ge(a_in[s], 16 * (u + 1))
                wait_from(dve, tr_ready, len(TRG) * (t - 1))
                f_ord(V_.tensor_scalar(Z[0:TILE, s, :], A_sb[0:TILE, s, :], 0.0, -BIG, ALU.is_equal, ALU.mult))
                for b, (c, n) in enumerate(SCH):
                    dve.wait_ge(s_ready, len(SCH) * t + b + 1)
                    dve.sem_inc(dve_mark, 1)
                    V_.tensor_tensor_reduce(out=Z[0:TILE, s, c:c + n], in0=bank[b % 3][0:TILE, 0:n], in1=Z[0:TILE, s, c:c + n],
                                            scale=1.0, scalar=-BIG, op0=ALU.add, op1=ALU.max,
                                            accum_out=mx[:, b:b + 1]).then_inc(s_used, 1)
                dve.wait_ge(s_used, len(SCH) * (t + 1))
                f_ord(V_.tensor_reduce(mxr[:, :], mx[:, 0:len(SCH)], AX, ALU.max))
                V_.tensor_scalar(nmax[:, s:s + 1], mxr[:, :], -1.0, SHIFT, ALU.mult, ALU.add).then_inc(nmax_set, 1)
                dve.wait_ge(e_ready, t + 1)
                V_.tensor_tensor_reduce(out=Z[0:TILE, s, :], in0=Z[0:TILE, s, :], in1=A_sb[0:TILE, s, :], scale=1.0,
                                        scalar=0.0, op0=ALU.mult, op1=ALU.add, accum_out=den[:, s:s + 1]).then_inc(p_ready, 1)
                f_ord.end()

            def back(t, s, u):
                b_ord.begin(t)
                dve.wait_ge(p_ready, t + 1)
                b_ord(V_.tensor_scalar_max(rden[:, s:s + 1], den[:, s:s + 1], 1e-37))
                b_ord(V_.reciprocal(rden[:, s:s + 1], rden[:, s:s + 1]))
                dve.wait_ge(attn_done, t + 1)
                b_ord(V_.scalar_tensor_tensor(yt[:, :], bank[5][0:TILE, 0:D], rden[:, s:s + 1], h[:, s, :], ALU.mult, ALU.add))
                V_.tensor_tensor(yt[:, :], yt[:, :], bank[5][0:TILE, D:2 * D], ALU.add).then_inc(o_used, 1)
                dve.wait_ge(o_used, t + 1)
                b_ord(V_.tensor_tensor(yt[:, :], yt[:, :], row["bs"][0:TILE, :], ALU.add))
                x1_t = node_tile(x1, t)
                ins = norm(b_ord, yt[:, :], yt[:, :])
                ins.then_inc(norm_set, 1)
                dve.wait_ge(norm_set, 2 * t + 1)
                V_.tensor_tensor(yt[:, :], yt[:, :], row["g1"][0:TILE, :], ALU.mult).then_inc(norm_set, 1)
                dve.wait_ge(norm_set, 2 * t + 2)
                V_.tensor_tensor(x1_t, yt[:, :], row["b1"][0:TILE, :], ALU.add).then_inc(x1_ready, 1)
                b_ord.end()

            skewed(dve, front, back)

            c_ord = Order(dve, cf_ord, 2 * NORM + 6)

            def c_front(t, s, u):
                c_ord.begin(t)
                dve.wait_ge(f2_ps, t + 1)
                dve.wait_ge(x1c_set, t + 1)
                V_.tensor_tensor(y2[0:TILE, s, :], bank[2][0:TILE, 0:D], x1c[0:TILE, s, :], ALU.add).then_inc(y2_set, 1)
                dve.wait_ge(y2_set, t + 1)
                c_ord(V_.tensor_tensor(y2[0:TILE, s, :], y2[0:TILE, s, :], row["bf2"][0:TILE, :], ALU.add))
                c_ord(norm(c_ord, y2[0:TILE, s, :], y2[0:TILE, s, :]))
                c_ord(V_.tensor_tensor(y2[0:TILE, s, :], y2[0:TILE, s, :], row["g2"][0:TILE, :], ALU.mult))
                c_ord(V_.tensor_tensor(y2[0:TILE, s, :], y2[0:TILE, s, :], row["b2"][0:TILE, :], ALU.add))
                dve.wait_ge(cx_in[s], 16 * (u + 1))
                V_.tensor_tensor(x2[0:TILE, s, :], y2[0:TILE, s, :], xt[:, s, :], ALU.add).then_inc(x2_set, 1)
                dve.wait_ge(x2_set, t + 1)
                wait_from(dve, xfT_ps, t - 1)
                norm(c_ord, x2[0:TILE, s, :], xf[0:TILE, s, :]).then_inc(xf_set, 1)
                dve.wait_ge(lg_ps, t + 1)
                V_.tensor_tensor(lg[0:TILE, s, :], bank[4][0:TILE, 0:NEXP], row["rb"][0:TILE, :], ALU.add).then_inc(lg_used, 1)
                dve.wait_ge(lg_used, t + 1)
                dve.sem_inc(dve_mark, 1)
                c_ord(V_.max(mx8[:, :], lg[0:TILE, s, :]), dve_mark)
                c_ord(V_.max_index(ix8[:, :], mx8[:, :], lg[0:TILE, s, :]))
                V_.tensor_copy(ixf[:, :], ix8[:, 0:1]).then_inc(ix_set, 1)
                dve.wait_ge(ix_set, t + 1)
                V_.tensor_scalar(hot[0:TILE, s, :], iota_row[0:TILE, 0:NEXP], ixf[:, 0:1], None, ALU.is_equal).then_inc(hot_set, 1)
                dve.wait_ge(ohT_ps, t + 1)
                wait_from(dve, moe_ps, t - 1)
                V_.tensor_copy(ohT[0:NEXP, s, :], bank[4][0:NEXP, 128:128 + TILE])
                V_.tensor_scalar(negT[:, s, :], bank[4][0:NEXP, 128:128 + TILE], -1.0, BIG, ALU.add, ALU.mult).then_inc(oh_set, 1)
                c_ord.end()

            def c_back(t, s, u):
                dve.wait_ge(moe_ps, t + 1)
                wait_from(dve, out_done[s], 16 * u)
                V_.scalar_tensor_tensor(o_sb[0:TILE, s, :], bank[5][0:TILE, D:2 * D], 0.0, x2[0:TILE, s, :],
                                        ALU.max, ALU.add).then_inc(o_set, 1)

            skewed(dve, c_front, c_back)

        @block.tensor
        def _(pe):
            mm = nc.tensor.matmul
            tr = nc.tensor.transpose
            pe.wait_ge(consts_set, 8)
            pe.wait_ge(diag_set, 1)
            mm(bank[1][:, 0:512], ones[:, :], diag[:, 0:4, :], start=True, stop=True)
            mm(bank[2][:, 0:(CB - 4) * P], ones[:, :], diag[:, 4:CB, :], start=True, stop=True).then_inc(rows_bc, 1)
            pe.wait_ge(diag_set, 2)
            mm(bank[0][:, 0:512], ones[:, :], diag[:, 0:4, :], start=True, stop=True).then_inc(rows_bc, 1)
            pe.wait_ge(diag_set, 3)
            for q in range(0, SBLK, 4):
                n = min(4, SBLK - q)
                ins = mm(bank[3 + q // 4][:, 0:n * P], ones[:, :], diag[:, q:q + n, :], start=True, stop=True)
            ins.then_inc(rows_bc, 1)
            for b in range(SBLK):
                pe.wait_ge(rel_set, b + 1)
                if b >= 2:
                    pe.wait_ge(tab_set, b - 1)
                for c in range(3):
                    ins = tr(bank[6 + b % 2][:, c * P:(c + 1) * P], gath[:, b % 2, c, :], ident[:, :])
                ins.then_inc(tabT_done, 1)

            pe.wait_ge(params_in, 16 * len(params))
            pe.wait_ge(tab_set, SBLK)
            pe.wait_ge(arow_set, 1)

            def transposed(src_ap, ps):
                for k in range(KH):
                    ins = tr(ps[:, k * TILE:(k + 1) * TILE], src_ap[:, k * P:(k + 1) * P], ident[0:TILE, 0:TILE])
                return ins

            def k_front(t, s, u):
                pe.wait_ge(kh_ready, t + 1)
                wait_from(pe, khT_ready, t - 1)
                transposed(h[:, s, :], bank[2 + s]).then_inc(khT_ps, 1)

            def k_back(t, s, u):
                pe.wait_ge(khT_ready, t + 1)
                wait_from(pe, k_ready, t)
                for m in range(KH):
                    for k in range(KH):
                        ins = mm(bank[4 + s][:, m * TILE:(m + 1) * TILE], wk_sb[:, k, m * P:(m + 1) * P], hT[:, s, k, :],
                                 start=(k == 0), stop=(k == KH - 1))
                ins.then_inc(k_ps, 1)
                wait_from(pe, v_ready, t)
                for k in range(KH):
                    ins = mm(bank[6 + s][0:TILE, 0:D], hT[:, s, k, :], wv_sb[:, k, :], start=(k == 0), stop=(k == KH - 1))
                ins.then_inc(v_ps, 1)

            skewed(pe, k_front, k_back)

            def product(g, s, u):
                pe.wait_ge(x_ready, g + 1)
                pe.wait_ge(y_ready, g + 1)
                if not (isinstance(g, int) and g < 2):
                    pe.wait_ge(stage_ready, g - 1)
                for k in range(GROUP):
                    ins = mm(bank[s][0:TILE, k * LO:(k + 1) * LO], Xs[:, s, k, :], Ys[:, s, k, :], start=True, stop=True)
                ins.then_inc(prod_done, 1)

            grouped(pe, lambda: (product(0, 0, 0), product(1, 1, 0)), product)

            pe.wait_ge(stage_ready, NG)
            pe.wait_ge(k_ready, NT)
            pe.wait_ge(v_ready, NT)

            def front(t, s, u):
                pe.wait_ge(h_ready, t + 1)
                wait_from(pe, hT_ready, t)
                transposed(h[:, s, :], bank[6]).then_inc(hT_ps, 1)
                pe.wait_ge(hT_ready, t + 1)
                wait_from(pe, q_ready, t + 1)
                for m in range(KH):
                    for k in range(KH):
                        ins = mm(bank[7][:, m * TILE:(m + 1) * TILE], wq_sb[:, k, m * P:(m + 1) * P], hT[:, s, k, :],
                                 start=(k == 0), stop=(k == KH - 1))
                ins.then_inc(q_ps, 1)
                pe.wait_ge(q_ready, t + 2)
                for b, (c, n) in enumerate(SCH):
                    wait_from(pe, s_used, len(SCH) * t + (b - 2 if b >= 3 else 0))
                    for k in range(KH):
                        ins = mm(bank[b % 3][0:TILE, 0:n], qT[:, s, k, :],
                                 kT[:, k, c // LO:(c + n) // LO, :].rearrange("p j l -> p (j l)"),
                                 start=(k == 0), stop=(k == KH - 1))
                    ins.then_inc(s_ready, 1)

            def back(t, s, u):
                wait_from(pe, o_used, t)
                for k in range(KH):
                    mm(bank[5][0:TILE, D:2 * D], hT[:, s, k, :], ws_sb[:, k, :], start=(k == 0), stop=(k == KH - 1))
                pe.wait_ge(p_ready, t + 1)

                def weigh(g):
                    j0, n = TRG[g]
                    pe.wait_ge(pt_ready, len(TRG) * t + g + 1)
                    for j in range(j0, j0 + n):
                        ins = mm(bank[5][0:TILE, 0:D], PT[0:TILE, j, :], V[:, j, :], start=(j == 0), stop=(j == NT - 1))
                    return ins

                for g, (j0, n) in enumerate(TRG):
                    wait_from(pe, pt_ready, len(TRG) * t + (g - 1 if g >= 2 else 0))
                    for j in range(n):
                        ins = tr(bank[3 + g % 2][0:TILE, j * TILE:(j + 1) * TILE],
                                 Z[0:TILE, s, (j0 + j) * LO:(j0 + j) * LO + TILE], ident[0:TILE, 0:TILE])
                    ins.then_inc(tr_ready, 1)
                    if g:
                        weigh(g - 1)
                weigh(len(TRG) - 1).then_inc(attn_done, 1)

            skewed(pe, front, back)

            pe.wait_ge(x1_ready, NT)
            pe.wait_ge(w1_in, 16 * KH)

            def c_front(t, s, u):
                pe.wait_ge(x1c_set, t + 1)
                wait_from(pe, x1T_set, t)
                transposed(x1c[0:TILE, s, :], bank[0]).then_inc(x1T_ps, 1)
                pe.wait_ge(x1T_set, t + 1)
                wait_from(pe, g_set, t)
                for m in range(FF // P):
                    for k in range(KH):
                        ins = mm(bank[1][:, m * TILE:(m + 1) * TILE], wf1_sb[:, k, m * P:(m + 1) * P], x1T[:, s, k, :],
                                 start=(k == 0), stop=(k == KH - 1))
                ins.then_inc(f1_ps, 1)
                pe.wait_ge(g_set, t + 1)
                wait_from(pe, y2_set, t)
                for m in range(FF // P):
                    ins = mm(bank[2][0:TILE, 0:D], gT[:, s, m, :], wf2_sb[:, m, :], start=(m == 0), stop=(m == FF // P - 1))
                ins.then_inc(f2_ps, 1)
                pe.wait_ge(xf_set, t + 1)
                wait_from(pe, xfT_set, t)
                transposed(xf[0:TILE, s, :], bank[3]).then_inc(xfT_ps, 1)
                pe.wait_ge(xfT_set, t + 1)
                wait_from(pe, oh_set, t)
                for k in range(KH):
                    ins = mm(bank[4][0:TILE, 0:NEXP], xfT[:, s, k, :], rw_sb[:, k, :], start=(k == 0), stop=(k == KH - 1))
                ins.then_inc(lg_ps, 1)
                pe.wait_ge(hot_set, t + 1)
                tr(bank[4][0:NEXP, 128:128 + TILE], hot[0:TILE, s, :], ident[0:TILE, 0:TILE]).then_inc(ohT_ps, 1)

            def c_back(t, s, u):
                pe.wait_ge(oh_set, t + 1)
                for q in range(NM // 4):
                    wait_from(pe, hm_set, NM // 4 * t + (q - 1 if q >= 2 else 0))
                    for j in range(4):
                        m = 4 * q + j
                        o = bank[6 + q % 2][:, j * TILE:(j + 1) * TILE]
                        for k in range(KH):
                            mm(o, w1_sb[:, k, 2 * m:2 * m + 2, :].rearrange("p e h -> p (e h)"), xfT[:, s, k, :],
                               start=(k == 0), stop=False)
                        ins = mm(o, sel[:, m, :, :].rearrange("e q h -> e (q h)"), negT[:, s, :], start=False, stop=True)
                    ins.then_inc(hm_ps, 1)
                wait_from(pe, o_set, t)
                o = bank[5][0:TILE, D:2 * D]
                mm(o, ohT[0:NEXP, s, :], eb2_sb[:, :], start=True, stop=False)
                for m in range(NM):
                    if m % 4 == 0:
                        pe.wait_ge(hm_set, NM // 4 * t + m // 4 + 1)
                    ins = mm(o, hmT[:, s, m, :], w2_sb[:, m, :], start=False, stop=(m == NM - 1))
                ins.then_inc(moe_ps, 1)

            skewed(pe, c_front, c_back)

    return nc


_INS = ['x', 'src', 'dst', 'edge_weight', 'L0_gnn_wq', 'L0_gnn_bq', 'L0_gnn_wk', 'L0_gnn_bk', 'L0_gnn_wv', 'L0_gnn_bv',
        'L0_gnn_ws', 'L0_gnn_bs', 'L0_gnn_we', 'L0_gnn_be', 'L0_gnn_g1', 'L0_gnn_b1', 'L0_gnn_g2', 'L0_gnn_b2',
        'L0_gnn_w_ff1', 'L0_gnn_b_ff1', 'L0_gnn_w_ff2', 'L0_gnn_b_ff2', 'L0_ffn_router_w', 'L0_ffn_router_b',
        'L0_ffn_W1', 'L0_ffn_b1', 'L0_ffn_W2', 'L0_ffn_b2']


def kernel(**inputs):
    import numpy as _np
    import concourse.bacc as _bacc
    from concourse import mybir as _mybir
    from concourse.bass_utils import run_bass_kernel_spmd as _run

    nc = _bacc.Bacc("TRN2", target_bir_lowering=False, num_devices=1)
    arrays, args = {}, []
    for name in _INS:
        a = _np.ascontiguousarray(inputs[name])
        arrays[f"in_{name}"] = a
        args.append(nc.dram_tensor(f"in_{name}", a.shape, _mybir.dt.from_np(a.dtype), kind="ExternalInput").ap())
    out = nc.dram_tensor("out_0", (3125, 256), _mybir.dt.float32, kind="ExternalOutput").ap()
    gnn_moe(nc, *args, out)
    r = _run(nc, [arrays], core_ids=[0])
    return r.results[0]["out_0"]
```

```python
import concourse.bass as bass
from concourse import mybir
from contextlib import ExitStack

F32 = mybir.dt.float32
BF16 = mybir.dt.bfloat16
I32 = mybir.dt.int32
U32 = mybir.dt.uint32
ALU = mybir.AluOpType
ACT = mybir.ActivationFunctionType
AX = mybir.AxisListType.X

N, D, E = 3125, 256, 100000
FF = 2 * D
NEXP, HID = 32, 64
EPS = 1e-5
RSQRT = float(0x5F3759DF)
NEWTON = 3
P = 128
TILE = 125
NT = N // TILE
KH = D // P
CHUNK = 128
SUB = 2
PC = 8
PP = 98
EROW = PC * CHUNK
NC = PP * PC
SPAN = SUB * CHUNK
PS = PC // SUB
NS = PP * PS
WIN = 5
NW = N // WIN
STEPS = -(-E // SPAN) + NW - 1
GROUP = 2
GC = GROUP * SUB
LOADG = 4
BODY = 2 * LOADG
NG = -(-STEPS // (BODY * GROUP)) * BODY
TURNS = NG // BODY
SLOTS = NG * GROUP
SBLK = SLOTS // P
LO = 128
ROW = NT * LO
DIST = 5
TABW = 2 * CHUNK + 3 * CHUNK // 2
BIG = 1e30
MAGIC = 12582912.0
SHIFT = 30.0
SCALE = float(D) ** -0.5
NM = NEXP * HID // P
SCH = [(c, min(512, ROW - c)) for c in range(0, ROW, 512)]
TRG = [(g, min(4, NT - g)) for g in range(0, NT, 4)]


class Order:

    def __init__(self, eng, sem, per=None):
        self.eng, self.sem, self.per, self.base, self.n = eng, sem, per, 0, 0

    def begin(self, t):
        self.base, self.n = t * self.per, 0

    def end(self):
        assert self.n == self.per, (self.n, self.per)

    def __call__(self, ins, mark=None):
        ins.then_inc(self.sem, 1)
        self.n += 1
        self.eng.wait_ge(self.sem, self.base + self.n)
        if mark is not None:
            self.eng.sem_inc(mark, 1)


def gnn_moe(nc, x, src, dst, edge_weight, wq, bq, wk, bk, wv, bv, ws, bs, we, be, g1, b1, g2, b2,
            w_ff1, b_ff1, w_ff2, b_ff2, router_w, router_b, W1, eb1, W2, eb2, out):
    ctx = ExitStack()
    with ctx:
        def sb(name, shape, dt=F32):
            return ctx.enter_context(nc.sbuf_tensor(name, shape, dt))

        def sem(name):
            return ctx.enter_context(nc.semaphore(name))

        def sem2(name):
            return [sem(name + "0"), sem(name + "1")]

        edge_tab = nc.dram_tensor("edge_tab", [NC, TABW], F32)
        term_rows = nc.dram_tensor("term_rows", [3, SLOTS * SUB, CHUNK], BF16)
        dist_dram = nc.dram_tensor("dist_dram", [DIST, LO], BF16)
        last_lin = nc.dram_tensor("last_lin", [NW], U32)
        adj = nc.dram_tensor("adj", [SLOTS * WIN, ROW], F32)
        q_dram = nc.dram_tensor("q_dram", [NT, P, KH * TILE], F32)

        ident = sb("ident", [P, P])
        ones = sb("ones", [P, P])
        iota_row = sb("iota_row", [P, P])
        step_col = sb("step_col", [P, SBLK])
        win_col = sb("win_col", [P, NW // TILE])
        pmod = sb("pmod", [P, 1])
        dist_line = sb("dist_line", [1, DIST, LO], BF16)
        dist_rhs = sb("dist_rhs", [DIST, LO], BF16)
        sel = sb("sel", [NEXP, NM, 2, HID], BF16)
        wq_sb = sb("wq_sb", [P, KH, D])
        wk_sb = sb("wk_sb", [P, KH, D])
        wv_sb = sb("wv_sb", [P, KH, D])
        ws_sb = sb("ws_sb", [P, KH, D])
        wf1_sb = sb("wf1_sb", [P, KH, FF])
        wf2_sb = sb("wf2_sb", [P, FF // P, D])
        rw_sb = sb("rw_sb", [P, KH, NEXP])
        eb2_sb = sb("eb2_sb", [NEXP, D])
        bq_col = sb("bq_col", [P, KH])
        bqs_col = sb("bqs_col", [P, KH])
        bk_col = sb("bk_col", [P, KH])
        bf1_col = sb("bf1_col", [P, FF // P])
        eb1_col = sb("eb1_col", [P, NM])
        rows = {}
        for nm, src_ap, n in (("bv", bv, D), ("bs", bs, D), ("g1", g1, D), ("b1", b1, D), ("g2", g2, D),
                              ("b2", b2, D), ("bf2", b_ff2, D), ("rb", router_b, NEXP), ("be", be, 1),
                              ("we", we.rearrange("a b -> (a b)"), 1)):
            rows[nm] = (sb(nm + "_row", [P, n]), src_ap)
        row = {k: v[0] for k, v in rows.items()}

        kT = sb("kT", [P, KH, NT, LO])
        V_buf = sb("V", [P, NT * D])
        V = V_buf[0:TILE, :].rearrange("p (t d) -> p t d", d=D)
        w1_sb = kT[:, :, :, :].rearrange("p k j l -> p (k j l)")[:, 0:KH * NEXP * HID].rearrange(
            "p (k e h) -> p k e h", k=KH, e=NEXP)
        w2_sb = V_buf[:, 0:NM * D].rearrange("p (m d) -> p m d", m=NM)
        x1 = sb("x1", [TILE, NT, D])
        ARENA = 21888
        arena = sb("arena", [P, ARENA])
        at = [0]

        def view(cols, rows_=P):
            at[0] += cols
            assert at[0] <= ARENA, at[0]
            return arena[0:rows_, at[0] - cols:at[0]]

        step_space = at[0]
        w_e, neg_e = view(EROW, PP), view(EROW + 1, PP)
        F_e, B_e, t_e, dstf = (view(EROW, PP) for _ in range(4))
        di, si = view(EROW, PP).bitcast(I32), view(EROW, PP).bitcast(I32)
        srcf, hi_e, sq_e, sqh_e = F_e, neg_e, w_e, B_e
        edges_only = at[0]
        tab_e = view(PC * TABW, PP).rearrange("p (k c) -> p k c", k=PC)
        codes_o, vals_o = tab_e[:, :, 0:CHUNK], tab_e[:, :, CHUNK:2 * CHUNK]
        terms_o = tab_e[:, :, 2 * CHUNK:TABW].bitcast(BF16).rearrange("p k (c e) -> p k c e", c=3)
        edges_end = at[0]
        gath = arena[:, 0:SBLK * SUB * TABW].rearrange("p (b u c) -> p b u c", b=SBLK, u=SUB)
        assert SBLK * SUB * TABW <= edges_only
        cmp_o = view(4 * P)
        s_row, o_row, iota_c = view(4 * P), view(4 * P), view(4 * P)
        cmp_s, s_row, o_row, iota_c = (v[:, 0:NS] for v in (cmp_o, s_row, o_row, iota_c))
        diag_flat = view(SBLK * P)
        diag = diag_flat.rearrange("p (b e) -> p b e", b=SBLK)
        s_diag = diag_flat[0:PP, 0:NS]
        diag_c = s_diag.rearrange("p (b e) -> p b e", b=PS)
        c_row = view(SLOTS)
        code_tab, nval_tab = view(SLOTS * SUB), view(SLOTS * SUB)
        keep_tab = view(SLOTS)
        at[0] = step_space
        Xs = view(2 * GC * P).rearrange("p (s k m) -> p s k m", s=2, k=GC)
        Ys = view(2 * GC * LO).rearrange("p (s k l) -> p s k l", s=2, k=GC)
        STAGES = 4
        stage = view(STAGES * GROUP * LO).rearrange("p (s k l) -> p s k l", s=STAGES, k=GROUP)
        LOADW = LOADG * GC * CHUNK
        dist_rows = view(LOADW)[0:DIST, :].bitcast(BF16).rearrange("p (s c) -> p s c", s=2)
        assert at[0] <= edges_end
        at[0] = 0
        A_sb = view(2 * ROW).rearrange("p (s c) -> p s c", s=2)
        Z = view(2 * ROW).rearrange("p (s c) -> p s c", s=2)
        PT = view(2 * NT * TILE).rearrange("p (s j d) -> p s j d", s=2, j=NT)
        at[0] = 0

        def two(*shape):
            n = 2
            for d in shape:
                n *= d
            v = view(n)
            if len(shape) == 1:
                return v.rearrange("p (s c) -> p s c", s=2)
            return v.rearrange("p (s a c) -> p s a c", s=2, a=shape[0])

        gT, hmT, x1T, xfT = two(FF // P, TILE), two(NM, TILE), two(KH, TILE), two(KH, TILE)
        x1c, xf, o_sb = two(D), two(D), two(D)
        x_all = view(NT * D, TILE).rearrange("p (t d) -> p t d", d=D)
        lg, hot, ohT = two(NEXP), two(NEXP), two(TILE)
        negT = sb("negT", [NEXP, 2, TILE], BF16)

        fcol = sb("fcol", [P, PS])
        guards = sb("guards", [P, 2])
        cnt = sb("cnt", [P, SBLK])
        cidx = sb("cidx", [P, SUB, SBLK], U32)
        wneg = sb("wneg", [P, SBLK])
        wcnt = sb("wcnt", [P, NW // TILE])
        wrow = sb("wrow", [P, NW // TILE], U32)
        arow0 = sb("arow0", [P, NT], U32)
        arowf = sb("arowf", [P, NT])
        arow = sb("arow", [P, NT], U32)
        gidx = sb("gidx", [P, 2], U32)

        xt = sb("xt", [TILE, 2, D])
        h = sb("h", [TILE, 2, D])
        hT = sb("hT", [P, 2, KH, TILE])
        qs = sb("qs", [P, 2, KH, TILE])
        qT = sb("qT", [P, 2, KH, TILE])
        st = sb("st", [TILE, NT, 6])
        st2 = sb("st2", [TILE, NT, 6])
        mean = sb("mean", [TILE, NT])
        var = sb("var", [TILE, NT])
        dif = sb("dif", [TILE, NT])
        rstd = sb("rstd", [TILE, NT])
        nmr = sb("nmr", [TILE, NT])
        mx = sb("mx", [TILE, 8])
        mxr = sb("mxr", [TILE, 1])
        nmax = sb("nmax", [TILE, 2])
        den = sb("den", [TILE, 2])
        rden = sb("rden", [TILE, 2])
        yt = sb("yt", [TILE, D])
        mx8 = sb("mx8", [TILE, 8])
        ix8 = sb("ix8", [TILE, 8], U32)
        ixf = sb("ixf", [TILE, 1])

        bank = [ctx.enter_context(nc.psum_tensor(f"bank{i}", [P, 512], F32)) for i in range(8)]

        XLOADS = 5
        (pads_set, dst_in, edges_in, nodes_in, scal_in, kv_params_in, params_in, pool_ord, consts_set, dist_in, ws_set,
         ones_set) = (sem(n) for n in (
            "pads_set", "dst_in", "edges_in", "nodes_in", "scal_in", "kv_params_in", "params_in", "pool_ord", "consts_set",
            "dist_in", "ws_set", "ones_set"))
        dve_mark, pool_mark = sem("dve_mark"), sem("pool_mark")
        dve_ord, diag_set, rows_bc, dist_set = sem("dve_ord"), sem("diag_set"), sem("rows_bc"), sem("dist_set")
        guard_set, val_set, tab_stored = sem("guard_set"), sem("val_set"), sem("tab_stored")
        terms_stored = sem("terms_stored")
        code_set, idx_set, rel_set, tabT_done, tab_set, keep_set = (sem(n) for n in (
            "code_set", "idx_set", "rel_set", "tabT_done", "tab_set", "keep_set"))
        gath_in = [sem(f"gath_in{b}") for b in range(SBLK)]
        last_set, last_stored, last_in, arow_set = (sem(n) for n in ("last_set", "last_stored", "last_in", "arow_set"))
        stats_set = sem("stats_set")
        h_ready, hT_ps, hT_ready, kq_ps, vs_ps, k_ready, q_ready, vs_ready = (sem(n) for n in (
            "h_ready", "hT_ps", "hT_ready", "kq_ps", "vs_ps", "k_ready", "q_ready", "vs_ready"))
        q_stored = sem2("q_stored")
        rows_in = sem2("rows_in")
        dist_done, x_ready, y_ready, prod_done, sum_ord, sums_ready = (sem(n) for n in (
            "dist_done", "x_ready", "y_ready", "prod_done", "sum_ord", "sums_ready"))
        stored = [sem(f"stored{q}") for q in range(STAGES)]
        q_in, a_in = sem2("q_in"), sem2("a_in")
        (gidx_set, s_ready, s_used, nmax_set, e_ready, p_ready, front_ord, tr_ready, pt_ready, attn_done, o_used, back_ord,
         x1_ready) = (sem(n) for n in (
            "gidx_set", "s_ready", "s_used", "nmax_set", "e_ready", "p_ready", "front_ord", "tr_ready", "pt_ready",
            "attn_done", "o_used", "back_ord", "x1_ready"))
        x_in = [sem(f"x_in{i}") for i in range(XLOADS)]
        n1_ord, y2_ord, x1n_set = sem("n1_ord"), sem("y2_ord"), sem("x1n_set")
        (x1c_set, x1T_ps, x1T_set, f1_ps, g_set, f2_ps, y2_used, cf_ord, xf_set, xfT_ps,
         xfT_set, lg_ps, lg_used, hot_set, ohT_ps, oh_set, hm_ps, hm_set, moe_ps, o_set, ix_set) = (sem(n) for n in (
            "x1c_set", "x1T_ps", "x1T_set", "f1_ps", "g_set", "f2_ps", "y2_used", "cf_ord", "xf_set", "xfT_ps", "xfT_set", "lg_ps", "lg_used", "hot_set", "ohT_ps", "oh_set", "hm_ps", "hm_set",
            "moe_ps", "o_set", "ix_set"))
        w_in = sem("w_in")
        out_done = sem2("out_done")

        NWB = NW // TILE
        NCONST = 7
        x_t = x.rearrange("(t p) d -> p t d", p=TILE)
        out_t = out.rearrange("(t p) d -> p t d", p=TILE)
        adj_v = adj.ap().rearrange("(s d) (h l) -> (d h) s l", d=WIN, l=LO)
        q_v = q_dram.ap().rearrange("t p c -> p t c")
        edge_tab_v = edge_tab.ap().rearrange("(p k) c -> p k c", k=PC)

        def node_tile(v, t):
            return v[:, bass.ds(t, 1), :].rearrange("p t d -> p (t d)")

        def skewed(eng, front, back, front_first=True):
            def both(f, b):
                if front_first:
                    front(*f)
                    back(*b)
                else:
                    back(*b)
                    front(*f)

            def pair(i):
                both((2 * i + 1, 1, i), (2 * i, 0, i))
                both((2 * i + 2, 0, i + 1), (2 * i + 1, 1, i))

            front(0, 0, 0)
            pair(0)
            with eng.Fori(1, NT // 2) as i:
                pair(i)
            back(NT - 1, 0, NT // 2)

        def pipeline(eng, *stages):
            most = max(lag for _, lag in stages)
            begin = (most + 4) // 2
            end = NT // 2

            def at_time(i, r):
                for step, lag in stages:
                    c = r - lag
                    if not (isinstance(i, int) and not 0 <= 2 * i + c < NT):
                        step(2 * i + c, c % 2, i + c // 2)

            for t in range(2 * begin):
                at_time(t // 2, t % 2)
            with eng.Fori(begin, end) as i:
                at_time(i, 0)
                at_time(i, 1)
            for t in range(2 * end, NT + most):
                at_time(t // 2, t % 2)

        def staged(norm_, front, back):
            def step(t, s, u, v):
                if not (isinstance(t, int) and t + 1 >= NT):
                    front(t + 1, 1 - s, v)
                if not (isinstance(t, int) and t + 2 >= NT):
                    norm_(t + 2, s, u + 1)
                back(t, s, u)

            norm_(0, 0, 0)
            norm_(1, 1, 0)
            front(0, 0, 0)
            step(0, 0, 0, 0)
            step(1, 1, 0, 1)
            return step

        def each(eng, step):
            for t in range(3):
                step(t, t % 2, t // 2)
            with eng.Fori(1, NT // 2) as i:
                step(2 * i + 1, 1, i)
                step(2 * i + 2, 0, i + 1)

        def turns(eng, step):
            def turn(i):
                for j in range(BODY):
                    step(i * BODY + j, j, i)

            turn(0)
            with eng.Fori(1, TURNS - 1) as i:
                turn(i)
            turn(TURNS - 1)

        def wait_from(eng, s, value):
            if not (isinstance(value, int) and value <= 0):
                eng.wait_ge(s, value)

        first_params, params = [], []
        for w_sb, w in ((wk_sb, wk), (wv_sb, wv), (wq_sb, wq), (ws_sb, ws)):
            first_params.append((w_sb[:, :, :], w.rearrange("(k p) n -> p k n", p=P)))
        for c_sb, v in ((bk_col, bk), (bq_col, bq)):
            first_params.append((c_sb[:, :], v.rearrange("(k p) -> p k", p=P)))
        first_params.append((rows["bv"][0][:, :], rows["bv"][1].partition_broadcast(P)))
        for w_sb, w in ((wf1_sb, w_ff1), (wf2_sb, w_ff2)):
            params.append((w_sb[:, :, :], w.rearrange("(k p) n -> p k n", p=P)))
        params.append((bf1_col[:, :], b_ff1.rearrange("(k p) -> p k", p=P)))
        for nm in ("bs", "g1", "b1", "g2", "b2", "bf2", "rb"):
            params.append((rows[nm][0][:, :], rows[nm][1].partition_broadcast(P)))
        params.append((eb1_col[:, :], eb1.rearrange("e h -> (e h)").rearrange("(m p) -> p m", p=P)))
        params.append((eb2_sb[:, :], eb2))
        for k in range(KH):
            params.append((rw_sb[:, k, :], router_w[:, k * P:(k + 1) * P].rearrange("e p -> p e")))

        block = ctx.enter_context(nc.Block())

        @block.sync
        def _(sp):
            sp.wait_ge(pads_set, 3)
            whole = E // EROW
            cut = whole // 16 * 16
            for ap, dram, s in ((di, dst, dst_in), (w_e, edge_weight, edges_in), (si, src, edges_in)):
                v = dram[0:whole * EROW].rearrange("(p j) -> p j", j=EROW)
                sp.dma_start(ap[0:cut, 0:EROW], v[0:cut, :]).then_inc(s, 16)
                sp.dma_start(ap[cut:whole, 0:EROW], v[cut:whole, :]).then_inc(s, 16)
                sp.dma_start(ap[whole:whole + 1, 0:E - whole * EROW], dram[whole * EROW:E].unsqueeze(0)).then_inc(s, 16)
            for i in range(XLOADS):
                c = slice(i * NT // XLOADS, (i + 1) * NT // XLOADS)
                sp.dma_start(V[:, c, :], x_t[:, c, :]).then_inc(nodes_in, 16)
            sp.wait_ge(dist_set, 1)
            sp.dma_start(dist_dram.ap().rearrange("c l -> (c l)").unsqueeze(0),
                         dist_line[:, :, :].rearrange("o c l -> o (c l)")).then_inc(dist_in, 16)
            sp.wait_ge(dist_in, 16)
            sp.dma_start(dist_rhs[:, :], dist_dram.ap()).then_inc(dist_in, 16)
            sp.wait_ge(last_set, 1)
            sp.dma_start(last_lin.ap().rearrange("(b p) -> p b", p=TILE), wrow[0:TILE, :],
                         allow_slow_non_contiguous=True).then_inc(last_stored, 16)
            sp.wait_ge(last_stored, 16)
            spread = last_lin.ap().rearrange("(t a) -> a t", a=TILE // WIN)
            for b in range(WIN):
                sp.dma_start(arow0[b:TILE:WIN, :], spread, allow_slow_non_contiguous=True).then_inc(last_in, 16)
            sp.wait_ge(code_set, 1)
            sp.wait_ge(val_set, 1)
            sp.dma_start(edge_tab_v, tab_e[:, :, :]).then_inc(tab_stored, 16)
            for b in range(SBLK):
                sp.wait_ge(gath_in[b], 16 * SUB)
                for u in range(SUB):
                    sp.dma_start(term_rows.ap().rearrange("c (i u) e -> i c u e", u=SUB)[b * P:(b + 1) * P, :, u, :],
                                 gath[:, b, u, 2 * CHUNK:TABW].bitcast(BF16).rearrange("p (c e) -> p c e", c=3)
                                 ).then_inc(terms_stored, 16)

            def load_rows(n, s):
                sp.dma_start(dist_rows[2:DIST, s, :], term_rows.ap().rearrange("c i e -> c (i e)")[
                    :, bass.ds(n * LOADW, LOADW)]).then_inc(rows_in[s], 16)

            sp.wait_ge(terms_stored, 16 * SUB * SBLK)
            sp.wait_ge(tabT_done, SBLK)
            load_rows(0, 0)
            load_rows(1, 1)

            def put(g, j, i):
                if j % LOADG == 2 and not (isinstance(i, int) and i == TURNS - 1):
                    sp.wait_ge(dist_done, g + 2)
                    load_rows(2 * i + j // LOADG + 2, j // LOADG)
                sp.wait_ge(sums_ready, g + 1)
                sp.dma_start(adj_v[:, bass.ds(g * GROUP, GROUP), :],
                             stage[0:TILE, j % STAGES, :, :]).then_inc(stored[j % STAGES], 16)

            turns(sp, put)

            def load_q(t, s, u):
                wait_from(sp, s_ready, len(SCH) * (t - 1))
                sp.dma_start(qT[:, s, :, :].rearrange("p k t -> p (k t)"),
                             q_v[:, bass.ds(t, 1), :].rearrange("p t c -> p (t c)")).then_inc(q_in[s], 16)

            sp.wait_ge(q_stored[0], 16 * (NT // 2 + 1))
            sp.wait_ge(q_stored[1], 16 * (NT // 2))
            each(sp, load_q)

            sp.wait_ge(s_ready, len(SCH) * NT)
            for k in range(KH):
                sp.dma_start(w1_sb[:, k, :, :], W1[:, k * P:(k + 1) * P, :].rearrange("e p h -> p e h")).then_inc(w_in, 16)
            sp.wait_ge(attn_done, NT)
            sp.dma_start(w2_sb, W2.rearrange("e h d -> (e h) d").rearrange("(m p) d -> p m d", p=P)).then_inc(w_in, 16)

            sp.wait_ge(x1_ready, NT)
            for i in range(XLOADS):
                c = slice(i * NT // XLOADS, (i + 1) * NT // XLOADS)
                sp.dma_start(x_all[:, c, :], x_t[:, c, :]).then_inc(x_in[i], 16)

            def put_o(t, s, u):
                sp.wait_ge(o_set, t + 1)
                sp.dma_start(node_tile(out_t, t), o_sb[0:TILE, s, :]).then_inc(out_done[s], 16)

            each(sp, put_o)
            sp.wait_ge(out_done[0], 16 * (NT // 2 + 1))
            sp.wait_ge(out_done[1], 16 * (NT // 2))

        @block.gpsimd
        def _(pool):
            nc.gpsimd.memset(ident[:, :], 0.0).then_inc(pool_ord, 1)
            nc.gpsimd.memset(sel[:, :, :, :], 0.0).then_inc(pool_ord, 1)
            pool.wait_ge(pool_ord, 2)
            nc.gpsimd.affine_select(out=ident[:, :], in_=ident[:, :], compare_op=ALU.not_equal, fill=1.0, base=0,
                                    pattern=[[-1, P]], channel_multiplier=1).then_inc(consts_set, 1)
            nc.gpsimd.memset(ones[:, :], 1.0).then_inc(consts_set, 1)
            nc.gpsimd.iota(iota_c[:, :], [[1, PS], [PS, PP]], base=0, channel_multiplier=0,
                           allow_small_or_imprecise_dtypes=True).then_inc(consts_set, 1)
            nc.gpsimd.iota(iota_row[:, :], [[1, P]], base=0, channel_multiplier=0,
                           allow_small_or_imprecise_dtypes=True).then_inc(consts_set, 1)
            nc.gpsimd.iota(step_col[:, :], [[P, SBLK]], base=0, channel_multiplier=1,
                           allow_small_or_imprecise_dtypes=True).then_inc(consts_set, 1)
            nc.gpsimd.iota(win_col[:, :], [[TILE, NWB]], base=0, channel_multiplier=1,
                           allow_small_or_imprecise_dtypes=True).then_inc(consts_set, 1)
            nc.gpsimd.memset(kT[:, :, :, TILE:LO], 0.0).then_inc(consts_set, 1)
            pool.wait_ge(kv_params_in, 16 * len(first_params))
            pool.wait_ge(consts_set, NCONST)
            for k in range(KH):
                d = ws_sb[:, k, k * P:(k + 1) * P]
                nc.gpsimd.tensor_tensor(d, d, ident[:, :], ALU.add).then_inc(ws_set, 1)
            nc.gpsimd.affine_select(out=sel[:, :, :, :], in_=sel[:, :, :, :], compare_op=ALU.not_equal, fill=1.0, base=0,
                                    pattern=[[-2, NM], [-1, 2], [0, HID]], channel_multiplier=1).then_inc(ws_set, 1)

            pool.wait_ge(idx_set, 1)
            pool.wait_ge(tab_stored, 16)
            for b in range(SBLK):
                for u in range(SUB):
                    nc.gpsimd.indirect_dma_start(
                        gath[:, b, u, :], None, edge_tab.ap()[:, :],
                        bass.IndirectOffsetOnAxis(ap=cidx[:, u, b:b + 1], axis=0)).then_inc(gath_in[b], 16)
            pool.wait_ge(tabT_done, SBLK)
            pool.wait_ge(terms_stored, 16 * SUB * SBLK)
            nc.gpsimd.memset(dist_rows[0:2, :, :], 1.0).then_inc(ones_set, 1)

            pool.wait_ge(arow_set, 1)
            for q in range(STAGES):
                pool.wait_ge(stored[q], 16 * (NG // STAGES))

            def fetch(t, s, u):
                wait_from(pool, p_ready, t - 1)
                nc.gpsimd.tensor_copy(gidx[0:TILE, s:s + 1], arow[0:TILE, bass.ds(t, 1)]).then_inc(gidx_set, 1)
                pool.wait_ge(gidx_set, t + 1)
                pool.sem_inc(pool_mark, 1)
                nc.gpsimd.indirect_dma_start(
                    A_sb[0:TILE, s, :], None, adj.ap()[:, :],
                    bass.IndirectOffsetOnAxis(ap=gidx[0:TILE, s:s + 1], axis=0)).then_inc(a_in[s], 16)

            each(pool, fetch)

            def pick(t, s, u):
                pool.wait_ge(x1n_set, t + 1)
                wait_from(pool, x1T_ps, t - 1)
                pool.sem_inc(pool_mark, 1)
                nc.gpsimd.tensor_copy(x1c[0:TILE, s, :], node_tile(x1, t)).then_inc(x1c_set, 1)

            each(pool, pick)

        @block.scalar
        def _(act):
            for nm in ("we", "be"):
                act.dma_start(rows[nm][0][:, :], rows[nm][1].partition_broadcast(P)).then_inc(scal_in, 16)
            for dst_ap, src_ap in first_params:
                act.dma_start(dst_ap, src_ap, allow_slow_non_contiguous=True).then_inc(kv_params_in, 16)
            for dst_ap, src_ap in params:
                act.dma_start(dst_ap, src_ap, allow_slow_non_contiguous=True).then_inc(params_in, 16)
            act.wait_ge(kv_params_in, 16 * len(first_params))
            act.wait_ge(consts_set, NCONST)
            nc.scalar.mul(bqs_col[:, :], bq_col[:, :], SCALE).then_inc(q_ready, 1)

            act.wait_ge(stats_set, 1)

            def n_norm(t, s, u):
                wait_from(act, hT_ps, t - 1)
                nc.scalar.activation(h[:, s, :], node_tile(V, t), ACT.Identity, bias=nmr[:, bass.ds(t, 1)],
                                     scale=rstd[:, bass.ds(t, 1)]).then_inc(h_ready, 1)

            def n_front(t, s, u):
                act.wait_ge(hT_ps, t + 1)
                wait_from(act, vs_ps, t - 1)
                nc.scalar.copy(hT[:, s, :, :], bank[2 + s][:, 0:KH * TILE].rearrange("p (k t) -> p k t", k=KH)).then_inc(hT_ready, 1)

            def n_back(t, s, u):
                act.wait_ge(kq_ps, t + 1)
                for m in range(KH):
                    ins = nc.scalar.activation(kT[:, m, bass.ds(t, 1), 0:TILE].rearrange("p a l -> p (a l)"),
                                               bank[4 + s][:, m * TILE:(m + 1) * TILE], ACT.Identity, bias=bk_col[:, m:m + 1])
                ins.then_inc(k_ready, 1)
                if isinstance(t, int):
                    act.wait_ge(q_ready, 1)
                wait_from(act, q_stored[s], 16 * u)
                for m in range(KH):
                    ins = nc.scalar.activation(qs[:, s, m, :], bank[4 + s][:, (KH + m) * TILE:(KH + m + 1) * TILE], ACT.Identity,
                                               bias=bqs_col[:, m:m + 1], scale=SCALE)
                ins.then_inc(q_ready, 1)
                act.wait_ge(vs_ps, t + 1)
                nc.scalar.copy(node_tile(V, t), bank[6 + s][0:TILE, 0:D])
                nc.scalar.copy(node_tile(x1, t), bank[6 + s][0:TILE, D:2 * D]).then_inc(vs_ready, 1)
                act.wait_ge(q_ready, t + 2)
                act.dma_start(q_v[:, bass.ds(t, 1), :].rearrange("p t c -> p (t c)"),
                              qs[:, s, :, :].rearrange("p k t -> p (k t)")).then_inc(q_stored[s], 16)

            step = staged(n_norm, n_front, n_back)
            act.wait_ge(guard_set, 1)
            nc.scalar.activation(vals_o, t_e.rearrange("p (k e) -> p k e", k=PC), ACT.Exp).then_inc(val_set, 1)
            with act.Fori(1, NT // 2 - 1) as i:
                step(2 * i, 0, i, i)
                step(2 * i + 1, 1, i, i + 1)
            for t in range(NT - 3, NT):
                step(t, t % 2, t // 2, (t + 1) // 2)

            for b in range(SBLK):
                act.wait_ge(tabT_done, b + 1)
                ps = bank[6 + b % 2][:, :].rearrange("p (c u i) -> p c i u", c=2, u=SUB)

                def steps(tab):
                    return tab[:, b * SUB * P:(b + 1) * SUB * P].rearrange("p (i u) -> p i u", u=SUB)

                nc.scalar.copy(steps(code_tab), ps[:, 0, :, :])
                nc.scalar.mul(steps(nval_tab), ps[:, 1, :, :], -1.0).then_inc(tab_set, 1)

            act.wait_ge(terms_stored, 16 * SUB * SBLK)

            def columns(g, s):
                act.wait_ge(dist_done, g + 1)
                wait_from(act, prod_done, g - 1)
                for k in range(GC):
                    i = g * GC + k
                    ins = nc.scalar.activation(Ys[:, s, k, :], bank[2 + s][:, k * LO:(k + 1) * LO], ACT.Relu,
                                               scale=nval_tab[:, bass.ds(i, 1)])
                ins.then_inc(y_ready, 1)

            turns(act, lambda g, j, i: columns(g, j % 2))

            def front(t, s, u):
                act.wait_ge(nmax_set, t + 1)
                nc.scalar.activation(Z[0:TILE, s, :], Z[0:TILE, s, :], ACT.Exp, bias=nmax[:, s:s + 1]).then_inc(e_ready, 1)

            def back(t, s, u):
                wait_from(act, attn_done, t - 1)
                for g, (j, n) in enumerate(TRG):
                    act.wait_ge(tr_ready, len(TRG) * t + g + 1)
                    nc.scalar.copy(PT[0:TILE, s, j:j + n, :], bank[4 + g % 2][0:TILE, 0:n * TILE].rearrange(
                        "p (n d) -> p n d", n=n)).then_inc(pt_ready, 1)

            skewed(act, front, back, front_first=False)

            act.wait_ge(params_in, 16 * len(params))

            def f_copy(t, s, u):
                act.wait_ge(x1T_ps, t + 1)
                wait_from(act, f1_ps, t - 1)
                nc.scalar.copy(x1T[:, s, :, :], bank[s][:, 0:KH * TILE].rearrange("p (k t) -> p k t", k=KH)).then_inc(x1T_set, 1)

            def f_gelu(t, s, u):
                act.wait_ge(f1_ps, t + 1)
                wait_from(act, f2_ps, t - 1)
                for m in range(FF // P):
                    ins = nc.scalar.activation(gT[:, s, m, :], bank[2 + s][:, m * TILE:(m + 1) * TILE], ACT.Gelu_apprx_tanh,
                                               bias=bf1_col[:, m:m + 1])
                ins.then_inc(g_set, 1)

            pipeline(act, (f_gelu, 1), (f_copy, 0))

            def c_front(t, s, u):
                act.wait_ge(xfT_ps, t + 1)
                wait_from(act, moe_ps, t - 1)
                nc.scalar.copy(xfT[:, s, :, :], bank[3][:, 0:KH * TILE].rearrange("p (k t) -> p k t", k=KH)).then_inc(xfT_set, 1)

            def c_back(t, s, u):
                for q in range(NM // 4):
                    act.wait_ge(hm_ps, NM // 4 * t + q + 1)
                    for j in range(4):
                        m = 4 * q + j
                        ins = nc.scalar.activation(hmT[:, s, m, :], bank[6 + q % 2][:, j * TILE:(j + 1) * TILE], ACT.Relu,
                                                   bias=eb1_col[:, m:m + 1])
                    ins.then_inc(hm_set, 1)

            skewed(act, c_front, c_back)

        @block.vector
        def _(dve):
            V_ = nc.vector
            pad0 = E % EROW
            V_.memset(di[:, pad0:EROW], N).then_inc(pads_set, 1)
            V_.memset(si[:, pad0:EROW], 0).then_inc(pads_set, 1)
            V_.memset(w_e[:, pad0:EROW], 0.0).then_inc(pads_set, 1)
            od = Order(dve, dve_ord)

            def rounded(ap, in_ap, mul, add):
                od(V_.tensor_scalar(ap, in_ap, mul, add, ALU.mult, ALU.add))
                od(V_.tensor_scalar_add(ap, ap, MAGIC))
                od(V_.tensor_scalar_add(ap, ap, -MAGIC))

            dve.wait_ge(consts_set, NCONST)
            i1 = iota_row[0:1, :]
            od(V_.tensor_tensor(cmp_o[0:1, 0:P], i1, i1, ALU.mult))
            rounded(cmp_o[0:1, P:2 * P], cmp_o[0:1, 0:P], 1.0 / P, 0.0)
            od(V_.tensor_scalar_mul(dist_line[:, 0, :], cmp_o[0:1, P:2 * P], float(P)))
            od(V_.scalar_tensor_tensor(dist_line[:, 1, :], cmp_o[0:1, 0:P], -1.0, dist_line[:, 0, :], ALU.add, ALU.subtract))
            od(V_.tensor_copy(dist_line[:, 2, :], i1))
            V_.memset(dist_line[:, 3:DIST, :], 1.0).then_inc(dist_set, 1)
            dve.wait_ge(dst_in, 16 * 3)
            od(V_.tensor_copy(fcol[0:PP, :], di[:, 0:EROW:SPAN]))
            rounded(fcol[0:PP, :], fcol[0:PP, :], 1.0 / WIN, 0.5 / WIN - 0.5)
            for b in range(PS):
                ins = V_.tensor_scalar(diag_c[:, b, :], ident[0:PP, 0:PP], fcol[0:PP, b:b + 1], None, ALU.mult)
            ins.then_inc(diag_set, 1)
            dve.wait_ge(edges_in, 16 * 6)
            dve.wait_ge(scal_in, 32)
            od(V_.tensor_scalar(w_e, w_e, row["we"][0:PP, 0:1], row["be"][0:PP, 0:1], ALU.mult, ALU.add))
            od(V_.tensor_copy(dstf, di))
            od(V_.tensor_tensor(neg_e[:, 1:EROW], dstf[:, 1:EROW], dstf[:, 0:EROW - 1], ALU.is_equal))
            od(V_.tensor_scalar(neg_e[:, 1:EROW], neg_e[:, 1:EROW], -1.0, BIG, ALU.add, ALU.mult))
            od(V_.memset(neg_e[:, 0:1], -BIG))
            od(V_.memset(neg_e[:, EROW:EROW + 1], -BIG))
            od(V_.tensor_tensor_scan(F_e, neg_e[:, 0:EROW], w_e, -BIG, ALU.add, ALU.max))
            od(V_.tensor_tensor_scan(B_e[:, ::-1], neg_e[:, 1:EROW + 1][:, ::-1], F_e[:, ::-1], -BIG, ALU.add, ALU.max))
            dve.wait_ge(rows_bc, 1)
            od(V_.tensor_copy(s_row, bank[0][:, 0:NS]))
            od(V_.memset(s_row[:, 0:1], 0.0))
            od(V_.tensor_tensor(o_row, s_row, iota_c, ALU.add))
            firsts, lasts = dstf[:, 0:1], dstf[:, EROW - 1:EROW]
            for q, col in enumerate((firsts, lasts, B_e[:, 0:1], B_e[:, EROW - 1:EROW])):
                ins = V_.tensor_scalar(diag_c[:, q, :], ident[0:PP, 0:PP], col, None, ALU.mult)
            ins.then_inc(diag_set, 1)
            dve.wait_ge(rows_bc, 2)
            segcmp, segval = cmp_o[0:PP, 0:2 * PP], cmp_o[0:PP, 2 * PP:4 * PP]
            for q, col in enumerate((firsts, lasts)):
                od(V_.tensor_scalar(segcmp, bank[2][0:PP, 0:2 * PP], col, -1.0, ALU.is_equal, ALU.add))
                od(V_.scalar_tensor_tensor(segval, segcmp, BIG, bank[2][0:PP, 2 * PP:4 * PP], ALU.mult, ALU.add))
                od(V_.tensor_reduce(guards[0:PP, q:q + 1], segval, AX, ALU.max))

            def statistics(st):
                od(V_.tensor_tensor(mean[:, :], st[:, :, 1], st[:, :, 4], ALU.add))
                od(V_.tensor_scalar_mul(mean[:, :], mean[:, :], 0.5))
                od(V_.tensor_tensor(dif[:, :], st[:, :, 1], st[:, :, 4], ALU.subtract))
                od(V_.tensor_tensor(var[:, :], st[:, :, 2], st[:, :, 5], ALU.add))
                od(V_.scalar_tensor_tensor(dif[:, :], dif[:, :], 0.25, dif[:, :], ALU.mult, ALU.mult))
                od(V_.tensor_scalar(var[:, :], var[:, :], 1.0 / D, EPS, ALU.mult, ALU.add))
                od(V_.tensor_tensor(var[:, :], var[:, :], dif[:, :], ALU.add))
                od(V_.tensor_single_scalar(rstd[:, :].bitcast(I32), var[:, :].bitcast(I32), 1, ALU.logical_shift_right))
                od(V_.tensor_scalar(rstd[:, :].bitcast(I32), rstd[:, :].bitcast(I32), -1.0, RSQRT, ALU.mult, ALU.add))
                for _ in range(NEWTON):
                    od(V_.tensor_tensor(dif[:, :], rstd[:, :], rstd[:, :], ALU.mult))
                    od(V_.tensor_tensor(dif[:, :], dif[:, :], var[:, :], ALU.mult))
                    od(V_.tensor_scalar(dif[:, :], dif[:, :], -0.5, 1.5, ALU.mult, ALU.add))
                    od(V_.tensor_tensor(rstd[:, :], rstd[:, :], dif[:, :], ALU.mult))

            def st_tile(t):
                return st[:, bass.ds(t, 1), :].rearrange("p t c -> p (t c)")

            def st2_tile(t):
                return st2[:, bass.ds(t, 1), :].rearrange("p t c -> p (t c)")

            def normalised(out_ap, in_ap, t):
                return V_.tensor_scalar(out_ap, in_ap, mean[:, bass.ds(t, 1)], rstd[:, bass.ds(t, 1)],
                                        ALU.subtract, ALU.mult)

            dve.wait_ge(nodes_in, 16 * XLOADS)
            with dve.Fori(0, NT) as t:
                V_.bn_stats(st_tile(t), node_tile(V, t)).then_inc(dve_ord, 1)
            od.n += NT
            dve.wait_ge(dve_ord, od.n)
            statistics(st)
            V_.scalar_tensor_tensor(nmr[:, :], mean[:, :], -1.0, rstd[:, :], ALU.mult, ALU.mult).then_inc(stats_set, 1)

            for q, col in enumerate((firsts, lasts)):
                od(V_.tensor_scalar(t_e, dstf, col, -1.0, ALU.is_equal, ALU.add))
                od(V_.tensor_scalar(t_e, t_e, BIG, guards[0:PP, q:q + 1], ALU.mult, ALU.add))
                od(V_.tensor_tensor(B_e, B_e, t_e, ALU.max))
            V_.scalar_tensor_tensor(t_e, w_e, SHIFT, B_e, ALU.add, ALU.subtract).then_inc(guard_set, 1)
            dve.wait_ge(guard_set, 1)
            for b in range(SBLK):
                od(V_.tensor_scalar(cmp_s, o_row, step_col[:, b:b + 1], None, ALU.is_le))
                od(V_.tensor_reduce(cnt[:, b:b + 1], cmp_s, AX, ALU.add))
            od(V_.tensor_scalar_add(cnt[:, :], cnt[:, :], -1.0))
            for u in range(SUB):
                ins = V_.tensor_scalar(cidx[:, u, :], cnt[:, :], float(SUB), float(u), ALU.mult, ALU.add)
            ins.then_inc(idx_set, 1)
            od(V_.tensor_tensor(wneg[:, :], cnt[:, :], step_col[:, :], ALU.subtract))
            od(V_.tensor_scalar_mul(wneg[:, :], wneg[:, :], float(WIN * NT)))
            chunked = lambda ap: ap.rearrange("p (k e) -> p k e", k=PC)
            od(V_.tensor_copy(srcf, si))
            rounded(hi_e[:, 0:EROW], srcf, 1.0 / TILE, 0.5 / TILE - 0.5)
            od(V_.scalar_tensor_tensor(codes_o, chunked(dstf), float(NT), chunked(hi_e[:, 0:EROW]), ALU.mult, ALU.add))
            od(V_.scalar_tensor_tensor(srcf, hi_e[:, 0:EROW], -float(TILE), srcf, ALU.mult, ALU.add))
            od(V_.tensor_scalar_mul(terms_o[:, :, 0, :], chunked(srcf), -2.0))
            od(V_.tensor_tensor(sq_e, srcf, srcf, ALU.mult))
            rounded(sqh_e, sq_e, 1.0 / P, 0.0)
            od(V_.tensor_scalar_mul(terms_o[:, :, 1, :], chunked(sqh_e), float(P)))
            V_.scalar_tensor_tensor(terms_o[:, :, 2, :], chunked(sqh_e), -float(P), chunked(sq_e), ALU.mult,
                                    ALU.add).then_inc(code_set, 1)
            dve.wait_ge(code_set, 1)
            for b in range(SBLK):
                ins = V_.tensor_scalar(diag[:, b, :], ident[:, :], cnt[:, b:b + 1], None, ALU.mult)
            ins.then_inc(diag_set, 1)
            for b in range(NWB):
                od(V_.tensor_scalar(cmp_s[0:TILE, :], s_row[0:TILE, :], win_col[0:TILE, b:b + 1], None, ALU.is_le))
                od(V_.tensor_reduce(wcnt[0:TILE, b:b + 1], cmp_s[0:TILE, :], AX, ALU.add))
            od(V_.tensor_tensor(wcnt[0:TILE, :], wcnt[0:TILE, :], win_col[0:TILE, :], ALU.add))
            od(V_.tensor_scalar(wcnt[0:TILE, :], wcnt[0:TILE, :], -1.0, float(WIN), ALU.add, ALU.mult))
            V_.tensor_copy(wrow[0:TILE, :], wcnt[0:TILE, :]).then_inc(last_set, 1)
            for b in range(SBLK):
                dve.wait_ge(gath_in[b], 16 * SUB)
                codes = gath[:, b, :, 0:CHUNK]
                V_.tensor_scalar_add(codes, codes, wneg[:, b:b + 1]).then_inc(rel_set, 1)
            rounded(pmod[:, :], step_col[:, 0:1], 1.0 / WIN, 0.5 / WIN - 0.5)
            od(V_.scalar_tensor_tensor(pmod[:, :], pmod[:, :], -float(WIN), step_col[:, 0:1], ALU.mult, ALU.add))
            dve.wait_ge(last_in, 16 * WIN)
            od(V_.tensor_copy(arowf[0:TILE, :], arow0[0:TILE, :]))
            od(V_.tensor_scalar_add(arowf[0:TILE, :], arowf[0:TILE, :], pmod[0:TILE, 0:1]))
            V_.tensor_copy(arow[0:TILE, :], arowf[0:TILE, :]).then_inc(arow_set, 1)
            dve.wait_ge(rows_bc, 3)
            for c in range(0, SLOTS, 512):
                n = min(512, SLOTS - c)
                od(V_.tensor_copy(c_row[:, c:c + n], bank[3 + c // 512][:, 0:n]))
            od(V_.memset(keep_tab[:, 0:1], 0.0))
            V_.tensor_tensor(keep_tab[:, 1:SLOTS], c_row[:, 1:SLOTS], c_row[:, 0:SLOTS - 1],
                             ALU.subtract).then_inc(keep_set, 1)
            dve.wait_ge(keep_set, 1)
            dve.wait_ge(tab_set, SBLK)
            dve.wait_ge(terms_stored, 16 * SUB * SBLK)

            def one_hot(g, s, k):
                cols = slice(k * SUB, (k + 1) * SUB)
                ins = V_.tensor_tensor(Xs[:, s, cols, :], iota_row[:, :].unsqueeze(1).to_broadcast([P, SUB, P]),
                                       code_tab[:, bass.ds(g * GC + k * SUB, SUB)].unsqueeze(2).to_broadcast([P, SUB, P]),
                                       ALU.is_equal)
                if k == GROUP - 1:
                    ins.then_inc(x_ready, 1)

            for g in range(2):
                for k in range(GROUP):
                    one_hot(g, g, k)

            def sums(g, j, i):
                s, q = j % 2, j % STAGES
                dve.wait_ge(prod_done, g + 1)
                wait_from(dve, stored[q], 16 * ((BODY // STAGES) * i + j // STAGES))
                for k in range(GROUP):
                    first = isinstance(g, int) and g == 0 and k == 0
                    if k:
                        dve.wait_ge(sum_ord, g * (GROUP - 1) + k)
                    elif not first:
                        dve.wait_ge(sums_ready, g)
                    prev = stage[0:TILE, q, k - 1, :] if k else stage[0:TILE, (q - 1) % STAGES, GROUP - 1, :]
                    ps = bank[s][0:TILE, k * LO:(k + 1) * LO]
                    if first:
                        ins = V_.tensor_copy(stage[0:TILE, q, k, :], ps)
                    else:
                        ins = V_.scalar_tensor_tensor(stage[0:TILE, q, k, :], prev,
                                                      keep_tab[0:TILE, bass.ds(g * GROUP + k, 1)], ps, ALU.mult, ALU.add)
                    ins.then_inc(sum_ord if k < GROUP - 1 else sums_ready, 1)
                    if not (isinstance(i, int) and i == TURNS - 1 and j >= BODY - 2):
                        one_hot(g + 2, s, k)

            turns(dve, sums)

            f_ord = Order(dve, front_ord, 3)
            b_ord = Order(dve, back_ord, 4)
            dve.wait_ge(params_in, 16 * len(params))

            def front(t, s, u):
                f_ord.begin(t)
                dve.wait_ge(a_in[s], 16 * (u + 1))
                wait_from(dve, tr_ready, len(TRG) * (t - 1))
                f_ord(V_.tensor_scalar(Z[0:TILE, s, :], A_sb[0:TILE, s, :], 0.0, -BIG, ALU.is_equal, ALU.mult))
                for b, (c, n) in enumerate(SCH):
                    dve.wait_ge(s_ready, len(SCH) * t + b + 1)
                    dve.sem_inc(dve_mark, 1)
                    V_.tensor_tensor_reduce(out=Z[0:TILE, s, c:c + n], in0=bank[b % 4][0:TILE, 0:n], in1=Z[0:TILE, s, c:c + n],
                                            scale=1.0, scalar=-BIG, op0=ALU.add, op1=ALU.max,
                                            accum_out=mx[:, b:b + 1]).then_inc(s_used, 1)
                dve.wait_ge(s_used, len(SCH) * (t + 1))
                f_ord(V_.tensor_reduce(mxr[:, :], mx[:, 0:len(SCH)], AX, ALU.max))
                V_.tensor_scalar(nmax[:, s:s + 1], mxr[:, :], -1.0, SHIFT, ALU.mult, ALU.add).then_inc(nmax_set, 1)
                dve.wait_ge(e_ready, t + 1)
                f_ord(V_.tensor_tensor_reduce(out=Z[0:TILE, s, :], in0=Z[0:TILE, s, :], in1=A_sb[0:TILE, s, :], scale=1.0,
                                              scalar=0.0, op0=ALU.mult, op1=ALU.add, accum_out=den[:, s:s + 1]))
                dve.sem_inc(p_ready, 1)
                f_ord.end()

            def back(t, s, u):
                b_ord.begin(t)
                b_ord(V_.tensor_scalar_max(rden[:, s:s + 1], den[:, s:s + 1], 1e-37))
                b_ord(V_.reciprocal(rden[:, s:s + 1], rden[:, s:s + 1]))
                dve.wait_ge(attn_done, t + 1)
                V_.scalar_tensor_tensor(yt[:, :], bank[6 + s][0:TILE, 0:D], rden[:, s:s + 1], node_tile(x1, t),
                                        ALU.mult, ALU.add).then_inc(o_used, 1)
                dve.wait_ge(o_used, t + 1)
                b_ord(V_.tensor_tensor(node_tile(x1, t), yt[:, :], row["bs"][0:TILE, :], ALU.add), dve_mark)
                b_ord(V_.bn_stats(st_tile(t), node_tile(x1, t)))
                dve.sem_inc(x1_ready, 1)
                b_ord.end()

            skewed(dve, front, back)
            statistics(st)

            n1_o = Order(dve, n1_ord, 2)
            y2_o = Order(dve, y2_ord, 2)

            def x1_norm(t, s, u):
                n1_o.begin(t)
                n1_o(normalised(node_tile(x1, t), node_tile(x1, t), t))
                n1_o(V_.tensor_tensor(node_tile(x1, t), node_tile(x1, t), row["g1"][0:TILE, :], ALU.mult))
                V_.tensor_tensor(node_tile(x1, t), node_tile(x1, t), row["b1"][0:TILE, :], ALU.add).then_inc(x1n_set, 1)
                n1_o.end()

            def y2_sum(t, s, u):
                y2_o.begin(t)
                dve.wait_ge(f2_ps, t + 1)
                dve.wait_ge(x1c_set, t + 1)
                V_.tensor_tensor(yt[:, :], bank[4 + s][0:TILE, 0:D], node_tile(x1, t), ALU.add).then_inc(y2_used, 1)
                dve.wait_ge(y2_used, t + 1)
                y2_o(V_.tensor_tensor(node_tile(x1, t), yt[:, :], row["bf2"][0:TILE, :], ALU.add), dve_mark)
                y2_o(V_.bn_stats(st2_tile(t), node_tile(x1, t)))
                y2_o.end()

            pipeline(dve, (x1_norm, 0), (y2_sum, 4))
            statistics(st2)

            def all_tiles(row_):
                return row_[0:TILE, :].unsqueeze(1).to_broadcast([TILE, NT, D])

            for i in range(XLOADS):
                dve.wait_ge(x_in[i], 16)
            od(V_.tensor_tensor(x_all, x_all, all_tiles(row["b2"]), ALU.add))
            with dve.Fori(0, NT) as t:
                normalised(node_tile(x1, t), node_tile(x1, t), t).then_inc(dve_ord, 1)
            od.n += NT
            dve.wait_ge(dve_ord, od.n)
            od(V_.tensor_tensor(x1[:, :, :], x1[:, :, :], all_tiles(row["g2"]), ALU.mult))
            od(V_.tensor_tensor(x1[:, :, :], x1[:, :, :], x_all, ALU.add))
            with dve.Fori(0, NT) as t:
                V_.bn_stats(st_tile(t), node_tile(x1, t)).then_inc(dve_ord, 1)
            od.n += NT
            dve.wait_ge(dve_ord, od.n)
            statistics(st)

            c_ord = Order(dve, cf_ord, 2)

            def r_front(t, s, u):
                c_ord.begin(t)
                wait_from(dve, xfT_ps, t - 1)
                normalised(xf[0:TILE, s, :], node_tile(x1, t), t).then_inc(xf_set, 1)
                dve.wait_ge(lg_ps, t + 1)
                V_.tensor_tensor(lg[0:TILE, s, :], bank[4][0:TILE, 0:NEXP], row["rb"][0:TILE, :], ALU.add).then_inc(lg_used, 1)
                dve.wait_ge(lg_used, t + 1)
                dve.sem_inc(dve_mark, 1)
                c_ord(V_.max(mx8[:, :], lg[0:TILE, s, :]), dve_mark)
                c_ord(V_.max_index(ix8[:, :], mx8[:, :], lg[0:TILE, s, :]))
                V_.tensor_copy(ixf[:, :], ix8[:, 0:1]).then_inc(ix_set, 1)
                dve.wait_ge(ix_set, t + 1)
                V_.tensor_scalar(hot[0:TILE, s, :], iota_row[0:TILE, 0:NEXP], ixf[:, 0:1], None, ALU.is_equal).then_inc(hot_set, 1)
                dve.wait_ge(ohT_ps, t + 1)
                wait_from(dve, moe_ps, t - 1)
                V_.tensor_copy(ohT[0:NEXP, s, :], bank[4][0:NEXP, 128:128 + TILE])
                V_.tensor_scalar(negT[:, s, :], bank[4][0:NEXP, 128:128 + TILE], -1.0, BIG, ALU.add, ALU.mult).then_inc(oh_set, 1)
                c_ord.end()

            def r_back(t, s, u):
                dve.wait_ge(moe_ps, t + 1)
                wait_from(dve, out_done[s], 16 * u)
                V_.scalar_tensor_tensor(o_sb[0:TILE, s, :], bank[5][0:TILE, 0:D], 0.0, node_tile(x1, t),
                                        ALU.max, ALU.add).then_inc(o_set, 1)

            skewed(dve, r_front, r_back)

        @block.tensor
        def _(pe):
            mm = nc.tensor.matmul
            tr = nc.tensor.transpose
            pe.wait_ge(consts_set, NCONST)
            pe.wait_ge(diag_set, 1)
            mm(bank[0][:, 0:NS], ones[0:PP, :], s_diag, start=True, stop=True).then_inc(rows_bc, 1)
            pe.wait_ge(diag_set, 2)
            mm(bank[2][:, 0:4 * PP], ones[0:PP, :], s_diag[:, 0:4 * PP], start=True, stop=True).then_inc(rows_bc, 1)

            def transposed(src_ap, ps):
                for k in range(KH):
                    ins = tr(ps[:, k * TILE:(k + 1) * TILE], src_ap[:, k * P:(k + 1) * P], ident[0:TILE, 0:TILE])
                return ins

            pe.wait_ge(kv_params_in, 16 * len(first_params))
            pe.wait_ge(ws_set, KH)

            def n_front(t, s, u):
                pe.wait_ge(h_ready, t + 1)
                wait_from(pe, hT_ready, t - 1)
                transposed(h[:, s, :], bank[2 + s]).then_inc(hT_ps, 1)

            def n_back(t, s, u):
                pe.wait_ge(hT_ready, t + 1)
                wait_from(pe, q_ready, t)
                for w, w_sb in enumerate((wk_sb, wq_sb)):
                    for m in range(KH):
                        for k in range(KH):
                            ins = mm(bank[4 + s][:, (KH * w + m) * TILE:(KH * w + m + 1) * TILE], w_sb[:, k, m * P:(m + 1) * P],
                                     hT[:, s, k, :], start=(k == 0), stop=(k == KH - 1))
                ins.then_inc(kq_ps, 1)
                wait_from(pe, vs_ready, t - 1)
                mm(bank[6 + s][0:TILE, 0:D], ones[0:1, 0:TILE], row["bv"][0:1, :], start=True, stop=False)
                for k in range(KH):
                    mm(bank[6 + s][0:TILE, 0:D], hT[:, s, k, :], wv_sb[:, k, :], start=False, stop=(k == KH - 1))
                for k in range(KH):
                    ins = mm(bank[6 + s][0:TILE, D:2 * D], hT[:, s, k, :], ws_sb[:, k, :], start=(k == 0), stop=(k == KH - 1))
                ins.then_inc(vs_ps, 1)

            skewed(pe, n_front, n_back)

            pe.wait_ge(hT_ready, NT)
            pe.wait_ge(q_ready, NT + 1)
            pe.wait_ge(vs_ready, NT)
            pe.wait_ge(diag_set, 3)
            for q in range(0, SBLK, 4):
                n = min(4, SBLK - q)
                ins = mm(bank[3 + q // 4][:, 0:n * P], ones[:, :], diag[:, q:q + n, :], start=True, stop=True)
            ins.then_inc(rows_bc, 1)
            for b in range(SBLK):
                pe.wait_ge(rel_set, b + 1)
                if b >= 2:
                    pe.wait_ge(tab_set, b - 1)
                for c in range(2):
                    for u in range(SUB):
                        q = c * SUB + u
                        ins = tr(bank[6 + b % 2][:, q * P:(q + 1) * P], gath[:, b, u, c * P:(c + 1) * P], ident[:, :])
                ins.then_inc(tabT_done, 1)

            pe.wait_ge(dist_in, 32)
            pe.wait_ge(ones_set, 1)
            pe.wait_ge(keep_set, 1)
            pe.wait_ge(tab_set, SBLK)

            def distances(g, s, j, loads):
                if j % LOADG == 0:
                    pe.wait_ge(rows_in[j // LOADG], 16 * loads)
                wait_from(pe, y_ready, g - 1)
                for k in range(GC):
                    c = ((j % LOADG) * GC + k) * CHUNK
                    ins = mm(bank[2 + s][:, k * LO:(k + 1) * LO], dist_rows[:, j // LOADG, c:c + CHUNK], dist_rhs[:, :],
                             start=True, stop=True)
                ins.then_inc(dist_done, 1)

            distances(0, 0, 0, 1)
            distances(1, 1, 1, 1)

            def product(g, j, i):
                s = j % 2
                pe.wait_ge(x_ready, g + 1)
                pe.wait_ge(y_ready, g + 1)
                wait_from(pe, sums_ready, g - 1)
                for k in range(GC):
                    o = bank[s][0:TILE, k // SUB * LO:(k // SUB + 1) * LO]
                    ins = mm(o, Xs[:, s, k, 0:TILE], Ys[:, s, k, :], start=(k % SUB == 0), stop=(k % SUB == SUB - 1))
                ins.then_inc(prod_done, 1)
                if not (isinstance(i, int) and i == TURNS - 1 and j >= BODY - 2):
                    distances(g + 2, s, (j + 2) % BODY, i + 1 + (j + 2) // BODY)

            turns(pe, product)

            pe.wait_ge(sums_ready, NG)
            pe.wait_ge(k_ready, NT)

            def front(t, s, u):
                pe.wait_ge(q_in[s], 16 * (u + 1))
                for b, (c, n) in enumerate(SCH):
                    ahead = len(SCH) - 4
                    wait_from(pe, s_used, len(SCH) * t + (b - 3 if b >= 4 else min(b + 1 - ahead, 0)))
                    for k in range(KH):
                        ins = mm(bank[b % 4][0:TILE, 0:n], qT[:, s, k, :],
                                 kT[:, k, c // LO:(c + n) // LO, :].rearrange("p j l -> p (j l)"),
                                 start=(k == 0), stop=(k == KH - 1))
                    ins.then_inc(s_ready, 1)

            def back(t, s, u):
                wait_from(pe, o_used, t - 1)
                pe.wait_ge(p_ready, t + 1)

                def weigh(g):
                    j0, n = TRG[g]
                    pe.wait_ge(pt_ready, len(TRG) * t + g + 1)
                    for j in range(j0, j0 + n):
                        ins = mm(bank[6 + s][0:TILE, 0:D], PT[0:TILE, s, j, :], V[:, j, :], start=(j == 0), stop=(j == NT - 1))
                    return ins

                for g, (j0, n) in enumerate(TRG):
                    wait_from(pe, pt_ready, len(TRG) * t + (g - 1 if g >= 2 else 0))
                    for j in range(n):
                        ins = tr(bank[4 + g % 2][0:TILE, j * TILE:(j + 1) * TILE],
                                 Z[0:TILE, s, (j0 + j) * LO:(j0 + j) * LO + TILE], ident[0:TILE, 0:TILE])
                    ins.then_inc(tr_ready, 1)
                    if g:
                        weigh(g - 1)
                weigh(len(TRG) - 1).then_inc(attn_done, 1)

            skewed(pe, front, back)

            pe.wait_ge(s_used, len(SCH) * NT)
            pe.wait_ge(pt_ready, len(TRG) * NT)
            pe.wait_ge(o_used, NT)
            pe.wait_ge(params_in, 16 * len(params))

            def f_tr(t, s, u):
                pe.wait_ge(x1c_set, t + 1)
                wait_from(pe, x1T_set, t - 1)
                transposed(x1c[0:TILE, s, :], bank[s]).then_inc(x1T_ps, 1)

            def f_1(t, s, u):
                pe.wait_ge(x1T_set, t + 1)
                wait_from(pe, g_set, t - 1)
                for m in range(FF // P):
                    for k in range(KH):
                        ins = mm(bank[2 + s][:, m * TILE:(m + 1) * TILE], wf1_sb[:, k, m * P:(m + 1) * P], x1T[:, s, k, :],
                                 start=(k == 0), stop=(k == KH - 1))
                ins.then_inc(f1_ps, 1)

            def f_2(t, s, u):
                pe.wait_ge(g_set, t + 1)
                wait_from(pe, y2_used, t - 1)
                for m in range(FF // P):
                    ins = mm(bank[4 + s][0:TILE, 0:D], gT[:, s, m, :], wf2_sb[:, m, :], start=(m == 0), stop=(m == FF // P - 1))
                ins.then_inc(f2_ps, 1)

            pipeline(pe, (f_1, 1), (f_tr, 0), (f_2, 2))

            pe.wait_ge(w_in, 16 * (KH + 1))
            pe.wait_ge(ws_set, KH + 1)
            pe.wait_ge(y2_used, NT)

            def c_front(t, s, u):
                pe.wait_ge(xf_set, t + 1)
                wait_from(pe, xfT_set, t)
                transposed(xf[0:TILE, s, :], bank[3]).then_inc(xfT_ps, 1)
                pe.wait_ge(xfT_set, t + 1)
                wait_from(pe, oh_set, t)
                for k in range(KH):
                    ins = mm(bank[4][0:TILE, 0:NEXP], xfT[:, s, k, :], rw_sb[:, k, :], start=(k == 0), stop=(k == KH - 1))
                ins.then_inc(lg_ps, 1)
                pe.wait_ge(hot_set, t + 1)
                tr(bank[4][0:NEXP, 128:128 + TILE], hot[0:TILE, s, :], ident[0:TILE, 0:TILE]).then_inc(ohT_ps, 1)

            def c_back(t, s, u):
                pe.wait_ge(oh_set, t + 1)
                for q in range(NM // 4):
                    wait_from(pe, hm_set, NM // 4 * t + (q - 1 if q >= 2 else 0))
                    for j in range(4):
                        m = 4 * q + j
                        o = bank[6 + q % 2][:, j * TILE:(j + 1) * TILE]
                        for k in range(KH):
                            mm(o, w1_sb[:, k, 2 * m:2 * m + 2, :].rearrange("p e h -> p (e h)"), xfT[:, s, k, :],
                               start=(k == 0), stop=False)
                        ins = mm(o, sel[:, m, :, :].rearrange("e q h -> e (q h)"), negT[:, s, :], start=False, stop=True)
                    ins.then_inc(hm_ps, 1)
                wait_from(pe, o_set, t)
                o = bank[5][0:TILE, 0:D]
                mm(o, ohT[0:NEXP, s, :], eb2_sb[:, :], start=True, stop=False)
                for m in range(NM):
                    if m % 4 == 0:
                        pe.wait_ge(hm_set, NM // 4 * t + m // 4 + 1)
                    ins = mm(o, hmT[:, s, m, :], w2_sb[:, m, :], start=False, stop=(m == NM - 1))
                ins.then_inc(moe_ps, 1)

            skewed(pe, c_front, c_back)

    return nc


_INS = ['x', 'src', 'dst', 'edge_weight', 'L0_gnn_wq', 'L0_gnn_bq', 'L0_gnn_wk', 'L0_gnn_bk', 'L0_gnn_wv', 'L0_gnn_bv',
        'L0_gnn_ws', 'L0_gnn_bs', 'L0_gnn_we', 'L0_gnn_be', 'L0_gnn_g1', 'L0_gnn_b1', 'L0_gnn_g2', 'L0_gnn_b2',
        'L0_gnn_w_ff1', 'L0_gnn_b_ff1', 'L0_gnn_w_ff2', 'L0_gnn_b_ff2', 'L0_ffn_router_w', 'L0_ffn_router_b',
        'L0_ffn_W1', 'L0_ffn_b1', 'L0_ffn_W2', 'L0_ffn_b2']


def kernel(**inputs):
    import numpy as _np
    import concourse.bacc as _bacc
    from concourse import mybir as _mybir
    from concourse.bass_utils import run_bass_kernel_spmd as _run

    nc = _bacc.Bacc("TRN2", target_bir_lowering=False, num_devices=1)
    arrays, args = {}, []
    for name in _INS:
        a = _np.ascontiguousarray(inputs[name])
        arrays[f"in_{name}"] = a
        args.append(nc.dram_tensor(f"in_{name}", a.shape, _mybir.dt.from_np(a.dtype), kind="ExternalInput").ap())
    out = nc.dram_tensor("out_0", (3125, 256), _mybir.dt.float32, kind="ExternalOutput").ap()
    gnn_moe(nc, *args, out)
    r = _run(nc, [arrays], core_ids=[0])
    return r.results[0]["out_0"]
```

```python
import concourse.bass as bass
from concourse import mybir
from contextlib import ExitStack

F32 = mybir.dt.float32
F32R = mybir.dt.float32r
BF16 = mybir.dt.bfloat16
I32 = mybir.dt.int32
U32 = mybir.dt.uint32
ALU = mybir.AluOpType
ACT = mybir.ActivationFunctionType
AX = mybir.AxisListType.X

N, D, E = 3125, 256, 100000
FF = 2 * D
NEXP, HID = 32, 64
EPS = 1e-5
RSQRT = float(0x5F3759DF)
NEWTON = 3
P = 128
TILE = 125
NT = N // TILE
KH = D // P
CHUNK = 128
SUB = 2
PC = 8
PP = 98
EROW = PC * CHUNK
NC = PP * PC
SPAN = SUB * CHUNK
PS = PC // SUB
NS = PP * PS
WIN = 5
NW = N // WIN
STEPS = -(-E // SPAN) + NW - 1
GROUP = 2
GC = GROUP * SUB
LOADG = 8
BODY = 2 * LOADG
NG = -(-STEPS // (BODY * GROUP)) * BODY
TURNS = NG // BODY
SLOTS = NG * GROUP
SBLK = SLOTS // P
LO = 128
ROW = NT * LO
DIST = 5
TABW = 2 * CHUNK + 3 * CHUNK // 2
BIG = 1e30
MAGIC = 12582912.0
SHIFT = 30.0
SCALE = float(D) ** -0.5
MT = (N + NEXP * (P - 1)) // P
ZROWS = MT * P // (2 * TURNS)
XROW = HID + 1
W_ROW = KH * HID + D + 1
SCH = [(c, min(512, ROW - c)) for c in range(0, ROW, 512)]
TRG = [(g, min(4, NT - g)) for g in range(0, NT, 4)]


class Order:

    def __init__(self, eng, sem, per=None):
        self.eng, self.sem, self.per, self.base, self.n = eng, sem, per, 0, 0

    def begin(self, t):
        self.base, self.n = t * self.per, 0

    def end(self):
        assert self.n == self.per, (self.n, self.per)

    def __call__(self, ins, mark=None):
        ins.then_inc(self.sem, 1)
        self.n += 1
        self.eng.wait_ge(self.sem, self.base + self.n)
        if mark is not None:
            self.eng.sem_inc(mark, 1)


def gnn_moe(nc, x, src, dst, edge_weight, wq, bq, wk, bk, wv, bv, ws, bs, we, be, g1, b1, g2, b2,
            w_ff1, b_ff1, w_ff2, b_ff2, router_w, router_b, W1, eb1, W2, eb2, out):
    ctx = ExitStack()
    with ctx:
        def sb(name, shape, dt=F32):
            return ctx.enter_context(nc.sbuf_tensor(name, shape, dt))

        def sem(name):
            return ctx.enter_context(nc.semaphore(name))

        def sem2(name):
            return [sem(name + "0"), sem(name + "1")]

        edge_tab = nc.dram_tensor("edge_tab", [NC, TABW], F32)
        term_rows = nc.dram_tensor("term_rows", [3, SLOTS * SUB, CHUNK], BF16)
        dist_dram = nc.dram_tensor("dist_dram", [DIST, LO], BF16)
        last_lin = nc.dram_tensor("last_lin", [NW], U32)
        adj = nc.dram_tensor("adj", [SLOTS * WIN, ROW], F32)
        xs_dram = nc.dram_tensor("xs_dram", [MT * P, D], F32)
        ys_dram = nc.dram_tensor("ys_dram", [MT * P, D], F32)
        w_dram = nc.dram_tensor("w_dram", [NEXP * P, W_ROW], F32)
        q_dram = nc.dram_tensor("q_dram", [NT, P, KH * TILE], F32)

        ident = sb("ident", [P, P])
        ones = sb("ones", [P, P])
        iota_row = sb("iota_row", [P, P])
        step_col = sb("step_col", [P, SBLK])
        win_col = sb("win_col", [P, NW // TILE])
        pmod = sb("pmod", [P, 1])
        dist_line = sb("dist_line", [1, DIST, LO], BF16)
        dist_rhs = sb("dist_rhs", [DIST, LO], BF16)
        before = sb("before", [P, P])
        zeros = sb("zeros", [P, D + 1])
        wq_sb = sb("wq_sb", [P, KH, D])
        wk_sb = sb("wk_sb", [P, KH, D])
        wv_sb = sb("wv_sb", [P, KH, D])
        ws_sb = sb("ws_sb", [P, KH, D])
        wf1_sb = sb("wf1_sb", [P, KH, FF])
        wf2_sb = sb("wf2_sb", [P, FF // P, D])
        rw_sb = sb("rw_sb", [P, KH, NEXP])
        bq_col = sb("bq_col", [P, KH])
        bqs_col = sb("bqs_col", [P, KH])
        bk_col = sb("bk_col", [P, KH])
        bf1_col = sb("bf1_col", [P, FF // P])
        rows = {}
        for nm, src_ap, n in (("bv", bv, D), ("bs", bs, D), ("g1", g1, D), ("b1", b1, D), ("g2", g2, D),
                              ("b2", b2, D), ("bf2", b_ff2, D), ("rb", router_b, NEXP), ("be", be, 1),
                              ("we", we.rearrange("a b -> (a b)"), 1)):
            rows[nm] = (sb(nm + "_row", [P, n]), src_ap)
        row = {k: v[0] for k, v in rows.items()}

        with nc.sbuf_tensor("kT", [P, KH, NT, LO], F32) as kT, nc.sbuf_tensor("tables", [P, KH * ROW], F32) as tables:
            pass
        k_lo = sb("k_lo", [P, KH, NT, LO], F32R)
        k_hi = sb("k_hi", [P, KH, NT, LO], F32R)
        q_hi, q_lo = sb("q_hi", [P, 2, KH, TILE], F32R), sb("q_lo", [P, 2, KH, TILE], F32R)
        V_buf = sb("V", [P, NT * D])
        V = V_buf[0:TILE, :].rearrange("p (t d) -> p t d", d=D)
        x1 = sb("x1", [TILE, NT, D])
        ARENA = 19050
        arena = sb("arena", [P, ARENA])
        at = [0]

        def view(cols, rows_=P):
            at[0] += cols
            assert at[0] <= ARENA, at[0]
            return arena[0:rows_, at[0] - cols:at[0]]

        step_space = at[0]
        w_e, neg_e = view(EROW, PP), view(EROW + 1, PP)
        F_e, B_e, t_e, dstf = (view(EROW, PP) for _ in range(4))
        di, si = view(EROW, PP).bitcast(I32), view(EROW, PP).bitcast(I32)
        srcf, hi_e, sq_e, sqh_e = F_e, neg_e, w_e, B_e
        edges_only = at[0]
        tab_e = view(PC * TABW, PP).rearrange("p (k c) -> p k c", k=PC)
        codes_o, vals_o = tab_e[:, :, 0:CHUNK], tab_e[:, :, CHUNK:2 * CHUNK]
        terms_o = tab_e[:, :, 2 * CHUNK:TABW].bitcast(BF16).rearrange("p k (c e) -> p k c e", c=3)
        edges_end = at[0]
        gath = arena[:, 0:SBLK * SUB * TABW].rearrange("p (b u c) -> p b u c", b=SBLK, u=SUB)
        assert SBLK * SUB * TABW <= edges_only
        cmp_o = view(4 * P)
        s_row, o_row, iota_c = view(4 * P), view(4 * P), view(4 * P)
        cmp_s, s_row, o_row, iota_c = (v[:, 0:NS] for v in (cmp_o, s_row, o_row, iota_c))
        diag_flat = view(SBLK * P)
        diag = diag_flat.rearrange("p (b e) -> p b e", b=SBLK)
        s_diag = diag_flat[0:PP, 0:NS]
        e_diag = diag_flat[0:PP, NS:NS + 4 * PP]
        diag_c, diag_e = s_diag.rearrange("p (b e) -> p b e", b=PS), e_diag.rearrange("p (b e) -> p b e", b=4)
        c_row = view(SLOTS)
        code_tab, nval_tab = (tables[:, i * SLOTS * SUB:(i + 1) * SLOTS * SUB] for i in range(2))
        keep_tab = tables[:, 2 * SLOTS * SUB:2 * SLOTS * SUB + SLOTS]
        h = view(2 * D, TILE).rearrange("p (s d) -> p s d", s=2)
        hT, qs = (view(2 * KH * TILE).rearrange("p (s k t) -> p s k t", s=2, k=KH) for _ in range(2))
        at[0] = step_space
        STAGES = 4
        Xs = view(STAGES * GC * TILE).rearrange("p (s k m) -> p s k m", s=STAGES, k=GC)
        Ys = view(STAGES * GC * LO).rearrange("p (s k l) -> p s k l", s=STAGES, k=GC)
        stage = view(STAGES * GROUP * LO).rearrange("p (s k l) -> p s k l", s=STAGES, k=GROUP)
        assert at[0] <= SBLK * SUB * TABW
        at[0] = SBLK * SUB * TABW
        LOADW = LOADG * GC * CHUNK
        dist_rows = view(LOADW)[0:DIST, :].bitcast(BF16).rearrange("p (s c) -> p s c", s=2)
        assert at[0] <= edges_end
        step_end = at[0]
        at[0] = 0
        PT = view(2 * NT * TILE).rearrange("p (s j d) -> p s j d", s=2, j=NT)
        Z = view(2 * ROW).rearrange("p (s c) -> p s c", s=2)
        A_sb = view(2 * ROW).rearrange("p (s c) -> p s c", s=2)
        assert at[0] - 2 * ROW >= step_end
        at[0] = 0

        def two(*shape):
            n = 2
            for d in shape:
                n *= d
            v = view(n)
            if len(shape) == 1:
                return v.rearrange("p (s c) -> p s c", s=2)
            return v.rearrange("p (s a c) -> p s a c", s=2, a=shape[0])

        gT, x1T, xfT = two(FF // P, TILE), two(KH, TILE), two(KH, TILE)
        x1c, xf = two(D), two(D)
        x_all = view(NT * D, TILE).rearrange("p (t d) -> p t d", d=D)
        xf_all = x_all
        owner = view(MT * NEXP).rearrange("p (j e) -> p j e", e=NEXP)
        RT = NT * NEXP
        k_flat = kT[:, :, :, :].rearrange("p k j l -> p (k j l)")
        lg, work, hot, total, upto, fresh = (k_flat[:, i * RT:(i + 1) * RT] for i in range(6))
        by_tile = lambda ap: ap.rearrange("p (t e) -> p t e", e=NEXP)
        by_exp = lambda ap: ap.rearrange("p (e t) -> p e t", t=NT)
        ES = 8

        xs, ws_e = (V_buf[:, a:a + ES * n].rearrange("p (s c) -> p s c", s=ES) for a, n in ((0, D), (ES * D, W_ROW + 1)))
        xsT, hid, ys = (view(ES * n).rearrange("p (s c) -> p s c", s=ES) for n in (KH * P, P, D))
        best, exp_of, pos = (view(NT, TILE) for _ in range(3))
        pos_i, own_row, oidx = view(NT, TILE).bitcast(U32), view(MT).bitcast(U32), view(ES).bitcast(U32)
        ntile, tincl, tbase, own = view(NEXP), view(NEXP), view(NEXP), view(MT)
        w1s, w2s = ws_e[:, :, 0:KH * HID], ws_e[:, :, KH * HID:W_ROW]

        fcol = sb("fcol", [P, PS])
        guards = sb("guards", [P, 2])
        cnt = sb("cnt", [P, SBLK])
        cidx = sb("cidx", [P, SUB, SBLK], U32)
        wneg = sb("wneg", [P, SBLK])
        wcnt = sb("wcnt", [P, NW // TILE])
        wrow = sb("wrow", [P, NW // TILE], U32)
        arow0 = sb("arow0", [P, NT], U32)
        arowf = sb("arowf", [P, NT])
        arow = sb("arow", [P, NT], U32)
        gidx = sb("gidx", [P, 2], U32)

        qT = wq_sb[:, :, :].rearrange("p k n -> p (k n)")[:, 0:2 * KH * TILE].rearrange("p (s k t) -> p s k t", s=2, k=KH)
        st0 = tables[0:TILE, KH * ROW - 6 * NT:KH * ROW].rearrange("p (t c) -> p t c", c=6)
        assert 2 * SLOTS * SUB + SLOTS + 7 * NT <= KH * ROW
        st1 = wv_sb[0:TILE, 0, 0:6 * NT].rearrange("p (t c) -> p t c", c=6)
        small_at = [0]

        def small(cols):
            small_at[0] += cols
            return wk_sb[0:TILE, 0, small_at[0] - cols:small_at[0]]

        st2, st3 = (small(2 * 6).rearrange("p (s c) -> p s c", s=2) for _ in range(2))
        mv2, mv3 = (small(2 * 2).rearrange("p (s c) -> p s c", s=2) for _ in range(2))
        minus_half = sb("minus_half", [TILE, 1])
        rs2, rs3 = small(2), small(2)
        mean, rstd = sb("mean", [TILE, NT]), sb("rstd", [TILE, NT])
        var, dif = sb("var", [TILE, NT]), sb("dif", [TILE, NT])
        nmr = tables[0:TILE, KH * ROW - 7 * NT:KH * ROW - 6 * NT]
        mx, mxr, nmax, den, rden = (small(n) for n in (8, 1, 2, 2, 2))
        has = small(2)
        yt = ws_sb[0:TILE, 0, :]

        bank = [ctx.enter_context(nc.psum_tensor(f"bank{i}", [P, 512], F32)) for i in range(8)]

        XLOADS = 5
        (pads_set, dst_in, edges_in, scal_in, kv_params_in, params_in, pool_ord, consts_set, dist_in, ws_set,
         ones_set) = (sem(n) for n in (
            "pads_set", "dst_in", "edges_in", "scal_in", "kv_params_in", "params_in", "pool_ord", "consts_set",
            "dist_in", "ws_set", "ones_set"))
        dve_mark, pool_mark = sem("dve_mark"), sem("pool_mark")
        dve_ord, diag_set, rows_bc, dist_set = sem("dve_ord"), sem("diag_set"), sem("rows_bc"), sem("dist_set")
        guard_set, val_set, tab_stored = sem("guard_set"), sem("val_set"), sem("tab_stored")
        terms_stored = sem("terms_stored")
        code_set, idx_set, rel_set, tabT_done, tab_set, keep_set = (sem(n) for n in (
            "code_set", "idx_set", "rel_set", "tabT_done", "tab_set", "keep_set"))
        gath_in = [sem(f"gath_in{b}") for b in range(SBLK)]
        last_set, last_stored, last_in, arow_set = (sem(n) for n in ("last_set", "last_stored", "last_in", "arow_set"))
        stats_set = sem("stats_set")
        nodes_in = [sem(f"nodes_in{i}") for i in range(XLOADS)]
        excluded, xb_set = sem("excluded"), sem("xb_set")
        h_ready, hT_ps, hT_ready, kq_ps, vs_ps, k_ready, q_ready, vs_ready = (sem(n) for n in (
            "h_ready", "hT_ps", "hT_ready", "kq_ps", "vs_ps", "k_ready", "q_ready", "vs_ready"))
        q_stored = sem2("q_stored")
        rows_in = sem2("rows_in")
        dist_done, x_ready, y_ready, prod_done, sum_ord, sums_ready = (sem(n) for n in (
            "dist_done", "x_ready", "y_ready", "prod_done", "sum_ord", "sums_ready"))
        stored = [sem(f"stored{q}") for q in range(STAGES)]
        q_in, a_in = sem2("q_in"), sem2("a_in")
        k_hi_set, k_split, q_hi_set, q_split = (sem(n) for n in ("k_hi_set", "k_split", "q_hi_set", "q_split"))
        (gidx_set, s_ready, s_used, nmax_set, e_ready, p_ready, front_ord, tr_ready, pt_ready, attn_done, o_used, back_ord,
         x1_ready) = (sem(n) for n in (
            "gidx_set", "s_ready", "s_used", "nmax_set", "e_ready", "p_ready", "front_ord", "tr_ready", "pt_ready",
            "attn_done", "o_used", "back_ord", "x1_ready"))
        (x1s_set, x1n_set, x1b_set, x2s_set, x2_set) = (sem(n) for n in ("x1s_set", "x1n_set", "x1b_set", "x2s_set", "x2_set"))
        st2_set, mv2_set, rs2_set, st3_set, mv3_set, rs3_set = (sem(n) for n in (
            "st2_set", "mv2_set", "rs2_set", "st3_set", "mv3_set", "rs3_set"))
        (x1c_set, x1T_ps, x1T_set, f1_ps, g_set, f2_ps, y2_used, xf_set, xfc_set, xfT_ps, xfT_set, lg_ps,
         lg_set) = (sem(n) for n in (
            "x1c_set", "x1T_ps", "x1T_set", "f1_ps", "g_set", "f2_ps", "y2_used", "xf_set", "xfc_set", "xfT_ps", "xfT_set",
            "lg_ps", "lg_set"))
        (zeros_set, xs_zeroed, w_made, hot_set, ranks_ps, own_set, pos_set, xs_stored, ones_row, oidx_set, xsT_ps, xsT_set,
         hid_ps, hid_set, o_ps, ys_set, o_set, out_done) = (sem(n) for n in (
            "zeros_set", "xs_zeroed", "w_made", "hot_set", "ranks_ps", "own_set", "pos_set", "xs_stored", "ones_row", "oidx_set",
            "xsT_ps", "xsT_set", "hid_ps", "hid_set", "o_ps", "ys_set", "o_set", "out_done"))
        xs_in, w_in, ys_stored = ([sem(f"{n}{q}") for q in range(ES)] for n in ("xs_in", "w_in", "ys_stored"))

        NWB = NW // TILE
        NCONST = 8
        x_t = x.rearrange("(t p) d -> p t d", p=TILE)
        xs_v, ys_v = (v.ap().rearrange("(j p) d -> p j d", p=P) for v in (xs_dram, ys_dram))
        out_t = out.rearrange("(t p) d -> p t d", p=TILE)
        adj_v = adj.ap().rearrange("(s d) (h l) -> (d h) s l", d=WIN, l=LO)
        q_v = q_dram.ap().rearrange("t p c -> p t c")
        edge_tab_v = edge_tab.ap().rearrange("(p k) c -> p k c", k=PC)

        def node_tile(v, t):
            return v[:, bass.ds(t, 1), :].rearrange("p t d -> p (t d)")

        R_LAG = 7
        KV_FIRST = 5

        def skewed(eng, front, back, pause=None):
            def pair(i):
                front(2 * i + 1, 1, i)
                back(2 * i, 0, i)
                front(2 * i + 2, 0, i + 1)
                back(2 * i + 1, 1, i)

            front(0, 0, 0)
            pair(0)
            begin = 1
            if pause:
                pair(begin)
                pause()
                begin += 1
            with eng.Fori(begin, NT // 2) as i:
                pair(i)
            back(NT - 1, 0, NT // 2)

        def pipeline(eng, *stages, n=NT, per=2):
            most = max(lag for _, lag in stages)
            begin = -(-(most + per + 1) // per)
            end = n // per

            def at_time(i, r):
                for step, lag in stages:
                    c = r - lag
                    if not (isinstance(i, int) and not 0 <= per * i + c < n):
                        step(per * i + c, c % per, i + c // per)

            for t in range(per * begin):
                at_time(t // per, t % per)
            with eng.Fori(begin, end) as i:
                for r in range(per):
                    at_time(i, r)
            for t in range(per * end, n + most):
                at_time(t // per, t % per)

        def staged(norm_, front, back):
            def step(t, s, u, v):
                if not (isinstance(t, int) and t + 1 >= NT):
                    front(t + 1, 1 - s, v)
                if not (isinstance(t, int) and t + 2 >= NT):
                    norm_(t + 2, s, u + 1)
                back(t, s, u)

            norm_(0, 0, 0)
            norm_(1, 1, 0)
            front(0, 0, 0)
            step(0, 0, 0, 0)
            step(1, 1, 0, 1)
            return step

        def each(eng, step):
            for t in range(3):
                step(t, t % 2, t // 2)
            with eng.Fori(1, NT // 2) as i:
                step(2 * i + 1, 1, i)
                step(2 * i + 2, 0, i + 1)

        def turns(eng, step):
            def turn(i):
                for j in range(BODY):
                    step(i * BODY + j, j, i)

            turn(0)
            with eng.Fori(1, TURNS - 1) as i:
                turn(i)
            turn(TURNS - 1)

        def wait_from(eng, s, value):
            if not (isinstance(value, int) and value <= 0):
                eng.wait_ge(s, value)

        def product_bank(j):
            return bank[j % 2 + 4 * (j % STAGES // 2)]

        def j_bank(first, s):
            return first + s % 2

        first_params, params = [], []
        for w_sb, w in ((wk_sb, wk), (wv_sb, wv), (wq_sb, wq), (ws_sb, ws)):
            first_params.append((w_sb[:, :, :], w.rearrange("(k p) n -> p k n", p=P)))
        for c_sb, v in ((bk_col, bk), (bq_col, bq)):
            first_params.append((c_sb[:, :], v.rearrange("(k p) -> p k", p=P)))
        for w_sb, w in ((wf1_sb, w_ff1), (wf2_sb, w_ff2)):
            params.append((w_sb[:, :, :], w.rearrange("(k p) n -> p k n", p=P)))
        params.append((bf1_col[:, :], b_ff1.rearrange("(k p) -> p k", p=P)))
        for nm in ("bv", "bs", "g1", "b1", "g2", "b2", "bf2", "rb"):
            params.append((rows[nm][0][:, :], rows[nm][1].partition_broadcast(P)))
        for k in range(KH):
            params.append((rw_sb[:, k, :], router_w[:, k * P:(k + 1) * P].rearrange("e p -> p e")))
        w_v = w_dram.ap().rearrange("(e r) c -> e r c", r=P)
        W2_AT = KH * HID
        w_parts = ((w_v[:, :, 0:W2_AT], W1.rearrange("e (p k) h -> e p (k h)", k=KH)),
                   (w_v[:, 0:HID, W2_AT:W2_AT + D], W2), (w_v[:, HID, W2_AT:W2_AT + D], eb2),
                   (w_v[:, 0:HID, W2_AT + D], eb1), (w_v[:, HID, W2_AT + D:W_ROW], eb2[:, 0:1]),
                   (w_v[:, XROW:P, W2_AT:W_ROW].rearrange("e r c -> r e c"),
                    zeros[0:P - XROW, :].unsqueeze(1).to_broadcast([P - XROW, NEXP, D + 1])))

        block = ctx.enter_context(nc.Block())

        @block.sync
        def _(sp):
            for i in range(XLOADS):
                c = slice(i * NT // XLOADS, (i + 1) * NT // XLOADS)
                sp.dma_start(V[:, c, :], x_t[:, c, :]).then_inc(nodes_in[i], 16)
            sp.wait_ge(pads_set, 3)
            whole = E // EROW
            cut = whole // 16 * 16
            for ap, dram, s in ((di, dst, dst_in), (w_e, edge_weight, edges_in), (si, src, edges_in)):
                v = dram[0:whole * EROW].rearrange("(p j) -> p j", j=EROW)
                sp.dma_start(ap[0:cut, 0:EROW], v[0:cut, :]).then_inc(s, 16)
                sp.dma_start(ap[cut:whole, 0:EROW], v[cut:whole, :]).then_inc(s, 16)
                sp.dma_start(ap[whole:whole + 1, 0:E - whole * EROW], dram[whole * EROW:E].unsqueeze(0)).then_inc(s, 16)
            sp.wait_ge(dist_set, 1)
            sp.dma_start(dist_dram.ap().rearrange("c l -> (c l)").unsqueeze(0),
                         dist_line[:, :, :].rearrange("o c l -> o (c l)")).then_inc(dist_in, 16)
            sp.wait_ge(dist_in, 16)
            sp.dma_start(dist_rhs[:, :], dist_dram.ap()).then_inc(dist_in, 16)
            sp.wait_ge(last_set, 1)
            sp.dma_start(last_lin.ap().rearrange("(b p) -> p b", p=TILE), wrow[0:TILE, :],
                         allow_slow_non_contiguous=True).then_inc(last_stored, 16)
            sp.wait_ge(last_stored, 16)
            spread = last_lin.ap().rearrange("(t a) -> a t", a=TILE // WIN)
            for b in range(WIN):
                sp.dma_start(arow0[b:TILE:WIN, :], spread, allow_slow_non_contiguous=True).then_inc(last_in, 16)
            sp.wait_ge(code_set, 1)
            sp.wait_ge(val_set, 1)
            sp.dma_start(edge_tab_v, tab_e[:, :, :]).then_inc(tab_stored, 16)
            for b in range(SBLK):
                sp.wait_ge(gath_in[b], 16 * SUB)
                for u in range(SUB):
                    sp.dma_start(term_rows.ap().rearrange("c (i u) e -> i c u e", u=SUB)[b * P:(b + 1) * P, :, u, :],
                                 gath[:, b, u, 2 * CHUNK:TABW].bitcast(BF16).rearrange("p (c e) -> p c e", c=3)
                                 ).then_inc(terms_stored, 16)

            def load_rows(n, s):
                sp.dma_start(dist_rows[2:DIST, s, :], term_rows.ap().rearrange("c i e -> c (i e)")[
                    :, bass.ds(n * LOADW, LOADW)]).then_inc(rows_in[s], 16)

            sp.wait_ge(terms_stored, 16 * SUB * SBLK)
            load_rows(0, 0)
            load_rows(1, 1)

            def load_q(t, s, u):
                wait_from(sp, q_split, t - 1)
                sp.dma_start(qT[:, s, :, :].rearrange("p k t -> p (k t)"),
                             q_v[:, bass.ds(t, 1), :].rearrange("p t c -> p (t c)")).then_inc(q_in[s], 16)

            sp.wait_ge(q_stored[0], 16 * (NT // 2 + 1))
            sp.wait_ge(q_stored[1], 16 * (NT // 2))
            for t in range(2):
                load_q(t, t, 0)

            sp.wait_ge(zeros_set, 1)

            def put(g, j, i):
                if j % LOADG == 0:
                    sp.dma_start(xs_dram.ap()[bass.ds((2 * i + j // LOADG) * ZROWS, ZROWS), :],
                                 zeros[0:ZROWS, 0:D]).then_inc(xs_zeroed, 16)
                if j % LOADG == LOADG - 2 and not (isinstance(i, int) and i == TURNS - 1):
                    sp.wait_ge(dist_done, g + 2)
                    load_rows(2 * i + j // LOADG + 2, j // LOADG)
                sp.wait_ge(sums_ready, g + 1)
                sp.dma_start(adj_v[:, bass.ds(g * GROUP, GROUP), :],
                             stage[0:TILE, j % STAGES, :, :]).then_inc(stored[j % STAGES], 16)

            turns(sp, put)

            for t in range(2, 4):
                load_q(t, t % 2, t // 2)
                for dst_ap, src_ap in w_parts[3 * (t - 2):3 * (t - 1)]:
                    sp.dma_start(dst_ap, src_ap, allow_slow_non_contiguous=True).then_inc(w_made, 16)
            with sp.Fori(2, NT // 2) as i:
                load_q(2 * i, 0, i)
                load_q(2 * i + 1, 1, i)
            load_q(NT - 1, 0, NT // 2)

            sp.wait_ge(x1_ready, NT)
            for i in range(XLOADS):
                c = slice(i * NT // XLOADS, (i + 1) * NT // XLOADS)
                sp.dma_start(x_all[:, c, :], x_t[:, c, :]).then_inc(nodes_in[i], 16)

            sp.wait_ge(xs_stored, 16 * NT)

            def load_xs(j, s, u):
                wait_from(sp, xsT_ps, j - ES + 1)
                sp.dma_start(xs[:, s, :], node_tile(xs_v, j)).then_inc(xs_in[s], 16)

            def put_ys(j, s, u):
                sp.wait_ge(ys_set, j + 1)
                sp.dma_start(node_tile(ys_v, j), ys[:, s, :]).then_inc(ys_stored[s], 16)

            pipeline(sp, (load_xs, 0), (put_ys, 6), n=MT, per=ES)
            for i in range(XLOADS):
                c = slice(i * NT // XLOADS, (i + 1) * NT // XLOADS)
                sp.wait_ge(o_set, i + 1)
                sp.dma_start(out_t[:, c, :], x1[:, c, :]).then_inc(out_done, 16)
            sp.wait_ge(out_done, 16 * XLOADS)

        @block.gpsimd
        def _(pool):
            nc.gpsimd.memset(ident[:, :], 0.0).then_inc(pool_ord, 1)
            nc.gpsimd.memset(before[:, :], 1.0).then_inc(pool_ord, 1)
            nc.gpsimd.memset(zeros[:, :], 0.0).then_inc(zeros_set, 1)
            pool.wait_ge(pool_ord, 2)
            nc.gpsimd.affine_select(out=ident[:, :], in_=ident[:, :], compare_op=ALU.not_equal, fill=1.0, base=0,
                                    pattern=[[-1, P]], channel_multiplier=1).then_inc(consts_set, 1)
            nc.gpsimd.memset(ones[:, :], 1.0).then_inc(consts_set, 1)
            nc.gpsimd.iota(iota_c[:, :], [[1, PS], [PS, PP]], base=0, channel_multiplier=0,
                           allow_small_or_imprecise_dtypes=True).then_inc(consts_set, 1)
            nc.gpsimd.iota(iota_row[:, :], [[1, P]], base=0, channel_multiplier=0,
                           allow_small_or_imprecise_dtypes=True).then_inc(consts_set, 1)
            nc.gpsimd.iota(step_col[:, :], [[P, SBLK]], base=0, channel_multiplier=1,
                           allow_small_or_imprecise_dtypes=True).then_inc(consts_set, 1)
            nc.gpsimd.iota(win_col[:, :], [[TILE, NWB]], base=0, channel_multiplier=1,
                           allow_small_or_imprecise_dtypes=True).then_inc(consts_set, 1)
            nc.gpsimd.memset(kT[:, :, :, TILE:LO], 0.0).then_inc(consts_set, 1)
            nc.gpsimd.memset(minus_half[:, :], -0.5).then_inc(consts_set, 1)
            pool.wait_ge(kv_params_in, 16 * len(first_params))
            pool.wait_ge(consts_set, NCONST)
            for k in range(KH):
                d = ws_sb[:, k, k * P:(k + 1) * P]
                nc.gpsimd.tensor_tensor(d, d, ident[:, :], ALU.add).then_inc(ws_set, 1)
            nc.gpsimd.affine_select(out=before[:, :], in_=before[:, :], compare_op=ALU.is_gt, fill=0.0, base=0,
                                    pattern=[[1, P]], channel_multiplier=-1).then_inc(ws_set, 1)

            pool.wait_ge(idx_set, 1)
            pool.wait_ge(tab_stored, 16)
            for b in range(SBLK):
                for u in range(SUB):
                    nc.gpsimd.indirect_dma_start(
                        gath[:, b, u, :], None, edge_tab.ap()[:, :],
                        bass.IndirectOffsetOnAxis(ap=cidx[:, u, b:b + 1], axis=0)).then_inc(gath_in[b], 16)
            nc.gpsimd.memset(dist_rows[0:2, :, :], 1.0).then_inc(ones_set, 1)

            pool.wait_ge(arow_set, 1)
            pool.wait_ge(keep_set, 1)
            pool.wait_ge(q_stored[0], 16 * (NT // 2 + 1))
            pool.wait_ge(q_stored[1], 16 * (NT // 2))
            last_group = (2 * TILE // WIN + NS - 2) // GROUP
            early_rows = (last_group + 1) * GROUP * WIN
            for q in range(STAGES):
                pool.wait_ge(stored[q], 16 * (last_group // STAGES + 1))

            def fetch(t, s, u):
                if isinstance(t, int) and t == 2:
                    for q in range(STAGES):
                        pool.wait_ge(stored[q], 16 * (NG // STAGES))
                wait_from(pool, p_ready, t - 1)
                nc.gpsimd.tensor_copy(gidx[0:TILE, s:s + 1], arow[0:TILE, bass.ds(t, 1)]).then_inc(gidx_set, 1)
                pool.wait_ge(gidx_set, t + 1)
                pool.sem_inc(pool_mark, 1)
                nc.gpsimd.indirect_dma_start(
                    A_sb[0:TILE, s, :], None, adj.ap()[0:early_rows if isinstance(t, int) and t < 2 else SLOTS * WIN, :],
                    bass.IndirectOffsetOnAxis(ap=gidx[0:TILE, s:s + 1], axis=0)).then_inc(a_in[s], 16)

            each(pool, fetch)

            def ffn_offset(t, s, u):
                pool.wait_ge(x1c_set, t + 1)
                pool.sem_inc(pool_mark, 1)
                nc.gpsimd.tensor_tensor(node_tile(x1, t), node_tile(x1, t), row["bf2"][0:TILE, :], ALU.add).then_inc(x1b_set, 1)

            def norm_offset(t, s, u):
                if isinstance(t, int) and t == 0:
                    for i in range(XLOADS):
                        pool.wait_ge(nodes_in[i], 32)
                nc.gpsimd.tensor_tensor(node_tile(x_all, t), node_tile(x_all, t), row["b2"][0:TILE, :], ALU.add).then_inc(xb_set, 1)

            def inverse_spread(rs, mv, s, done, t):
                nc.gpsimd.tensor_scalar_add(rs[:, s:s + 1], mv[:, s, 1:2], EPS).then_inc(done, 1)
                pool.wait_ge(done, 2 * t + 1)
                pool.sem_inc(pool_mark, 1)
                nc.gpsimd.tensor_tensor(rs[:, s:s + 1], rs[:, s:s + 1], minus_half[:, :], ALU.pow).then_inc(done, 1)

            def spread_2(t, s, u):
                pool.wait_ge(mv2_set, t + 1)
                pool.sem_inc(pool_mark, 1)
                inverse_spread(rs2, mv2, s, rs2_set, t)

            def spread_3(t, s, u):
                pool.wait_ge(mv3_set, t + 1)
                pool.sem_inc(pool_mark, 1)
                inverse_spread(rs3, mv3, s, rs3_set, t)

            pool.wait_ge(params_in, 16 * len(params))
            pipeline(pool, (spread_3, 6), (ffn_offset, 0), (spread_2, 4), (norm_offset, 4))

            pool.wait_ge(xs_zeroed, 16 * 2 * TURNS)
            pool.wait_ge(pos_set, 1)
            for t in range(NT):
                nc.gpsimd.indirect_dma_start(xs_dram.ap()[:, :], bass.IndirectOffsetOnAxis(ap=pos_i[:, t:t + 1], axis=0),
                                             xf_all[:, t, :], None).then_inc(xs_stored, 16)

            pool.wait_ge(w_made, 16 * len(w_parts))
            pool.wait_ge(own_set, 1)

            def weights(j, s, u):
                wait_from(pool, o_ps, j - ES + 1)
                nc.gpsimd.tensor_copy(oidx[:, s:s + 1], own_row[:, bass.ds(j, 1)]).then_inc(oidx_set, 1)
                pool.wait_ge(oidx_set, j + 1)
                pool.sem_inc(pool_mark, 1)
                nc.gpsimd.indirect_dma_start(ws_e[:, s, 0:W_ROW], None, w_dram.ap()[:, :],
                                             bass.IndirectOffsetOnAxis(ap=oidx[:, s:s + 1], axis=0)).then_inc(w_in[s], 16)

            pipeline(pool, (weights, 0), n=MT, per=ES)

            for s in range(ES):
                pool.wait_ge(ys_stored[s], 16 * (MT // ES))
            for i in range(XLOADS):
                for t in range(i * NT // XLOADS, (i + 1) * NT // XLOADS):
                    nc.gpsimd.indirect_dma_start(xf_all[:, t, :], None, ys_dram.ap()[:, :],
                                                 bass.IndirectOffsetOnAxis(ap=pos_i[:, t:t + 1], axis=0)).then_inc(gath_in[i], 16)

        @block.scalar
        def _(act):
            for nm in ("we", "be"):
                act.dma_start(rows[nm][0][:, :], rows[nm][1].partition_broadcast(P)).then_inc(scal_in, 16)
            for dst_ap, src_ap in first_params:
                act.dma_start(dst_ap, src_ap, allow_slow_non_contiguous=True).then_inc(kv_params_in, 16)
            for dst_ap, src_ap in params:
                act.dma_start(dst_ap, src_ap, allow_slow_non_contiguous=True).then_inc(params_in, 16)
            act.wait_ge(kv_params_in, 16 * len(first_params))
            act.wait_ge(consts_set, NCONST)
            nc.scalar.mul(bqs_col[:, :], bq_col[:, :], SCALE).then_inc(q_ready, 1)

            act.wait_ge(stats_set, 1)

            def n_norm(t, s, u):
                wait_from(act, hT_ps, t - 1)
                nc.scalar.activation(h[:, s, :], node_tile(V, t), ACT.Identity, bias=nmr[:, bass.ds(t, 1)],
                                     scale=rstd[:, bass.ds(t, 1)]).then_inc(h_ready, 1)

            def n_front(t, s, u):
                act.wait_ge(hT_ps, t + 1)
                wait_from(act, vs_ps, t - 1)
                nc.scalar.copy(hT[:, s, :, :], bank[2 + s][:, 0:KH * TILE].rearrange("p (k t) -> p k t", k=KH)).then_inc(hT_ready, 1)

            def n_back(t, s, u):
                act.wait_ge(kq_ps, t + 1)
                for m in range(KH):
                    ins = nc.scalar.activation(kT[:, m, bass.ds(t, 1), 0:TILE].rearrange("p a l -> p (a l)"),
                                               bank[4 + s][:, m * TILE:(m + 1) * TILE], ACT.Identity, bias=bk_col[:, m:m + 1])
                ins.then_inc(k_ready, 1)
                if isinstance(t, int):
                    act.wait_ge(q_ready, 1)
                wait_from(act, q_stored[s], 16 * u)
                for m in range(KH):
                    ins = nc.scalar.activation(qs[:, s, m, :], bank[4 + s][:, (KH + m) * TILE:(KH + m + 1) * TILE], ACT.Identity,
                                               bias=bqs_col[:, m:m + 1], scale=SCALE)
                ins.then_inc(q_ready, 1)
                act.wait_ge(vs_ps, t + 1)
                nc.scalar.copy(node_tile(V, t), bank[6 + s][0:TILE, 0:D])
                nc.scalar.copy(node_tile(x1, t), bank[6 + s][0:TILE, D:2 * D]).then_inc(vs_ready, 1)
                act.wait_ge(q_ready, t + 2)
                act.dma_start(q_v[:, bass.ds(t, 1), :].rearrange("p t c -> p (t c)"),
                              qs[:, s, :, :].rearrange("p k t -> p (k t)")).then_inc(q_stored[s], 16)

            step = staged(n_norm, n_front, n_back)

            def turn_of_nodes(i):
                step(2 * i, 0, i, i)
                step(2 * i + 1, 1, i, i + 1)

            act.wait_ge(stats_set, 2)
            with act.Fori(1, KV_FIRST) as i:
                turn_of_nodes(i)
            act.wait_ge(guard_set, 1)
            nc.scalar.activation(vals_o, t_e.rearrange("p (k e) -> p k e", k=PC), ACT.Exp).then_inc(val_set, 1)
            with act.Fori(KV_FIRST, NT // 2 - 1) as i:
                turn_of_nodes(i)
            for t in range(NT - 3, NT):
                step(t, t % 2, t // 2, (t + 1) // 2)

            for b in range(SBLK):
                act.wait_ge(tabT_done, b + 1)
                ps = bank[6 + b % 2][:, :].rearrange("p (c u i) -> p c i u", c=2, u=SUB)

                def steps(tab):
                    return tab[:, b * SUB * P:(b + 1) * SUB * P].rearrange("p (i u) -> p i u", u=SUB)

                nc.scalar.copy(steps(code_tab), ps[:, 0, :, :])
                nc.scalar.mul(steps(nval_tab), ps[:, 1, :, :], -1.0).then_inc(tab_set, 1)

            def query_parts(t, s, u):
                act.wait_ge(q_in[s], 16 * (u + 1))
                wait_from(act, s_ready, len(SCH) * (t - 1))
                nc.scalar.copy(q_hi[:, s, :, :], qT[:, s, :, :]).then_inc(q_hi_set, 1)

            for t in range(2):
                query_parts(t, t, 0)

            act.wait_ge(terms_stored, 16 * SUB * SBLK)

            def columns(g, j, i):
                s, q = j % 2, j % STAGES
                act.wait_ge(dist_done, g + 1)
                wait_from(act, prod_done, g - STAGES + 1)
                for k in range(GC):
                    i = g * GC + k
                    ins = nc.scalar.activation(Ys[:, q, k, :], bank[2 + s][:, k * LO:(k + 1) * LO], ACT.Relu,
                                               scale=nval_tab[:, bass.ds(i, 1)])
                ins.then_inc(y_ready, 1)

            turns(act, columns)

            def exps(t, s, b):
                c, n = SCH[b]
                ins = nc.scalar.activation(Z[0:TILE, s, c:c + n], Z[0:TILE, s, c:c + n], ACT.Exp, bias=nmax[:, s:s + 1])
                if b == len(SCH) - 1:
                    ins.then_inc(e_ready, 1)

            def key_parts(b):
                c, n = SCH[b]
                j = slice(c // LO, (c + n) // LO)
                nc.scalar.copy(k_hi[:, :, j, :], kT[:, :, j, :]).then_inc(k_hi_set, 1)

            def weights(t, s, t_next, u):
                if not (isinstance(t, int) and t + 2 >= NT):
                    query_parts(t + 2, s, u + 1)
                wait_from(act, attn_done, t - 1)
                for g, (j, n) in enumerate(TRG):
                    act.wait_ge(tr_ready, len(TRG) * t + g + 1)
                    nc.scalar.copy(PT[0:TILE, s, j:j + n, :], bank[4 + g % 2][0:TILE, 0:n * TILE].rearrange(
                        "p (n d) -> p n d", n=n)).then_inc(pt_ready, 1)
                    if t_next is not None and g:
                        if g == 1:
                            act.wait_ge(nmax_set, t_next + 1)
                        exps(t_next, 1 - s, g - 1)
                if t_next is not None:
                    exps(t_next, 1 - s, len(SCH) - 1)

            assert len(TRG) == len(SCH)
            act.wait_ge(k_ready, NT)
            act.wait_ge(sums_ready, NG)
            for b in range(len(SCH)):
                key_parts(b)
            act.wait_ge(nmax_set, 1)
            for b in range(len(SCH)):
                exps(0, 0, b)
            for t in range(2):
                weights(t, t, t + 1, 0)
            with act.Fori(1, NT // 2 - 1) as i:
                weights(2 * i, 0, 2 * i + 1, i)
                weights(2 * i + 1, 1, 2 * i + 2, i)
            for t in range(NT - 3, NT):
                weights(t, t % 2, t + 1 if t + 1 < NT else None, t // 2)

            act.wait_ge(params_in, 16 * len(params))

            def f_pick(t, s, u):
                act.wait_ge(x1n_set, t + 1)
                wait_from(act, x1T_ps, t - 1)
                nc.scalar.copy(x1c[0:TILE, s, :], node_tile(x1, t)).then_inc(x1c_set, 1)

            def f_copy(t, s, u):
                act.wait_ge(x1T_ps, t + 1)
                wait_from(act, f1_ps, t - 1)
                nc.scalar.copy(x1T[:, s, :, :], bank[s][:, 0:KH * TILE].rearrange("p (k t) -> p k t", k=KH)).then_inc(x1T_set, 1)

            def f_gelu(t, s, u):
                act.wait_ge(f1_ps, t + 1)
                wait_from(act, f2_ps, t - 1)
                for m in range(FF // P):
                    ins = nc.scalar.activation(gT[:, s, m, :], bank[2 + s][:, m * TILE:(m + 1) * TILE], ACT.Gelu_apprx_tanh,
                                               bias=bf1_col[:, m:m + 1])
                ins.then_inc(g_set, 1)

            def r_pick(t, s, u):
                act.wait_ge(xf_set, t + 1)
                wait_from(act, xfT_ps, t - 1)
                nc.scalar.copy(xf[0:TILE, s, :], node_tile(xf_all, t)).then_inc(xfc_set, 1)

            def r_copy(t, s, u):
                act.wait_ge(xfT_ps, t + 1)
                wait_from(act, lg_ps, t - 1)
                nc.scalar.copy(xfT[:, s, :, :], bank[6 + s][:, 0:KH * TILE].rearrange("p (k t) -> p k t", k=KH)).then_inc(xfT_set, 1)

            pipeline(act, (f_pick, 0), (r_copy, R_LAG + 1), (f_gelu, 1), (f_copy, 0), (r_pick, R_LAG))

            act.wait_ge(ones_row, 1)

            def e_copy(j, s, u):
                act.wait_ge(xsT_ps, j + 1)
                wait_from(act, hid_ps, j - ES + 1)
                nc.scalar.copy(xsT[:, s, :], bank[j_bank(0, s)][:, 0:KH * P]).then_inc(xsT_set, 1)

            def e_relu(j, s, u):
                act.wait_ge(hid_ps, j + 1)
                wait_from(act, o_ps, j - ES + 1)
                nc.scalar.activation(hid[0:HID, s, :], bank[j_bank(2, s)][0:HID, 0:P], ACT.Relu,
                                     bias=w2s[0:HID, s, D:D + 1]).then_inc(hid_set, 1)

            pipeline(act, (e_relu, 2), (e_copy, 0), n=MT, per=ES)

        @block.vector
        def _(dve):
            V_ = nc.vector
            pad0 = E % EROW
            V_.memset(di[:, pad0:EROW], N).then_inc(pads_set, 1)
            V_.memset(si[:, pad0:EROW], 0).then_inc(pads_set, 1)
            V_.memset(w_e[:, pad0:EROW], 0.0).then_inc(pads_set, 1)
            od = Order(dve, dve_ord)

            def rounded(ap, in_ap, mul, add):
                od(V_.tensor_scalar(ap, in_ap, mul, add, ALU.mult, ALU.add))
                od(V_.tensor_scalar_add(ap, ap, MAGIC))
                od(V_.tensor_scalar_add(ap, ap, -MAGIC))

            def statistics(st, t0=0, t1=NT):
                st = st[:, t0:t1, :]
                mean_, dif_, var_, rstd_ = (v[:, t0:t1] for v in (mean, dif, var, rstd))
                od(V_.tensor_tensor(mean_, st[:, :, 1], st[:, :, 4], ALU.add))
                od(V_.tensor_scalar_mul(mean_, mean_, 0.5))
                od(V_.tensor_tensor(dif_, st[:, :, 1], st[:, :, 4], ALU.subtract))
                od(V_.tensor_tensor(var_, st[:, :, 2], st[:, :, 5], ALU.add))
                od(V_.scalar_tensor_tensor(dif_, dif_, 0.25, dif_, ALU.mult, ALU.mult))
                od(V_.tensor_scalar(var_, var_, 1.0 / D, EPS, ALU.mult, ALU.add))
                od(V_.tensor_tensor(var_, var_, dif_, ALU.add))
                od(V_.tensor_single_scalar(rstd_.bitcast(I32), var_.bitcast(I32), 1, ALU.logical_shift_right))
                od(V_.tensor_scalar(rstd_.bitcast(I32), rstd_.bitcast(I32), -1.0, RSQRT, ALU.mult, ALU.add))
                for _ in range(NEWTON):
                    od(V_.tensor_tensor(dif_, rstd_, rstd_, ALU.mult))
                    od(V_.tensor_tensor(dif_, dif_, var_, ALU.mult))
                    od(V_.tensor_scalar(dif_, dif_, -0.5, 1.5, ALU.mult, ALU.add))
                    od(V_.tensor_tensor(rstd_, rstd_, dif_, ALU.mult))

            def st_tile(st, t):
                return st[:, bass.ds(t, 1), :].rearrange("p t c -> p (t c)")

            for part in ((0,), range(1, XLOADS)):
                for i in part:
                    dve.wait_ge(nodes_in[i], 16)
                    for t in range(i * NT // XLOADS, (i + 1) * NT // XLOADS):
                        V_.bn_stats(st_tile(st0, t), node_tile(V, t)).then_inc(dve_ord, 1)
                t0, t1 = part[0] * NT // XLOADS, (part[-1] + 1) * NT // XLOADS
                od.n += t1 - t0
                dve.wait_ge(dve_ord, od.n)
                statistics(st0, t0, t1)
                V_.scalar_tensor_tensor(nmr[:, t0:t1], mean[:, t0:t1], -1.0, rstd[:, t0:t1], ALU.mult, ALU.mult).then_inc(stats_set, 1)

            dve.wait_ge(consts_set, NCONST)
            i1 = iota_row[0:1, :]
            od(V_.tensor_tensor(cmp_o[0:1, 0:P], i1, i1, ALU.mult))
            rounded(cmp_o[0:1, P:2 * P], cmp_o[0:1, 0:P], 1.0 / P, 0.0)
            od(V_.tensor_scalar_mul(dist_line[:, 0, :], cmp_o[0:1, P:2 * P], float(P)))
            od(V_.scalar_tensor_tensor(dist_line[:, 1, :], cmp_o[0:1, 0:P], -1.0, dist_line[:, 0, :], ALU.add, ALU.subtract))
            od(V_.tensor_copy(dist_line[:, 2, :], i1))
            V_.memset(dist_line[:, 3:DIST, :], 1.0).then_inc(dist_set, 1)
            dve.wait_ge(dst_in, 16 * 3)
            od(V_.tensor_copy(fcol[0:PP, :], di[:, 0:EROW:SPAN]))
            rounded(fcol[0:PP, :], fcol[0:PP, :], 1.0 / WIN, 0.5 / WIN - 0.5)
            for b in range(PS):
                ins = V_.tensor_scalar(diag_c[:, b, :], ident[0:PP, 0:PP], fcol[0:PP, b:b + 1], None, ALU.mult)
            ins.then_inc(diag_set, 1)
            dve.wait_ge(edges_in, 16 * 6)
            dve.wait_ge(scal_in, 32)
            od(V_.tensor_scalar(w_e, w_e, row["we"][0:PP, 0:1], row["be"][0:PP, 0:1], ALU.mult, ALU.add))
            od(V_.tensor_copy(dstf, di))
            od(V_.tensor_tensor(neg_e[:, 1:EROW], dstf[:, 1:EROW], dstf[:, 0:EROW - 1], ALU.is_equal))
            od(V_.tensor_scalar(neg_e[:, 1:EROW], neg_e[:, 1:EROW], -1.0, BIG, ALU.add, ALU.mult))
            od(V_.memset(neg_e[:, 0:1], -BIG))
            od(V_.memset(neg_e[:, EROW:EROW + 1], -BIG))
            od(V_.tensor_tensor_scan(F_e, neg_e[:, 0:EROW], w_e, -BIG, ALU.add, ALU.max))
            od(V_.tensor_tensor_scan(B_e[:, ::-1], neg_e[:, 1:EROW + 1][:, ::-1], F_e[:, ::-1], -BIG, ALU.add, ALU.max))
            firsts, lasts = dstf[:, 0:1], dstf[:, EROW - 1:EROW]
            for q, col in enumerate((firsts, lasts, B_e[:, 0:1], B_e[:, EROW - 1:EROW])):
                ins = V_.tensor_scalar(diag_e[:, q, :], ident[0:PP, 0:PP], col, None, ALU.mult)
            ins.then_inc(diag_set, 1)
            dve.wait_ge(rows_bc, 1)
            od(V_.tensor_copy(s_row, bank[0][:, 0:NS]))
            od(V_.memset(s_row[:, 0:1], 0.0))
            od(V_.tensor_tensor(o_row, s_row, iota_c, ALU.add))
            dve.wait_ge(rows_bc, 2)
            segcmp, segval = cmp_o[0:PP, 0:2 * PP], cmp_o[0:PP, 2 * PP:4 * PP]
            for q, col in enumerate((firsts, lasts)):
                od(V_.tensor_scalar(segcmp, bank[1][0:PP, 0:2 * PP], col, -1.0, ALU.is_equal, ALU.add))
                od(V_.scalar_tensor_tensor(segval, segcmp, BIG, bank[1][0:PP, 2 * PP:4 * PP], ALU.mult, ALU.add))
                od(V_.tensor_reduce(guards[0:PP, q:q + 1], segval, AX, ALU.max))

            for q, col in enumerate((firsts, lasts)):
                od(V_.tensor_scalar(t_e, dstf, col, -1.0, ALU.is_equal, ALU.add))
                od(V_.tensor_scalar(t_e, t_e, BIG, guards[0:PP, q:q + 1], ALU.mult, ALU.add))
                od(V_.tensor_tensor(B_e, B_e, t_e, ALU.max))
            V_.scalar_tensor_tensor(t_e, w_e, SHIFT, B_e, ALU.add, ALU.subtract).then_inc(guard_set, 1)
            dve.wait_ge(guard_set, 1)
            for b in range(SBLK):
                od(V_.tensor_scalar(cmp_s, o_row, step_col[:, b:b + 1], None, ALU.is_le))
                od(V_.tensor_reduce(cnt[:, b:b + 1], cmp_s, AX, ALU.add))
            od(V_.tensor_scalar_add(cnt[:, :], cnt[:, :], -1.0))
            for u in range(SUB):
                ins = V_.tensor_scalar(cidx[:, u, :], cnt[:, :], float(SUB), float(u), ALU.mult, ALU.add)
            ins.then_inc(idx_set, 1)
            od(V_.tensor_tensor(wneg[:, :], cnt[:, :], step_col[:, :], ALU.subtract))
            od(V_.tensor_scalar_mul(wneg[:, :], wneg[:, :], float(WIN * NT)))
            chunked = lambda ap: ap.rearrange("p (k e) -> p k e", k=PC)
            od(V_.tensor_copy(srcf, si))
            rounded(hi_e[:, 0:EROW], srcf, 1.0 / TILE, 0.5 / TILE - 0.5)
            od(V_.scalar_tensor_tensor(codes_o, chunked(dstf), float(NT), chunked(hi_e[:, 0:EROW]), ALU.mult, ALU.add))
            od(V_.scalar_tensor_tensor(srcf, hi_e[:, 0:EROW], -float(TILE), srcf, ALU.mult, ALU.add))
            od(V_.tensor_scalar_mul(terms_o[:, :, 0, :], chunked(srcf), -2.0))
            od(V_.tensor_tensor(sq_e, srcf, srcf, ALU.mult))
            rounded(sqh_e, sq_e, 1.0 / P, 0.0)
            od(V_.tensor_scalar_mul(terms_o[:, :, 1, :], chunked(sqh_e), float(P)))
            V_.scalar_tensor_tensor(terms_o[:, :, 2, :], chunked(sqh_e), -float(P), chunked(sq_e), ALU.mult,
                                    ALU.add).then_inc(code_set, 1)
            dve.wait_ge(code_set, 1)
            for b in range(SBLK):
                ins = V_.tensor_scalar(diag[:, b, :], ident[:, :], cnt[:, b:b + 1], None, ALU.mult)
            ins.then_inc(diag_set, 1)
            for b in range(NWB):
                od(V_.tensor_scalar(cmp_s[0:TILE, :], s_row[0:TILE, :], win_col[0:TILE, b:b + 1], None, ALU.is_le))
                od(V_.tensor_reduce(wcnt[0:TILE, b:b + 1], cmp_s[0:TILE, :], AX, ALU.add))
            od(V_.tensor_tensor(wcnt[0:TILE, :], wcnt[0:TILE, :], win_col[0:TILE, :], ALU.add))
            od(V_.tensor_scalar(wcnt[0:TILE, :], wcnt[0:TILE, :], -1.0, float(WIN), ALU.add, ALU.mult))
            V_.tensor_copy(wrow[0:TILE, :], wcnt[0:TILE, :]).then_inc(last_set, 1)
            for b in range(SBLK):
                dve.wait_ge(gath_in[b], 16 * SUB)
                codes = gath[:, b, :, 0:CHUNK]
                V_.tensor_scalar_add(codes, codes, wneg[:, b:b + 1]).then_inc(rel_set, 1)
            rounded(pmod[:, :], step_col[:, 0:1], 1.0 / WIN, 0.5 / WIN - 0.5)
            od(V_.scalar_tensor_tensor(pmod[:, :], pmod[:, :], -float(WIN), step_col[:, 0:1], ALU.mult, ALU.add))
            dve.wait_ge(last_in, 16 * WIN)
            od(V_.tensor_copy(arowf[0:TILE, :], arow0[0:TILE, :]))
            od(V_.tensor_scalar_add(arowf[0:TILE, :], arowf[0:TILE, :], pmod[0:TILE, 0:1]))
            V_.tensor_copy(arow[0:TILE, :], arowf[0:TILE, :]).then_inc(arow_set, 1)
            dve.wait_ge(rows_bc, 3)
            for c in range(0, SLOTS, 512):
                n = min(512, SLOTS - c)
                od(V_.tensor_copy(c_row[:, c:c + n], bank[3 + c // 512][:, 0:n]))
            od(V_.memset(keep_tab[:, 0:1], 0.0))
            V_.tensor_tensor(keep_tab[:, 1:SLOTS], c_row[:, 1:SLOTS], c_row[:, 0:SLOTS - 1],
                             ALU.subtract).then_inc(keep_set, 1)
            dve.wait_ge(keep_set, 1)
            dve.wait_ge(tab_set, SBLK)
            dve.wait_ge(terms_stored, 16 * SUB * SBLK)

            def query_rest(t, s, u):
                dve.wait_ge(q_hi_set, t + 1)
                V_.tensor_tensor(q_lo[:, s, :, :], qT[:, s, :, :], q_hi[:, s, :, :].bitcast(F32), ALU.subtract).then_inc(q_split, 1)

            for t in range(2):
                query_rest(t, t, 0)

            def one_hot(g, s, k):
                cols = slice(k * SUB, (k + 1) * SUB)
                ins = V_.tensor_tensor(Xs[:, s, cols, :], iota_row[:, 0:TILE].unsqueeze(1).to_broadcast([P, SUB, TILE]),
                                       code_tab[:, bass.ds(g * GC + k * SUB, SUB)].unsqueeze(2).to_broadcast([P, SUB, TILE]),
                                       ALU.is_equal)
                if k == GROUP - 1:
                    ins.then_inc(x_ready, 1)

            for g in range(STAGES - 1):
                for k in range(GROUP):
                    one_hot(g, g, k)

            def sums(g, j, i):
                q = j % STAGES
                dve.wait_ge(prod_done, g + 1)
                wait_from(dve, stored[q], 16 * ((BODY // STAGES) * i + j // STAGES))
                for k in range(GROUP):
                    first = isinstance(g, int) and g == 0 and k == 0
                    if k:
                        dve.wait_ge(sum_ord, g * (GROUP - 1) + k)
                    elif not first:
                        dve.wait_ge(sums_ready, g)
                    prev = stage[0:TILE, q, k - 1, :] if k else stage[0:TILE, (q - 1) % STAGES, GROUP - 1, :]
                    ps = product_bank(j)[0:TILE, k * LO:(k + 1) * LO]
                    if first:
                        ins = V_.tensor_copy(stage[0:TILE, q, k, :], ps)
                    else:
                        ins = V_.scalar_tensor_tensor(stage[0:TILE, q, k, :], prev,
                                                      keep_tab[0:TILE, bass.ds(g * GROUP + k, 1)], ps, ALU.mult, ALU.add)
                    ins.then_inc(sum_ord if k < GROUP - 1 else sums_ready, 1)
                    if not (isinstance(i, int) and i == TURNS - 1 and j > BODY - STAGES):
                        one_hot(g + STAGES - 1, (q - 1) % STAGES, k)

            turns(dve, sums)

            f_ord = Order(dve, front_ord, 1)
            b_ord = Order(dve, back_ord, 6)
            dve.wait_ge(params_in, 16 * len(params))

            def key_rest(b):
                c, n = SCH[b]
                j = slice(c // LO, (c + n) // LO)
                dve.wait_ge(k_hi_set, b + 1)
                V_.tensor_tensor(k_lo[:, :, j, :], kT[:, :, j, :], k_hi[:, :, j, :].bitcast(F32), ALU.subtract).then_inc(k_split, 1)

            def exclude(t, s, u):
                dve.wait_ge(a_in[s], 16 * (u + 1))
                wait_from(dve, tr_ready, len(TRG) * (t - 1))
                V_.tensor_scalar(Z[0:TILE, s, :], A_sb[0:TILE, s, :], 0.0, -BIG, ALU.is_equal, ALU.mult).then_inc(excluded, 1)

            def guard(t, s, u):
                f_ord.begin(t)
                dve.wait_ge(excluded, t + 1)
                for b, (c, n) in enumerate(SCH):
                    dve.wait_ge(s_ready, len(SCH) * t + b + 1)
                    dve.sem_inc(dve_mark, 1)
                    V_.tensor_tensor_reduce(out=Z[0:TILE, s, c:c + n], in0=bank[b % 4][0:TILE, 0:n], in1=Z[0:TILE, s, c:c + n],
                                            scale=1.0, scalar=-BIG, op0=ALU.add, op1=ALU.max,
                                            accum_out=mx[:, b:b + 1]).then_inc(s_used, 1)
                dve.wait_ge(s_used, len(SCH) * (t + 1))
                f_ord(V_.tensor_reduce(mxr[:, :], mx[:, 0:len(SCH)], AX, ALU.max))
                V_.tensor_scalar(nmax[:, s:s + 1], mxr[:, :], -1.0, SHIFT, ALU.mult, ALU.add).then_inc(nmax_set, 1)
                f_ord.end()

            def weigh(t, s, u):
                dve.wait_ge(e_ready, t + 1)
                V_.tensor_tensor_reduce(out=Z[0:TILE, s, :], in0=Z[0:TILE, s, :], in1=A_sb[0:TILE, s, :], scale=1.0,
                                        scalar=0.0, op0=ALU.mult, op1=ALU.add, accum_out=den[:, s:s + 1]).then_inc(p_ready, 1)

            def back(t, s, u):
                b_ord.begin(t)
                dve.wait_ge(p_ready, t + 1)
                b_ord(V_.tensor_scalar(has[:, s:s + 1], den[:, s:s + 1], 0.0, None, ALU.is_gt))
                b_ord(V_.tensor_scalar_max(rden[:, s:s + 1], den[:, s:s + 1], 1e-37))
                b_ord(V_.reciprocal(rden[:, s:s + 1], rden[:, s:s + 1]))
                dve.wait_ge(attn_done, t + 1)
                V_.scalar_tensor_tensor(yt[:, :], bank[6 + s][0:TILE, 0:D], rden[:, s:s + 1], node_tile(x1, t),
                                        ALU.mult, ALU.add).then_inc(o_used, 1)
                dve.wait_ge(o_used, t + 1)
                b_ord(V_.scalar_tensor_tensor(yt[:, :], row["bv"][0:TILE, :], has[:, s:s + 1], yt[:, :], ALU.mult, ALU.add))
                b_ord(V_.tensor_tensor(node_tile(x1, t), yt[:, :], row["bs"][0:TILE, :], ALU.add), dve_mark)
                b_ord(V_.bn_stats(st_tile(st1, t), node_tile(x1, t)))
                dve.sem_inc(x1_ready, 1)
                b_ord.end()

            for b in range(len(SCH)):
                key_rest(b)
            def early_statistics(t, s, u):
                if isinstance(t, int) and t == NT - 1:
                    statistics(st1, 0, NT - 2)

            def later_query_rest(t, s, u):
                if not (isinstance(t, int) and t < 2):
                    query_rest(t, s, u)

            pipeline(dve, (guard, 1), (back, 3), (early_statistics, 2), (later_query_rest, 0), (weigh, 1), (exclude, 0))

            od(V_.memset(hid[HID:XROW, :, :], 1.0))
            dve.sem_inc(ones_row, 1)

            def x1_scale(t, s, u):
                v = node_tile(x1, t)
                if isinstance(t, int) and t == 3:
                    statistics(st1, NT - 2, NT)
                V_.scalar_tensor_tensor(v, v, mean[:, bass.ds(t, 1)], row["g1"][0:TILE, :], ALU.subtract, ALU.mult).then_inc(
                    x1s_set, 1)

            def x1_offset(t, s, u):
                v = node_tile(x1, t)
                dve.wait_ge(x1s_set, t + 1)
                V_.scalar_tensor_tensor(v, v, rstd[:, bass.ds(t, 1)], row["b1"][0:TILE, :], ALU.mult, ALU.add).then_inc(x1n_set, 1)

            def y2_sum(t, s, u):
                dve.wait_ge(f2_ps, t + 1)
                dve.wait_ge(x1b_set, t + 1)
                V_.tensor_tensor(node_tile(x1, t), bank[4 + s][0:TILE, 0:D], node_tile(x1, t), ALU.add).then_inc(y2_used, 1)

            def y2_stats(t, s, u):
                dve.wait_ge(y2_used, t + 1)
                dve.sem_inc(dve_mark, 1)
                V_.bn_stats(st2[:, s, :], node_tile(x1, t)).then_inc(st2_set, 1)

            def y2_var(t, s, u):
                dve.wait_ge(st2_set, t + 1)
                dve.sem_inc(dve_mark, 1)
                V_.bn_aggr(mv2[:, s, :], st2[:, s, :]).then_inc(mv2_set, 1)

            def x2_scale(t, s, u):
                v = node_tile(x1, t)
                dve.wait_ge(rs2_set, 2 * t + 2)
                V_.scalar_tensor_tensor(v, v, mv2[:, s, 0:1], row["g2"][0:TILE, :], ALU.subtract, ALU.mult).then_inc(x2s_set, 1)

            def x2_sum(t, s, u):
                v = node_tile(x1, t)
                dve.wait_ge(x2s_set, t + 1)
                dve.wait_ge(xb_set, t + 1)
                V_.scalar_tensor_tensor(v, v, rs2[:, s:s + 1], node_tile(x_all, t), ALU.mult, ALU.add).then_inc(x2_set, 1)

            def x2_stats(t, s, u):
                dve.wait_ge(x2_set, t + 1)
                dve.sem_inc(dve_mark, 1)
                V_.bn_stats(st3[:, s, :], node_tile(x1, t)).then_inc(st3_set, 1)

            def x2_var(t, s, u):
                dve.wait_ge(st3_set, t + 1)
                wait_from(dve, xf_set, t - 1)
                dve.sem_inc(dve_mark, 1)
                V_.bn_aggr(mv3[:, s, :], st3[:, s, :]).then_inc(mv3_set, 1)

            def r_norm(t, s, u):
                dve.wait_ge(rs3_set, 2 * t + 2)
                V_.tensor_scalar(node_tile(xf_all, t), node_tile(x1, t), mv3[:, s, 0:1], rs3[:, s:s + 1],
                                 ALU.subtract, ALU.mult).then_inc(xf_set, 1)

            def r_logits(t, s, u):
                dve.wait_ge(lg_ps, t + 1)
                V_.tensor_tensor(node_tile(by_tile(lg), t)[0:TILE, :], bank[6 + s][0:TILE, D:D + NEXP], row["rb"][0:TILE, :],
                                 ALU.add).then_inc(lg_set, 1)

            pipeline(dve, (r_logits, R_LAG + 3), (x2_var, 6), (y2_sum, 4), (x1_scale, 0), (x2_scale, 5), (y2_stats, 4), (x1_offset, 0),
                     (x2_sum, 5), (r_norm, 7), (y2_var, 4), (x2_stats, 5))
            dve.wait_ge(lg_set, NT)
            lg_t, work_t, hot_t = (by_tile(ap)[0:TILE] for ap in (lg, work, hot))
            e_bc = iota_row[0:TILE, 0:NEXP].unsqueeze(1).to_broadcast([TILE, NT, NEXP])

            def over_experts(ap):
                return ap[:, :].unsqueeze(2).to_broadcast([TILE, NT, NEXP])

            FAR = 1024.0
            od(V_.tensor_reduce(best[:, :], lg_t, AX, ALU.max))
            od(V_.tensor_tensor(work_t, lg_t, over_experts(best), ALU.is_equal))
            od(V_.scalar_tensor_tensor(work_t, work_t, -FAR, e_bc, ALU.mult, ALU.add))
            od(V_.tensor_reduce(exp_of[:, :], work_t, AX, ALU.min))
            od(V_.tensor_scalar_add(exp_of[:, :], exp_of[:, :], FAR))
            V_.tensor_tensor(hot_t, e_bc, over_experts(exp_of), ALU.is_equal).then_inc(hot_set, 1)
            od(V_.memset(fresh, 1.0))
            od(V_.memset(by_exp(fresh)[:, :, 0:1], 0.0))
            dve.wait_ge(ranks_ps, 1)
            half = (NT + 1) // 2
            for q, (t0, n) in enumerate(((0, half), (half, NT - half))):
                ps = bank[2 + q][:, 0:n * NEXP].rearrange("p (t e) -> p e t", e=NEXP)
                od(V_.tensor_copy(by_exp(total)[:, :, t0:t0 + n], ps))
            od(V_.tensor_tensor_scan(upto, fresh, total, 0.0, ALU.mult, ALU.add))
            rounded(ntile[:, :], by_exp(upto)[:, :, NT - 1], 1.0 / P, (P - 1.0) / P - 0.5 + 0.5 / P)
            od(V_.tensor_tensor_scan(tincl[:, :], ones[:, 0:NEXP], ntile[:, :], 0.0, ALU.mult, ALU.add))
            od(V_.tensor_tensor(tbase[:, :], tincl[:, :], ntile[:, :], ALU.subtract))
            od(V_.tensor_scalar_mul(tbase[:, :], tbase[:, :], float(P)))
            od(V_.tensor_tensor(upto, upto, total, ALU.subtract))
            od(V_.tensor_tensor(by_exp(upto), by_exp(upto), tbase[:, :].unsqueeze(2).to_broadcast([P, NEXP, NT]), ALU.add))
            for q, (t0, n) in enumerate(((0, half), (half, NT - half))):
                ps = bank[q][0:TILE, 0:n * NEXP].rearrange("p (t e) -> p t e", e=NEXP)
                od(V_.tensor_tensor(work_t[:, t0:t0 + n, :], ps, by_exp(upto)[0:TILE, :, t0:t0 + n].rearrange("p e t -> p t e"),
                                    ALU.add))
            od(V_.tensor_tensor(work_t, work_t, hot_t, ALU.mult))
            od(V_.tensor_reduce(pos[:, :], work_t, AX, ALU.add))
            V_.tensor_copy(pos_i[:, :], pos[:, :]).then_inc(pos_set, 1)
            od(V_.tensor_tensor(owner, tincl[:, :].unsqueeze(1).to_broadcast([P, MT, NEXP]),
                                iota_row[:, 0:MT].unsqueeze(2).to_broadcast([P, MT, NEXP]), ALU.is_le))
            od(V_.tensor_reduce(own[:, :], owner, AX, ALU.add))
            od(V_.tensor_scalar_min(own[:, :], own[:, :], NEXP - 1.0))
            V_.tensor_scalar(own_row[:, :], own[:, :], float(P), step_col[:, 0:1], ALU.mult, ALU.add).then_inc(own_set, 1)

            def e_out(j, s, u):
                dve.wait_ge(o_ps, j + 1)
                wait_from(dve, ys_stored[s], 16 * u)
                V_.tensor_scalar_max(ys[:, s, :], bank[j_bank(4, s)][:, 0:D], 0.0).then_inc(ys_set, 1)

            pipeline(dve, (e_out, 0), n=MT, per=ES)
            for i in range(XLOADS):
                c = slice(i * NT // XLOADS, (i + 1) * NT // XLOADS)
                dve.wait_ge(gath_in[i], 16 * (SUB + NT // XLOADS))
                V_.tensor_tensor(x1[:, c, :], x1[:, c, :], xf_all[:, c, :], ALU.add).then_inc(o_set, 1)

        @block.tensor
        def _(pe):
            mm = nc.tensor.matmul
            tr = nc.tensor.transpose
            pe.wait_ge(consts_set, NCONST)
            def transposed(src_ap, ps):
                for k in range(KH):
                    ins = tr(ps[:, k * TILE:(k + 1) * TILE], src_ap[:, k * P:(k + 1) * P], ident[0:TILE, 0:TILE])
                return ins

            pe.wait_ge(kv_params_in, 16 * len(first_params))
            pe.wait_ge(ws_set, KH)

            def n_front(t, s, u):
                pe.wait_ge(h_ready, t + 1)
                wait_from(pe, hT_ready, t - 1)
                transposed(h[:, s, :], bank[2 + s]).then_inc(hT_ps, 1)

            def n_back(t, s, u):
                pe.wait_ge(hT_ready, t + 1)
                wait_from(pe, q_ready, t)
                for w, w_sb in enumerate((wk_sb, wq_sb)):
                    for m in range(KH):
                        for k in range(KH):
                            ins = mm(bank[4 + s][:, (KH * w + m) * TILE:(KH * w + m + 1) * TILE], w_sb[:, k, m * P:(m + 1) * P],
                                     hT[:, s, k, :], start=(k == 0), stop=(k == KH - 1))
                ins.then_inc(kq_ps, 1)
                wait_from(pe, vs_ready, t - 1)
                for k in range(KH):
                    mm(bank[6 + s][0:TILE, 0:D], hT[:, s, k, :], wv_sb[:, k, :], start=(k == 0), stop=(k == KH - 1))
                for k in range(KH):
                    ins = mm(bank[6 + s][0:TILE, D:2 * D], hT[:, s, k, :], ws_sb[:, k, :], start=(k == 0), stop=(k == KH - 1))
                ins.then_inc(vs_ps, 1)

            def spread():
                pe.wait_ge(diag_set, 1)
                mm(bank[0][:, 0:NS], ones[0:PP, :], s_diag, start=True, stop=True).then_inc(rows_bc, 1)
                pe.wait_ge(diag_set, 2)
                mm(bank[1][:, 0:4 * PP], ones[0:PP, :], e_diag, start=True, stop=True).then_inc(rows_bc, 1)

            skewed(pe, n_front, n_back, pause=spread)

            pe.wait_ge(hT_ready, NT)
            pe.wait_ge(q_ready, NT + 1)
            pe.wait_ge(vs_ready, NT)
            pe.wait_ge(diag_set, 3)
            for q in range(0, SBLK, 4):
                n = min(4, SBLK - q)
                ins = mm(bank[3 + q // 4][:, 0:n * P], ones[:, :], diag[:, q:q + n, :], start=True, stop=True)
            ins.then_inc(rows_bc, 1)
            for b in range(SBLK):
                pe.wait_ge(rel_set, b + 1)
                if b >= 2:
                    pe.wait_ge(tab_set, b - 1)
                for c in range(2):
                    for u in range(SUB):
                        q = c * SUB + u
                        ins = tr(bank[6 + b % 2][:, q * P:(q + 1) * P], gath[:, b, u, c * P:(c + 1) * P], ident[:, :])
                ins.then_inc(tabT_done, 1)

            pe.wait_ge(dist_in, 32)
            pe.wait_ge(ones_set, 1)
            pe.wait_ge(keep_set, 1)
            pe.wait_ge(tab_set, SBLK)

            def distances(g, s, j, loads):
                if j % LOADG == 0:
                    pe.wait_ge(rows_in[j // LOADG], 16 * loads)
                for k in range(GC):
                    c = ((j % LOADG) * GC + k) * CHUNK
                    ins = mm(bank[2 + s][:, k * LO:(k + 1) * LO], dist_rows[:, j // LOADG, c:c + CHUNK], dist_rhs[:, :],
                             start=True, stop=True)
                ins.then_inc(dist_done, 1)

            distances(0, 0, 0, 1)
            distances(1, 1, 1, 1)

            def product(g, j, i):
                s = j % 2
                pe.wait_ge(y_ready, g + 1)
                if not (isinstance(i, int) and i == TURNS - 1 and j >= BODY - 2):
                    distances(g + 2, s, (j + 2) % BODY, i + 1 + (j + 2) // BODY)
                pe.wait_ge(x_ready, g + 1)
                for k in range(GC):
                    o = product_bank(j)[0:TILE, k // SUB * LO:(k // SUB + 1) * LO]
                    ins = mm(o, Xs[:, j % STAGES, k, :], Ys[:, j % STAGES, k, :], start=(k % SUB == 0), stop=(k % SUB == SUB - 1))
                ins.then_inc(prod_done, 1)

            turns(pe, product)

            pe.wait_ge(sums_ready, NG)
            pe.wait_ge(k_ready, NT)

            def front(t, s, u):
                pe.wait_ge(q_split, t + 1)
                for b, (c, n) in enumerate(SCH):
                    ahead = len(SCH) - 4
                    wait_from(pe, s_used, len(SCH) * t + (b - 3 if b >= 4 else min(b + 1 - ahead, 0)))
                    if isinstance(t, int) and t == 0:
                        pe.wait_ge(k_split, b + 1)
                    j = slice(c // LO, (c + n) // LO)
                    parts = [(q, v, k) for k in range(KH) for q, v in ((q_hi, k_hi), (q_hi, k_lo), (q_lo, k_hi))]
                    for i, (q, v, k) in enumerate(parts):
                        ins = mm(bank[b % 4][0:TILE, 0:n], q[:, s, k, :], v[:, k, j, :].rearrange("p j l -> p (j l)"),
                                 start=(i == 0), stop=(i == len(parts) - 1))
                    ins.then_inc(s_ready, 1)

            def back(t, s, u):
                wait_from(pe, o_used, t - 1)
                pe.wait_ge(p_ready, t + 1)

                def weigh(g):
                    j0, n = TRG[g]
                    pe.wait_ge(pt_ready, len(TRG) * t + g + 1)
                    for j in range(j0, j0 + n):
                        ins = mm(bank[6 + s][0:TILE, 0:D], PT[0:TILE, s, j, :], V[:, j, :], start=(j == 0), stop=(j == NT - 1))
                    return ins

                for g, (j0, n) in enumerate(TRG):
                    wait_from(pe, pt_ready, len(TRG) * t + (g - 1 if g >= 2 else 0))
                    for j in range(n):
                        ins = tr(bank[4 + g % 2][0:TILE, j * TILE:(j + 1) * TILE],
                                 Z[0:TILE, s, (j0 + j) * LO:(j0 + j) * LO + TILE], ident[0:TILE, 0:TILE])
                    ins.then_inc(tr_ready, 1)
                    if g:
                        weigh(g - 1)
                weigh(len(TRG) - 1).then_inc(attn_done, 1)

            skewed(pe, front, back)

            pe.wait_ge(s_used, len(SCH) * NT)
            pe.wait_ge(pt_ready, len(TRG) * NT)
            pe.wait_ge(o_used, NT)
            pe.wait_ge(params_in, 16 * len(params))

            def f_tr(t, s, u):
                pe.wait_ge(x1c_set, t + 1)
                wait_from(pe, x1T_set, t - 1)
                transposed(x1c[0:TILE, s, :], bank[s]).then_inc(x1T_ps, 1)

            def f_1(t, s, u):
                pe.wait_ge(x1T_set, t + 1)
                wait_from(pe, g_set, t - 1)
                for m in range(FF // P):
                    for k in range(KH):
                        ins = mm(bank[2 + s][:, m * TILE:(m + 1) * TILE], wf1_sb[:, k, m * P:(m + 1) * P], x1T[:, s, k, :],
                                 start=(k == 0), stop=(k == KH - 1))
                ins.then_inc(f1_ps, 1)

            def f_2(t, s, u):
                pe.wait_ge(g_set, t + 1)
                wait_from(pe, y2_used, t - 1)
                for m in range(FF // P):
                    ins = mm(bank[4 + s][0:TILE, 0:D], gT[:, s, m, :], wf2_sb[:, m, :], start=(m == 0), stop=(m == FF // P - 1))
                ins.then_inc(f2_ps, 1)

            def r_tr(t, s, u):
                pe.wait_ge(xfc_set, t + 1)
                wait_from(pe, lg_set, t - 1)
                transposed(xf[0:TILE, s, :], bank[6 + s]).then_inc(xfT_ps, 1)

            def r_logits(t, s, u):
                pe.wait_ge(xfT_set, t + 1)
                for k in range(KH):
                    ins = mm(bank[6 + s][0:TILE, D:D + NEXP], xfT[:, s, k, :], rw_sb[:, k, :], start=(k == 0), stop=(k == KH - 1))
                ins.then_inc(lg_ps, 1)

            pipeline(pe, (f_1, 1), (r_logits, R_LAG + 1), (f_tr, 0), (f_2, 2), (r_tr, R_LAG))
            pe.wait_ge(y2_used, NT)
            pe.wait_ge(hot_set, 1)
            pe.wait_ge(ws_set, KH + 1)
            half = (NT + 1) // 2 * NEXP
            for q, c in enumerate((slice(0, half), slice(half, NT * NEXP))):
                n = c.stop - c.start
                mm(bank[q][0:TILE, 0:n], before[0:TILE, 0:TILE], hot[0:TILE, c], start=True, stop=True)
                ins = mm(bank[2 + q][:, 0:n], ones[0:TILE, :], hot[0:TILE, c], start=True, stop=True)
            ins.then_inc(ranks_ps, 1)

            pe.wait_ge(pos_set, 1)

            def e_tr(j, s, u):
                pe.wait_ge(xs_in[s], 16 * (u + 1))
                wait_from(pe, xsT_set, j - 1)
                for k in range(KH):
                    ins = tr(bank[j_bank(0, s)][:, k * P:(k + 1) * P], xs[:, s, k:D:KH], ident[:, :])
                ins.then_inc(xsT_ps, 1)

            def e_1(j, s, u):
                pe.wait_ge(xsT_set, j + 1)
                pe.wait_ge(w_in[s], 16 * (u + 1))
                wait_from(pe, hid_set, j - 1)
                for k in range(KH):
                    ins = mm(bank[j_bank(2, s)][0:HID, 0:P], w1s[:, s, k * HID:(k + 1) * HID], xsT[:, s, k * P:(k + 1) * P],
                             start=(k == 0), stop=(k == KH - 1))
                ins.then_inc(hid_ps, 1)

            def e_2(j, s, u):
                pe.wait_ge(hid_set, j + 1)
                wait_from(pe, ys_set, j - 1)
                mm(bank[j_bank(4, s)][:, 0:D], hid[0:XROW, s, :], w2s[0:XROW, s, 0:D], start=True, stop=True).then_inc(o_ps, 1)

            pipeline(pe, (e_1, 2), (e_tr, 0), (e_2, 3), n=MT, per=ES)

    return nc


_INS = ['x', 'src', 'dst', 'edge_weight', 'L0_gnn_wq', 'L0_gnn_bq', 'L0_gnn_wk', 'L0_gnn_bk', 'L0_gnn_wv', 'L0_gnn_bv',
        'L0_gnn_ws', 'L0_gnn_bs', 'L0_gnn_we', 'L0_gnn_be', 'L0_gnn_g1', 'L0_gnn_b1', 'L0_gnn_g2', 'L0_gnn_b2',
        'L0_gnn_w_ff1', 'L0_gnn_b_ff1', 'L0_gnn_w_ff2', 'L0_gnn_b_ff2', 'L0_ffn_router_w', 'L0_ffn_router_b',
        'L0_ffn_W1', 'L0_ffn_b1', 'L0_ffn_W2', 'L0_ffn_b2']


def kernel(**inputs):
    import numpy as _np
    import concourse.bacc as _bacc
    from concourse import mybir as _mybir
    from concourse.bass_utils import run_bass_kernel_spmd as _run

    nc = _bacc.Bacc("TRN2", target_bir_lowering=False, num_devices=1)
    arrays, args = {}, []
    for name in _INS:
        a = _np.ascontiguousarray(inputs[name])
        arrays[f"in_{name}"] = a
        args.append(nc.dram_tensor(f"in_{name}", a.shape, _mybir.dt.from_np(a.dtype), kind="ExternalInput").ap())
    out = nc.dram_tensor("out_0", (3125, 256), _mybir.dt.float32, kind="ExternalOutput").ap()
    gnn_moe(nc, *args, out)
    r = _run(nc, [arrays], core_ids=[0])
    return r.results[0]["out_0"]
```
